# Optimizing a Trainium2 kernel written in Bass

```python
import numpy as np
import jax
import jax.numpy as jnp

def _softmax(x, axis=-1):
    return jax.nn.softmax(x, axis=axis)

def _gelu(x):
    return jax.nn.gelu(x, approximate=True)

def _silu(x):
    return jax.nn.silu(x)

def _sigmoid(x):
    return jax.nn.sigmoid(x)

def _layernorm(x, axis=-1, eps=1e-05):
    m = jnp.mean(x, axis=axis, keepdims=True)
    v = jnp.var(x, axis=axis, keepdims=True)
    return (x - m) / jnp.sqrt(v + eps)

def _scatter_add(tgt, idx, src, axis=0):
    return tgt.at[idx].add(src)

def _segment_sum(src, seg, n):
    return jax.ops.segment_sum(src, seg, n)
kernel_name = 'mk_gnn_resnorm_d4_gnn_r8_6271f7'

def setup_inputs(seed: int=0):
    np.random.seed(seed)
    _w = jnp.asarray

    def _rec_inputs():
        import jax
        import jax.numpy as jnp
        _gk = jax.random.key(seed)
        x = -0.0005121 + 1.001 * jax.random.normal(jax.random.fold_in(_gk, 1), (6250, 64), jnp.float32)
        src = jax.random.randint(jax.random.fold_in(_gk, 2), (200000,), 0, 6250, jnp.int32)
        dst = jax.random.randint(jax.random.fold_in(_gk, 3), (200000,), 0, 6250, jnp.int32)
        _o = jnp.argsort(dst, stable=True)
        src = src[_o]
        dst = dst[_o]
        edge_attr_16 = 0.000254156 + 0.999948 * jax.random.normal(jax.random.fold_in(_gk, 12), (200000, 16), jnp.float32)
        edge_attr_32 = 0.000216709 + 1.00012 * jax.random.normal(jax.random.fold_in(_gk, 13), (200000, 32), jnp.float32)
        edge_weight = jax.random.uniform(jax.random.fold_in(_gk, 15), (200000,), jnp.float32, 0.0, 1)
        return (x, src, dst, edge_attr_16, edge_attr_32, edge_weight)
    x, src, dst, edge_attr_16, edge_attr_32, edge_weight = _rec_inputs()

    def _L0_gnn_setup():
        import jax, jax.numpy as jnp
        import numpy as np
        N, E, F, FE, L = (6250, 100000, 64, 16, 2)
        AVG_DEG_LOG = float(np.log(17.0))
        EPS_STD = 1e-05
        EPS_BN = 1e-05

        def _pna_layer(x, src, dst, edge_attr, We, be, Wp, bp, Wo, bo, Wl, bl, g, b):
            n = x.shape[0]
            e = edge_attr @ We.T + be
            m = jnp.concatenate([x[dst], x[src], e], axis=-1) @ Wp.T + bp
            ones = jnp.ones((m.shape[0],), x.dtype)
            cnt = jax.ops.segment_sum(ones, dst, n)
            ssum = jax.ops.segment_sum(m, dst, n)
            denom = jnp.maximum(cnt, 1.0)[:, None]
            mean = ssum / denom
            mean_sq = jax.ops.segment_sum(m * m, dst, n) / denom
            std = jnp.sqrt(jnp.maximum(mean_sq - mean * mean, 0.0) + EPS_STD)
            mn = jax.ops.segment_min(m, dst, n)
            mn = jnp.where(jnp.isfinite(mn), mn, 0.0)
            mx = jax.ops.segment_max(m, dst, n)
            mx = jnp.where(jnp.isfinite(mx), mx, 0.0)
            agg = jnp.concatenate([mean, mn, mx, std, ssum], axis=-1)
            deg = jnp.maximum(cnt, 1.0)[:, None]
            amp = jnp.log(deg + 1.0) / AVG_DEG_LOG
            att = AVG_DEG_LOG / jnp.log(deg + 1.0)
            out = jnp.concatenate([agg, agg * amp, agg * att], axis=-1)
            out = jnp.concatenate([x, out], axis=-1) @ Wo.T + bo
            out = out @ Wl.T + bl
            mu = out.mean(axis=0)
            var = out.var(axis=0)
            out = (out - mu) / jnp.sqrt(var + EPS_BN) * g + b
            return jax.nn.relu(out)
        key = jax.random.key(seed)
        ks = jax.random.split(key, 13)
        s = 0.05
        return {'x': jax.random.normal(ks[0], (N, F), jnp.float32), 'edge_index': jax.random.randint(ks[1], (2, E), 0, N, dtype=jnp.int32), 'edge_attr': jax.random.normal(ks[2], (E, FE), jnp.float32), 'W_edge': s * jax.random.normal(ks[3], (L, F, FE), jnp.float32), 'b_edge': s * jax.random.normal(ks[4], (L, F), jnp.float32), 'W_pre': s * jax.random.normal(ks[5], (L, F, 3 * F), jnp.float32), 'b_pre': s * jax.random.normal(ks[6], (L, F), jnp.float32), 'W_post': s * jax.random.normal(ks[7], (L, F, 16 * F), jnp.float32), 'b_post': s * jax.random.normal(ks[8], (L, F), jnp.float32), 'W_lin': s * jax.random.normal(ks[9], (L, F, F), jnp.float32), 'b_lin': s * jax.random.normal(ks[10], (L, F), jnp.float32), 'bn_gamma': jnp.ones((L, F), jnp.float32), 'bn_beta': jnp.zeros((L, F), jnp.float32)}
    _L0_gnn_all = _L0_gnn_setup()
    _L0_gnn_in = {k: v for k, v in _L0_gnn_all.items() if k in ('W_edge', 'b_edge', 'W_pre', 'b_pre', 'W_post', 'b_post', 'W_lin', 'b_lin', 'bn_gamma', 'bn_beta')}
    del _L0_gnn_all

    def _L1_gnn_setup():
        import jax, jax.numpy as jnp
        import numpy as np
        N_NODES = 12500
        N_EDGES = 200000
        D_FEAT = 64
        key = jax.random.key(seed)
        k_seq, k_val, k_src, k_dst = jax.random.split(key, 4)
        seq = jax.random.normal(k_seq, (N_NODES, D_FEAT), dtype=jnp.float32)
        edge_val = jax.random.uniform(k_val, (N_EDGES,), dtype=jnp.float32)
        edge_src = jax.random.randint(k_src, (N_EDGES,), 0, N_NODES, dtype=jnp.int32)
        edge_dst = jax.random.randint(k_dst, (N_EDGES,), 0, N_NODES, dtype=jnp.int32)
        return {'seq': seq, 'edge_val': edge_val, 'edge_src': edge_src, 'edge_dst': edge_dst, 'propa_times': 3}
    _L1_gnn_all = _L1_gnn_setup()
    _L1_gnn_in = {k: v for k, v in _L1_gnn_all.items() if k in ()}
    del _L1_gnn_all

    def _L2_gnn_setup():
        import jax, jax.numpy as jnp
        import numpy as np
        N_NODES = 12500
        N_EDGES = 200000
        DIM = 64
        LAYERS = 2
        key = jax.random.key(seed)
        k1, k2, k3, k4 = jax.random.split(key, 4)
        h = jax.random.normal(k1, (N_NODES, DIM), dtype=jnp.float32)
        w = jax.random.uniform(k2, (N_EDGES,), dtype=jnp.float32)
        src = jax.random.randint(k3, (N_EDGES,), 0, N_NODES, dtype=jnp.int32)
        dst = jax.random.randint(k4, (N_EDGES,), 0, N_NODES, dtype=jnp.int32)
        return {'h': h, 'w': w, 'src': src, 'dst': dst}
    _L2_gnn_all = _L2_gnn_setup()
    _L2_gnn_in = {k: v for k, v in _L2_gnn_all.items() if k in ()}
    del _L2_gnn_all

    def _L3_gnn_setup():
        import jax, jax.numpy as jnp
        import numpy as np
        N_NODES = 6250
        N_EDGES = 100000
        D_NODE = 64
        D_EDGE = 32
        D_HID = 128

        def _mlp(x, W1, b1, W2, b2):
            return jax.nn.relu(x @ W1 + b1) @ W2 + b2
        key = jax.random.key(seed)
        ks = jax.random.split(key, 12)
        inp = {'nodes': jax.random.normal(ks[0], (N_NODES, D_NODE), dtype=jnp.float32), 'row': jax.random.randint(ks[1], (N_EDGES,), 0, N_NODES, dtype=jnp.int32), 'col': jax.random.randint(ks[2], (N_EDGES,), 0, N_NODES, dtype=jnp.int32), 'edge_features': jax.random.normal(ks[3], (N_EDGES, D_EDGE), dtype=jnp.float32)}
        d_in_msg = 2 * D_NODE + D_EDGE
        inp['mW1'] = jax.random.normal(ks[4], (d_in_msg, D_HID), dtype=jnp.float32) / np.sqrt(d_in_msg)
        inp['mb1'] = jnp.zeros((D_HID,), dtype=jnp.float32)
        inp['mW2'] = jax.random.normal(ks[5], (D_HID, D_NODE), dtype=jnp.float32) / np.sqrt(D_HID)
        inp['mb2'] = jnp.zeros((D_NODE,), dtype=jnp.float32)
        d_in_upd = 2 * D_NODE
        inp['uW1'] = jax.random.normal(ks[6], (d_in_upd, D_HID), dtype=jnp.float32) / np.sqrt(d_in_upd)
        inp['ub1'] = jnp.zeros((D_HID,), dtype=jnp.float32)
        inp['uW2'] = jax.random.normal(ks[7], (D_HID, D_NODE), dtype=jnp.float32) / np.sqrt(D_HID)
        inp['ub2'] = jnp.zeros((D_NODE,), dtype=jnp.float32)
        return inp
    _L3_gnn_all = _L3_gnn_setup()
    _L3_gnn_in = {k: v for k, v in _L3_gnn_all.items() if k in ('mW1', 'mb1', 'mW2', 'mb2', 'uW1', 'ub1', 'uW2', 'ub2')}
    del _L3_gnn_all
    return {'x': x, 'src': src, 'dst': dst, 'edge_attr_16': edge_attr_16, 'edge_attr_32': edge_attr_32, 'edge_weight': edge_weight, 'L0_gnn_W_edge': _L0_gnn_in['W_edge'], 'L0_gnn_b_edge': _L0_gnn_in['b_edge'], 'L0_gnn_W_pre': _L0_gnn_in['W_pre'], 'L0_gnn_b_pre': _L0_gnn_in['b_pre'], 'L0_gnn_W_post': _L0_gnn_in['W_post'], 'L0_gnn_b_post': _L0_gnn_in['b_post'], 'L0_gnn_W_lin': _L0_gnn_in['W_lin'], 'L0_gnn_b_lin': _L0_gnn_in['b_lin'], 'L0_gnn_bn_gamma': _L0_gnn_in['bn_gamma'], 'L0_gnn_bn_beta': _L0_gnn_in['bn_beta'], 'L3_gnn_mW1': _L3_gnn_in['mW1'], 'L3_gnn_mb1': _L3_gnn_in['mb1'], 'L3_gnn_mW2': _L3_gnn_in['mW2'], 'L3_gnn_mb2': _L3_gnn_in['mb2'], 'L3_gnn_uW1': _L3_gnn_in['uW1'], 'L3_gnn_ub1': _L3_gnn_in['ub1'], 'L3_gnn_uW2': _L3_gnn_in['uW2'], 'L3_gnn_ub2': _L3_gnn_in['ub2']}

def reference(x, src, dst, edge_attr_16, edge_attr_32, edge_weight, L0_gnn_W_edge, L0_gnn_b_edge, L0_gnn_W_pre, L0_gnn_b_pre, L0_gnn_W_post, L0_gnn_b_post, L0_gnn_W_lin, L0_gnn_b_lin, L0_gnn_bn_gamma, L0_gnn_bn_beta, L3_gnn_mW1, L3_gnn_mb1, L3_gnn_mW2, L3_gnn_mb2, L3_gnn_uW1, L3_gnn_ub1, L3_gnn_uW2, L3_gnn_ub2):
    import jax
    import jax.numpy as jnp

    def _L0_gnn_ref(x, edge_index, edge_attr, W_edge, b_edge, W_pre, b_pre, W_post, b_post, W_lin, b_lin, bn_gamma, bn_beta):
        import jax, jax.numpy as jnp
        import numpy as np
        N, E, F, FE, L = (6250, 100000, 64, 16, 2)
        AVG_DEG_LOG = float(np.log(17.0))
        EPS_STD = 1e-05
        EPS_BN = 1e-05

        def _pna_layer(x, src, dst, edge_attr, We, be, Wp, bp, Wo, bo, Wl, bl, g, b):
            n = x.shape[0]
            e = edge_attr @ We.T + be
            m = jnp.concatenate([x[dst], x[src], e], axis=-1) @ Wp.T + bp
            ones = jnp.ones((m.shape[0],), x.dtype)
            cnt = jax.ops.segment_sum(ones, dst, n)
            ssum = jax.ops.segment_sum(m, dst, n)
            denom = jnp.maximum(cnt, 1.0)[:, None]
            mean = ssum / denom
            mean_sq = jax.ops.segment_sum(m * m, dst, n) / denom
            std = jnp.sqrt(jnp.maximum(mean_sq - mean * mean, 0.0) + EPS_STD)
            mn = jax.ops.segment_min(m, dst, n)
            mn = jnp.where(jnp.isfinite(mn), mn, 0.0)
            mx = jax.ops.segment_max(m, dst, n)
            mx = jnp.where(jnp.isfinite(mx), mx, 0.0)
            agg = jnp.concatenate([mean, mn, mx, std, ssum], axis=-1)
            deg = jnp.maximum(cnt, 1.0)[:, None]
            amp = jnp.log(deg + 1.0) / AVG_DEG_LOG
            att = AVG_DEG_LOG / jnp.log(deg + 1.0)
            out = jnp.concatenate([agg, agg * amp, agg * att], axis=-1)
            out = jnp.concatenate([x, out], axis=-1) @ Wo.T + bo
            out = out @ Wl.T + bl
            mu = out.mean(axis=0)
            var = out.var(axis=0)
            out = (out - mu) / jnp.sqrt(var + EPS_BN) * g + b
            return jax.nn.relu(out)
        src, dst = (edge_index[0], edge_index[1])
        for l in range(L):
            x = _pna_layer(x, src, dst, edge_attr, W_edge[l], b_edge[l], W_pre[l], b_pre[l], W_post[l], b_post[l], W_lin[l], b_lin[l], bn_gamma[l], bn_beta[l])
        return x

    def _L1_gnn_ref(seq, edge_val, edge_src, edge_dst, propa_times):
        import jax, jax.numpy as jnp
        import numpy as np
        N_NODES = 12500
        N_EDGES = 200000
        D_FEAT = 64
        n = seq.shape[0]
        for _ in range(propa_times):
            msgs = edge_val[:, None] * seq[edge_src]
            seq = jax.ops.segment_sum(msgs, edge_dst, num_segments=n)
        return seq

    def _L2_gnn_ref(h, w, src, dst):
        import jax, jax.numpy as jnp
        import numpy as np
        N_NODES = 12500
        N_EDGES = 200000
        DIM = 64
        LAYERS = 2
        N = h.shape[0]
        deg = jnp.maximum(jax.ops.segment_sum(w, dst, num_segments=N), 1.0)
        norm = deg[:, None] ** (-0.5)
        embs = [h]
        for _ in range(LAYERS):
            h_norm = h * norm
            m = h_norm[src] * w[:, None]
            neigh_sum = jax.ops.segment_sum(m, dst, num_segments=N)
            h = neigh_sum * norm
            embs.append(h)
        return jnp.mean(jnp.stack(embs, axis=1), axis=1)

    def _L3_gnn_ref(nodes, row, col, edge_features, mW1, mb1, mW2, mb2, uW1, ub1, uW2, ub2):
        import jax, jax.numpy as jnp
        import numpy as np
        N_NODES = 6250
        N_EDGES = 100000
        D_NODE = 64
        D_EDGE = 32
        D_HID = 128

        def _mlp(x, W1, b1, W2, b2):
            return jax.nn.relu(x @ W1 + b1) @ W2 + b2
        msg_in = jnp.concatenate([nodes[row], nodes[col], edge_features], axis=-1)
        messages = _mlp(msg_in, mW1, mb1, mW2, mb2)
        aggregated = jax.ops.segment_sum(messages, col, num_segments=nodes.shape[0])
        upd_in = jnp.concatenate([nodes, aggregated], axis=-1)
        return _mlp(upd_in, uW1, ub1, uW2, ub2)
    edge_index = jnp.stack([src, dst])
    x = _layernorm(x + _L0_gnn_ref(x, edge_index, edge_attr_16, L0_gnn_W_edge, L0_gnn_b_edge, L0_gnn_W_pre, L0_gnn_b_pre, L0_gnn_W_post, L0_gnn_b_post, L0_gnn_W_lin, L0_gnn_b_lin, L0_gnn_bn_gamma, L0_gnn_bn_beta), axis=-1)
    x = _layernorm(x + _L1_gnn_ref(x, edge_weight, src, dst, 3), axis=-1)
    x = _layernorm(x + _L2_gnn_ref(x, edge_weight, src, dst), axis=-1)
    x = _layernorm(x + _L3_gnn_ref(x, src, dst, edge_attr_32, L3_gnn_mW1, L3_gnn_mb1, L3_gnn_mW2, L3_gnn_mb2, L3_gnn_uW1, L3_gnn_ub1, L3_gnn_uW2, L3_gnn_ub2), axis=-1)
    return x

_drawn_inputs = setup_inputs


def setup_inputs(seed=0):
    import zlib

    import numpy as np

    out = dict(_drawn_inputs(seed))
    spreads = {'L0_gnn_bn_gamma': (1.0, 0.2),
     'L0_gnn_bn_beta': (0.0, 0.1),
     'L3_gnn_mb1': (0.0, 0.1),
     'L3_gnn_mb2': (0.0, 0.1),
     'L3_gnn_ub1': (0.0, 0.8),
     'L3_gnn_ub2': (0.0, 0.784)}
    factors = {'edge_attr_16': 8.0,
     'L0_gnn_W_edge': 8.0,
     'L0_gnn_b_edge': 48.824,
     'L0_gnn_b_post': 200.0,
     'L0_gnn_b_lin': 200.0,
     'L0_gnn_b_pre': 33.197}
    for name, (base, spread) in spreads.items():
        noise = np.random.default_rng([zlib.crc32(name.encode()), seed]).standard_normal(out[name].shape)
        drawn = base * np.exp(spread * noise) if base else spread * noise
        out[name] = jnp.asarray(drawn.astype(out[name].dtype))
    for name, factor in factors.items():
        out[name] = (out[name] * factor).astype(out[name].dtype)
    return out
```

```python
import numpy as np
import concourse.bass as bass
from concourse import mybir
from contextlib import ExitStack

N, E, F, FE16, FE32, HID = 6250, 200000, 64, 16, 32, 128
P = 128
NB = -(-N // P)
NP = NB * P
TG = 16
GE = TG * P
NI = -(-E // (2 * GE))
NG = 2 * NI
EP = NG * GE
NT = EP // P
SUB = 4
SE = GE // SUB
ST = TG // SUB
WL = F + 1
BIG = 1.7e38
AVG = float(np.log(17.0))
EPS = 1e-5
CB = 7
NC4 = -(-NB // 4)
KINDS = ["pna", "pna", "lin", "lin", "lin", "lin", "lin", "mlp"]
NPASS = len(KINDS)
W_OF = {"pna": 4 * F, "lin": WL, "mlp": HID}


def before(per_pass):
    out = [0]
    for kind in KINDS:
        out.append(out[-1] + per_pass[kind])
    return out


LOADS = {"pna": 3, "lin": 3, "mlp": 4}
LD0 = before({k: 16 * NI * v for k, v in LOADS.items()})
SCANS = {"pna": 2, "lin": 1, "mlp": 1}
SC0 = before({k: NG * SUB * v for k, v in SCANS.items()})
MIDS = {"pna": 4, "lin": 0, "mlp": 1}
MD0 = before({k: NG * SUB * v for k, v in MIDS.items()})
ONE0 = before({k: NG * SUB for k in SCANS})
WX0 = before({"pna": 0, "lin": 2 * NG, "mlp": 0})
ST0 = before({k: 16 * NI for k in SCANS})
ER0 = before({k: 16 * NB for k in SCANS})
TABLES = {"pna": 1, "lin": 1, "mlp": 2}
XT0 = {0: 0, 1: NC4, 7: 2 * NC4}
PJN = {0: NC4, 1: NC4, 7: -(-NB // 2)}
PJ0 = {0: 0, 1: NC4, 7: 2 * NC4}
SQRTS = [("log",)] + [(n, l, c) for l in (0, 1) for n, m in (("agg", NB // CB), ("bn", 1)) for c in range(m)] \
    + [("ln", 0), ("norm",), ("ln", 1), ("ln", 2), ("ln", 3)]
ORD = {s: n + 1 for n, s in enumerate(SQRTS)}


def build(nc, inp, out):
    f32, bf16, i32 = mybir.dt.float32, mybir.dt.bfloat16, mybir.dt.int32
    ALU, ACT, AX = mybir.AluOpType, mybir.ActivationFunctionType, mybir.AxisListType.X
    ctx = ExitStack()
    with ctx:
        def sb(name, shape, dt=f32):
            return ctx.enter_context(nc.sbuf_tensor(name, shape, dt))

        def sem(name):
            return ctx.enter_context(nc.semaphore(name))

        table = nc.dram_tensor("table", (NP, F), f32).ap()
        vtab = nc.dram_tensor("vtab", (NP, HID), f32).ap()
        utab = nc.dram_tensor("utab", (NP, HID), f32).ap()
        keep_d = nc.dram_tensor("keep_d", (NG, GE), bf16).ap()
        scan_d = {k: nc.dram_tensor(f"scan_{k}", (EP, w), f32).ap() for k, w in W_OF.items()}
        scan_store = {k: v.rearrange("(g p t) w -> g p (t w)", p=P, t=TG) for k, v in scan_d.items()}

        arena = sb("arena", [P, NB * 4 * F])
        ident = sb("ident", [P, P])
        lim_buf = sb("lim_buf", [P, 2 * SE])
        ones = sb("ones", [P, P])
        down = lim_buf[:, 0:P]
        corner = lim_buf[:, P:2 * P]
        sgn = sb("sgn", [P, 1])
        nid = sb("nid", [P, NB])
        valid = sb("valid", [P, NB])
        cnt = sb("cnt", [P, NB])
        nz = sb("nz", [P, NB])
        rden = sb("rden", [P, NB])
        amp = sb("amp", [P, NB])
        att = sb("att", [P, NB])
        norm = sb("norm", [P, NB])
        eidx = sb("eidx", [P, NB], i32)
        cur = sb("cur", [P, NB, F])
        acc = sb("acc", [P, NB, F])
        tmp = sb("tmp", [P, NB, F])
        adst = sb("adst", [P, NB, F])
        xt = sb("xt", [F, NP])
        st1 = sb("st1", [P, NB])
        st2 = sb("st2", [P, NB])
        mu = sb("mu", [P, F])
        sd = sb("sd", [P, F])
        idx = sb("idx", [P, 2, TG], i32)
        idx2 = sb("idx2", [P, 2, TG], i32)
        keep = sb("keep", [P, 2, GE], bf16)
        wcol = sb("wcol", [P, 2, TG])
        attr = sb("attr", [FE32, 2, GE])
        gat = sb("gat", [P, 2 * GE])
        mid = sb("mid", [P, 2 * TG * WL])
        lim = lim_buf[:, :].rearrange("p (r n) -> p r n", r=2)
        proj = [sb(f"proj{l}", [F, 2 * F]) for l in range(2)]
        projb = [sb(f"projb{l}", [1, 2 * F]) for l in range(2)]
        gw = [sb(f"gw{l}", [FE16, 2 * F]) for l in range(2)]
        wpost = [sb(f"wpost{l}", [P, 3, 3 * F]) for l in range(2)]
        wx = [sb(f"wx{l}", [F, 3 * F]) for l in range(2)]
        wxb = [sb(f"wxb{l}", [1, 3 * F]) for l in range(2)]
        gam = [sb(f"gam{l}", [P, F]) for l in range(2)]
        bet = [sb(f"bet{l}", [P, F]) for l in range(2)]
        p3 = sb("p3", [F, 2 * HID])
        p3b = sb("p3b", [1, 2 * HID])
        w1c = sb("w1c", [FE32, HID])
        w2 = sb("w2", [HID, F])
        b2 = sb("b2", [P, F])
        u1a = sb("u1a", [F, HID])
        u1b = sb("u1b", [F, HID])
        ub1 = sb("ub1", [HID, 1])
        u2 = sb("u2", [HID, F])
        ub2 = sb("ub2", [P, F])
        ps = ctx.enter_context(nc.psum_tensor("ps", [P, 8, 512], f32))

        rows_out = {k: arena[:, 0:2 * TG * w].rearrange("p (q n) -> p q n", q=2) for k, w in W_OF.items()}
        scan = arena[:, 8192:12288].rearrange("p (k n) -> p k n", k=2)
        ugat = arena[:, 4096:8192].rearrange("p (q t f) -> p q t f", q=2, f=HID)
        gat_l = gat[:, 0:2 * TG * F].rearrange("p (q t f) -> p q t f", q=2, f=F)
        gat_m = gat[:, :].rearrange("p (q t f) -> p q t f", q=2, f=HID)
        wxe = mid[:, :].rearrange("p (q t f) -> p q t f", q=2, f=WL)
        qm = mid[:, 0:4 * SE].rearrange("p (r k n) -> p r k n", r=2, k=2)
        ends = {k: arena[:, 0:NB * w].rearrange("p (b w) -> p b w", w=w) for k, w in W_OF.items()}
        agg = gat[:, 0:CB * 5 * F].rearrange("p (b c) -> p b c", c=5 * F)
        aggt = gat[:, CB * 5 * F:CB * 5 * F + 6 * P].rearrange("p (r k n) -> p r k n", r=2, k=3)
        vu = arena[:, 0:NB * 2 * HID].rearrange("p (b w) -> p b w", w=2 * HID)
        dcur = arena[:, 0:NT].bitcast(i32)
        dprev = arena[:, NT:2 * NT].bitcast(i32)
        keep0 = keep[:, 0, 0:NT]
        lasti = arena[:, 2 * NT:3 * NT].bitcast(i32)
        lastf = arena[:, 3 * NT:4 * NT]
        lcmp = arena[:, 4 * NT:5 * NT]
        drow = arena[:, 0:NP].rearrange("p (b n) -> p b n", n=P).bitcast(i32)
        dcmp = arena[:, NP:2 * NP].rearrange("p (b n) -> p b n", n=P)
        tcount = st1
        tidx = sb("tidx", [P, NB], i32)
        ccount = st2
        ub = sb("ub", [P, NB])
        eint = sb("eint", [P, NB], i32)
        epart = sb("epart", [P, 3, NB], i32)
        pet = [sb(f"pet{l}", [F, F]) for l in range(2)]
        wlt = [sb(f"wlt{l}", [F, F]) for l in range(2)]
        we = [sb(f"we{l}", [F, FE16]) for l in range(2)]
        be = [sb(f"be{l}", [F, 1]) for l in range(2)]
        bo = [sb(f"bo{l}", [F, 1]) for l in range(2)]
        bp = [sb(f"bp{l}", [1, F]) for l in range(2)]
        bl = [sb(f"bl{l}", [1, F]) for l in range(2)]
        wo = [gat[0:F, 1024 * l:1024 * (l + 1)] for l in range(2)]

        ld_w = sem("weights_loaded")
        ld_d = sem("dst_loaded")
        made = sem("constants_made")
        keep_ok = sem("keep_made")
        keep_st = sem("keep_stored")
        t_ok = sem("tile_index_made")
        drow_ok = sem("dst_rows_gathered")
        ub_ok = sem("upper_bounds_made")
        ubp_ok = sem("bounds_shifted")
        wps = sem("weight_products")
        wcp = sem("weight_products_copied")
        ld = [sem(f"group_loaded{q}") for q in range(2)]
        gt = [[sem(f"gathered{k}_{q}") for q in range(2)] for k in range(NPASS)]
        wxd = sem("weighted")
        zt = sem("turned")
        md = sem("mid_ready")
        scn = sem("scanned")
        bt = sem("turned_back")
        ev = sem("evacuated")
        st = [sem(f"rows_stored{q}") for q in range(2)]
        er = sem("ends_gathered")
        xr = sem("x_ready")
        go = sem("group_gathers_begun")
        xin = sem("x_loaded_again")
        xtp = sem("x_turned")
        xts = sem("xt_stored")
        pjp = sem("projected")
        pjs = sem("projection_copied")
        tbr = sem("table_rows_ready")
        tab = sem("table_stored")
        agr = sem("agg_ready")
        atp = sem("agg_turned")
        ats = sem("aggt_copied")
        omp = sem("post_product")
        oms = sem("post_used")
        rq = sem("root_asked")
        rs = sem("root_done")
        bns = sem("bn_rows_ready")
        bnp = sem("bn_summed")
        m_e = sem("mlp_sum_turned")
        m_et = sem("mlp_sum_copied")
        m_a = sem("mlp_message")
        m_as = sem("mlp_message_biased")
        m_t = sem("mlp_message_turned")
        m_ts = sem("mlp_message_copied")
        m_h = sem("mlp_hidden")
        m_hs = sem("mlp_hidden_relu")
        m_o = sem("mlp_out")
        m_os = sem("mlp_out_used")
        dch = sem("vector_chain")
        fin = sem("result_ready")
        outs = sem("result_stored")
        block = ctx.enter_context(nc.Block())

        def reach(eng, s, base, rel):
            if isinstance(rel, int):
                rel = max(rel, 0)
                if base + rel == 0:
                    return
            eng.wait_ge(s, rel + base)

        def turns(eng, body):
            body(0)
            with eng.Fori(1, NI) as i:
                body(i)

        def bcast(ap, n):
            return ap.unsqueeze(2).broadcast_to([P, ap.shape[1], n])

        def chunks(n, size):
            return [(j, j * size, min(size, n - j * size)) for j in range(-(-n // size))]

        wl = []

        @block.sync
        def _(sp):
            sp.dma_start(dcur, inp["dst_pad"][1:1 + EP].rearrange("(p n) -> p n", p=P)).then_inc(ld_d, 16)
            sp.dma_start(dprev, inp["dst_pad"][0:EP].rearrange("(p n) -> p n", p=P)).then_inc(ld_d, 16)
            sp.dma_start(lasti, inp["dst_last"].partition_broadcast(P)).then_inc(ld_d, 16)

            def w(dst, src):
                wl.append(1)
                sp.dma_start(dst, src).then_inc(ld_w, 16)

            for l in range(2):
                w(proj[l][:, 0:F], inp["wpT"][l, F:2 * F, :])
                w(proj[l][:, F:2 * F], inp["wpT"][l, 0:F, :])
                w(pet[l][:, :], inp["wpT"][l, 2 * F:3 * F, :])
                w(wlt[l][:, :], inp["wlT"][l, :, :])
                w(we[l][:, :], inp["we"][l, :, :])
                w(be[l][:, :], inp["be"][l:l + 1, :].rearrange("a f -> f a"))
                w(bo[l][:, :], inp["bo"][l:l + 1, :].rearrange("a f -> f a"))
                w(bp[l][:, :], inp["bp"][l:l + 1, :])
                w(bl[l][:, :], inp["bl"][l:l + 1, :])
                w(wo[l], inp["wo"][l, :, :])
                w(gam[l][:, :], inp["gam"][l, :].partition_broadcast(P))
                w(bet[l][:, :], inp["bet"][l, :].partition_broadcast(P))
            w(cur[:, :, :], inp["x"].rearrange("(b p) f -> p b f", p=P))
            w(p3[:, 0:HID], inp["mw1"][0:F, :])
            w(p3[:, HID:2 * HID], inp["mw1"][F:2 * F, :])
            w(p3b[:, HID:2 * HID], inp["mb1"].rearrange("(a f) -> a f", a=1))
            w(w1c[:, :], inp["mw1"][2 * F:2 * F + FE32, :])
            w(w2[:, :], inp["mw2"])
            w(b2[:, :], inp["mb2"].partition_broadcast(P))
            w(u1a[:, :], inp["uw1"][0:F, :])
            w(u1b[:, :], inp["uw1"][F:2 * F, :])
            w(ub1[:, :], inp["ub1"].rearrange("(f a) -> f a", a=1))
            w(u2[:, :], inp["uw2"])
            w(ub2[:, :], inp["ub2"].partition_broadcast(P))
            sp.wait_ge(keep_ok, 1)
            sp.dma_start(keep_d.rearrange("g n -> (g n)").rearrange("(p n) -> p n", p=P), keep0).then_inc(keep_st, 16)
            sp.wait_ge(keep_st, 16)
            for k, kind in enumerate(KINDS):
                if k == 2:
                    sp.wait_ge(bns, 3)
                    sp.dma_start(adst[:, :, :], inp["x"].rearrange("(b p) f -> p b f", p=P)).then_inc(xin, 16)
                sp.wait_ge(tbr, k + 1)
                if kind == "mlp":
                    sp.dma_start(vtab.rearrange("(b p) f -> p b f", p=P), vu[:, :, 0:HID]).then_inc(tab, 16)
                    sp.dma_start(utab.rearrange("(b p) f -> p b f", p=P), vu[:, :, HID:2 * HID]).then_inc(tab, 16)
                else:
                    rows = tmp if kind == "pna" else acc
                    sp.dma_start(table.rearrange("(b p) f -> p b f", p=P), rows[:, :, :]).then_inc(tab, 16)

                def body(i):
                    for q in range(2):
                        reach(sp, scn, SC0[k], (2 * i + q - 1) * SUB * SCANS[kind])
                        g = 2 * i + q
                        sp.dma_start(idx[:, q, :], inp["src_g"][g, :, :]).then_inc(ld[q], 16)
                        if kind == "mlp":
                            sp.dma_start(idx2[:, q, :], inp["dst_g"][g, :, :]).then_inc(ld[q], 16)
                        sp.dma_start(keep[:, q, :], keep_d[g, :].partition_broadcast(P)).then_inc(ld[q], 16)
                        if kind == "lin":
                            sp.dma_start(wcol[:, q, :], inp["w_g"][g, :, :]).then_inc(ld[q], 16)
                        if kind == "pna":
                            sp.dma_start(attr[0:FE16, q, :], inp["a16_g"][g, :, :]).then_inc(ld[q], 16)
                        if kind == "mlp":
                            sp.dma_start(attr[:, q, :], inp["a32_g"][g, :, :]).then_inc(ld[q], 16)

                turns(sp, body)
            sp.wait_ge(fin, 1)
            full = N // P
            sp.dma_start(out[0:full * P, :].rearrange("(b p) f -> p b f", p=P), acc[:, 0:full, :]).then_inc(outs, 16)
            sp.dma_start(out[full * P:N, :], acc[0:N - full * P, full, :]).then_inc(outs, 16)
            sp.wait_ge(outs, 32)

        @block.gpsimd
        def _(pool):
            pool.memset(ident[:, :], 0.0).then_inc(made, 1)
            pool.memset(ones[:, :], 1.0).then_inc(made, 1)
            pool.iota(epart[:, 0, :], pattern=[[P, NB]], base=0, channel_multiplier=1).then_inc(made, 1)
            pool.memset(lim_buf[:, 0:2 * P], 0.0).then_inc(made, 1)
            pool.wait_ge(made, 4)
            pool.affine_select(out=ident[:, :], in_=ident[:, :], compare_op=ALU.not_equal, fill=1.0,
                               base=0, pattern=[[-1, P]], channel_multiplier=1).then_inc(made, 1)
            pool.affine_select(out=down, in_=down, compare_op=ALU.not_equal, fill=1.0,
                               base=1, pattern=[[-1, P]], channel_multiplier=1).then_inc(made, 1)
            pool.affine_select(out=corner, in_=corner, compare_op=ALU.not_equal, fill=1.0,
                               base=1 - P, pattern=[[P, P]], channel_multiplier=1).then_inc(made, 1)
            pool.wait_ge(t_ok, 1)
            for b in range(NB):
                pool.indirect_dma_start(drow[:, b, :], None, inp["dst_tiles"],
                                        bass.IndirectOffsetOnAxis(ap=tidx[:, b:b + 1], axis=0)).then_inc(drow_ok, 16)
            need = 0
            for k, kind in enumerate(KINDS):
                need += 16 * TABLES[kind]
                pool.wait_ge(tab, need)

                def body(i):
                    for q in range(2):
                        g = 2 * i + q
                        reach(pool, ld[q], LD0[k], 16 * LOADS[kind] * (i + 1))
                        if kind == "lin":
                            reach(pool, wxd, WX0[k], 2 * (g - 1))
                        else:
                            reach(pool, zt, ONE0[k], SUB * (g - 1))
                        pool.sem_inc(go, 1)
                        for t in range(TG):
                            if kind == "mlp":
                                pool.indirect_dma_start(gat_m[:, q, t, :], None, vtab, bass.IndirectOffsetOnAxis(
                                    ap=idx[:, q, t:t + 1], axis=0)).then_inc(gt[k][q], 16)
                                pool.indirect_dma_start(ugat[:, q, t, :], None, utab, bass.IndirectOffsetOnAxis(
                                    ap=idx2[:, q, t:t + 1], axis=0)).then_inc(gt[k][q], 16)
                            else:
                                pool.indirect_dma_start(gat_l[:, q, t, :], None, table, bass.IndirectOffsetOnAxis(
                                    ap=idx[:, q, t:t + 1], axis=0)).then_inc(gt[k][q], 16)

                turns(pool, body)
                for q in range(2):
                    pool.wait_ge(st[q], ST0[k + 1])
                for b in range(NB):
                    pool.indirect_dma_start(ends[kind][:, b, :], None, scan_d[kind], bass.IndirectOffsetOnAxis(
                        ap=eidx[:, b:b + 1], axis=0)).then_inc(er, 16)

        @block.vector
        def _(dve):
            chain = [0]

            def link(ins):
                chain[0] += 1
                ins.then_inc(dch, 1)
                dve.wait_ge(dch, chain[0])

            dve.wait_ge(ld_d, 48)
            dve.tensor_tensor(keep0, dcur, dprev, ALU.is_equal).then_inc(keep_ok, 1)
            dve.memset(sgn[0:F, :], 1.0)
            dve.memset(sgn[F:2 * F, :], -1.0)
            for l in range(2):
                dve.memset(wpost[l][:, :, :], 0.0)
                dve.memset(wx[l][:, :], 0.0)
                dve.memset(wxb[l][:, :], 0.0)
                dve.memset(projb[l][:, :], 0.0)
            link(dve.memset(p3b[:, 0:HID], 0.0))
            dve.wait_ge(made, 7)
            link(dve.tensor_copy(nid[:, :], epart[:, 0, :]))
            link(dve.tensor_scalar(valid[:, :], nid[:, :], float(N), None, ALU.is_lt))
            link(dve.tensor_copy(lastf, lasti))
            for b in range(NB):
                link(dve.tensor_scalar(lcmp, lastf, nid[:, b:b + 1], None, ALU.is_le))
                link(dve.reduce_sum(tcount[:, b:b + 1], lcmp, AX))
            link(dve.tensor_copy(tidx[:, :], tcount[:, :]))
            dve.wait_ge(keep_st, 16)
            dve.memset(st2[:, 0:1], 0.0).then_inc(t_ok, 1)
            dve.wait_ge(drow_ok, 16 * NB)
            link(dve.tensor_tensor(dcmp, drow, bcast(nid[:, :], P), ALU.is_le))
            link(dve.reduce_sum(ccount[:, :], dcmp, AX))
            link(dve.scalar_tensor_tensor(out=ub[:, :], in0=tcount[:, :], scalar=float(P), in1=ccount[:, :],
                                          op0=ALU.mult, op1=ALU.add))
            link(dve.tensor_scalar(st1[:, :], ub[:, :], 1.0, -1.0, ALU.max, ALU.add))
            dve.tensor_copy(eint[:, :], st1[:, :]).then_inc(ub_ok, 1)
            dve.wait_ge(ub_ok, 1)
            link(dve.tensor_scalar(epart[:, 0, :], eint[:, :], P - 1, 4, ALU.bitwise_and, ALU.logical_shift_left))
            link(dve.tensor_scalar(epart[:, 1, :], eint[:, :], 7, TG - 1, ALU.logical_shift_right, ALU.bitwise_and))
            link(dve.tensor_scalar(epart[:, 2, :], eint[:, :], 11, 11, ALU.logical_shift_right, ALU.logical_shift_left))
            link(dve.tensor_tensor(epart[:, 0, :], epart[:, 0, :], epart[:, 1, :], ALU.bitwise_or))
            link(dve.tensor_tensor(eidx[:, :], epart[:, 0, :], epart[:, 2, :], ALU.bitwise_or))
            dve.wait_ge(ubp_ok, 1)
            link(dve.tensor_tensor(cnt[:, :], ub[:, :], ps[:, 3, 0:NB], ALU.subtract))
            link(dve.tensor_scalar(nz[:, :], cnt[:, :], 1.0, None, ALU.min))
            link(dve.tensor_scalar(st1[:, :], cnt[:, :], 1.0, None, ALU.max))
            link(dve.reciprocal(rden[:, :], st1[:, :]))
            dve.tensor_scalar(st2[:, :], st1[:, :], 1.0, None, ALU.add).then_inc(rq, 1)
            dve.wait_ge(rs, ORD["log",])
            link(dve.reciprocal(st1[:, :], st2[:, :]))
            link(dve.tensor_scalar(amp[:, :], st2[:, :], 1.0 / AVG, None, ALU.mult))
            link(dve.tensor_scalar(att[:, :], st1[:, :], AVG, None, ALU.mult))
            for l in range(2):
                dve.wait_ge(wps, l + 1)
                dve.tensor_copy(gw[l][:, 0:F], ps[0:FE16, 0, 0:F])
                dve.tensor_copy(gw[l][:, F:2 * F], ps[0:FE16, 0, 0:F])
                dve.tensor_tensor(projb[l][:, F:2 * F], ps[0:1, 0, F:2 * F], bp[l][:, :], ALU.add)
                dve.tensor_copy(wx[l][:, 0:F], ps[0:F, 0, 2 * F:3 * F])
                dve.tensor_tensor(wxb[l][:, 0:F], ps[0:1, 0, 3 * F:4 * F], bl[l][:, :], ALU.add)
                dve.tensor_copy(wpost[l][:, 0:2, :], ps[:, 1, 0:6 * F].rearrange("p (k n) -> p k n", k=2))
                dve.tensor_copy(wpost[l][0:F, 2, :], ps[0:F, 2, 0:3 * F]).then_inc(wcp, 1)

            def layer_norm(n, src, res):
                link(dve.reduce_sum(st1[:, :], src[:, :, :], AX))
                link(dve.tensor_scalar(st1[:, :], st1[:, :], 1.0 / F, None, ALU.mult))
                link(dve.tensor_tensor(src[:, :, :], src[:, :, :], bcast(st1[:, :], F), ALU.subtract))
                link(dve.tensor_tensor(tmp[:, :, :], src[:, :, :], src[:, :, :], ALU.mult))
                link(dve.reduce_sum(st2[:, :], tmp[:, :, :], AX))
                dve.tensor_scalar(st2[:, :], st2[:, :], 1.0 / F, EPS, ALU.mult, ALU.add).then_inc(rq, 1)
                dve.wait_ge(rs, ORD["ln", n])
                link(dve.reciprocal(st2[:, :], st2[:, :]))
                link(dve.tensor_tensor(res[:, :, :], src[:, :, :], bcast(st2[:, :], F), ALU.mult))

            def projection(k):
                for j in range(PJN[k]):
                    dve.wait_ge(pjp, PJ0[k] + j + 1)
                    if k == 7:
                        n = min(2, NB - 2 * j)
                        dve.tensor_copy(vu[:, 2 * j:2 * j + n, :], ps[:, 4 + j % 4, 0:n * 2 * HID].rearrange(
                            "p (b w) -> p b w", b=n)).then_inc(pjs, 1)
                    else:
                        n = min(4, NB - 4 * j)
                        v = ps[:, 4 + j % 4, 0:n * 2 * F].rearrange("p (b w) -> p b w", b=n)
                        dve.tensor_copy(tmp[:, 4 * j:4 * j + n, :], v[:, :, 0:F])
                        dve.tensor_copy(adst[:, 4 * j:4 * j + n, :], v[:, :, F:2 * F]).then_inc(pjs, 1)
                dve.wait_ge(pjs, PJ0[k] + PJN[k])
                dve.memset(st2[:, 0:1], 0.0).then_inc(tbr, 1)

            def segment_scans(k, kind):
                width = {"pna": P, "lin": WL, "mlp": P}[kind]

                def body(i):
                    for q in range(2):
                        g = 2 * i + q
                        if kind == "lin":
                            dve.wait_ge(gt[k][q], 16 * TG * (i + 1))
                            reach(dve, ld[q], LD0[k], 16 * LOADS[kind] * (i + 1))
                            reach(dve, zt, ONE0[k], SUB * (g - 1))
                            dve.tensor_tensor(wxe[:, q, :, 0:F], gat_l[:, q, :, :], bcast(wcol[:, q, :], F),
                                              ALU.mult).then_inc(wxd, 1)
                            dve.tensor_copy(wxe[:, q, :, F], wcol[:, q, :]).then_inc(wxd, 1)
                        else:
                            reach(dve, ld[q], LD0[k], 16 * LOADS[kind] * (i + 1))
                        for s in range(SUB):
                            n = SUB * g + s
                            if kind == "lin":
                                reach(dve, zt, ONE0[k], n + 1)
                                data = ps[0:width, s, :]
                            else:
                                reach(dve, md, MD0[k], MIDS[kind] * (n + 1))
                                data = qm[:, s % 2, 0, :]
                            reach(dve, bt, ONE0[k], n - SUB + 1)
                            reach(dve, scn, SC0[k], SCANS[kind] * n)
                            here = slice(s * SE, (s + 1) * SE)
                            last = (s * SE - 1) % GE
                            dve.tensor_tensor_scan(scan[0:width, 0, here], keep[0:width, q, here], data,
                                                   scan[0:width, 0, last:last + 1], ALU.mult, ALU.add).then_inc(scn, 1)
                            if kind == "pna":
                                dve.tensor_tensor_scan(scan[:, 1, here], lim[:, s % 2, :], qm[:, s % 2, 1, :],
                                                       scan[:, 1, last:last + 1], ALU.min, ALU.max).then_inc(scn, 1)

                turns(dve, body)
                dve.wait_ge(er, ER0[k + 1])

            def pna_nodes(l):
                e = ends["pna"]
                for c in range(NB // CB):
                    bs = slice(c * CB, (c + 1) * CB)
                    reach(dve, atp, NB * l, c * CB)
                    mean, mn, mx, std, ssum = (agg[:, :, f * F:(f + 1) * F] for f in range(5))
                    rd, z = bcast(rden[:, bs], F), bcast(nz[:, bs], F)
                    a = adst[:, bs, :]
                    link(dve.tensor_tensor(mean, e[:, bs, 0:F], rd, ALU.mult))
                    link(dve.tensor_tensor(std, e[:, bs, F:2 * F], rd, ALU.mult))
                    link(dve.tensor_tensor(ssum, mean, mean, ALU.mult))
                    link(dve.tensor_tensor(std, std, ssum, ALU.subtract))
                    link(dve.tensor_tensor(std, std, z, ALU.mult))
                    dve.tensor_scalar(std, std, 0.0, EPS, ALU.max, ALU.add).then_inc(rq, 1)
                    link(dve.tensor_tensor(mean, mean, a, ALU.add))
                    link(dve.tensor_tensor(mean, mean, z, ALU.mult))
                    link(dve.tensor_tensor(mn, a, e[:, bs, 3 * F:4 * F], ALU.subtract))
                    link(dve.tensor_tensor(mn, mn, z, ALU.mult))
                    link(dve.tensor_tensor(mx, a, e[:, bs, 2 * F:3 * F], ALU.add))
                    link(dve.tensor_tensor(mx, mx, z, ALU.mult))
                    dve.tensor_tensor(ssum, mean, bcast(cnt[:, bs], F), ALU.mult).then_inc(agr, 1)
                    for b in range(c * CB, (c + 1) * CB):
                        dve.wait_ge(omp, NB * l + b + 1)
                        o = ps[:, 4 + b % 4, :]
                        link(dve.tensor_copy(acc[:, b, :], o[:, 0:F]))
                        link(dve.scalar_tensor_tensor(out=acc[:, b, :], in0=o[:, F:2 * F], scalar=amp[:, b:b + 1],
                                                      in1=acc[:, b, :], op0=ALU.mult, op1=ALU.add))
                        dve.scalar_tensor_tensor(out=acc[:, b, :], in0=o[:, 2 * F:3 * F], scalar=att[:, b:b + 1],
                                                 in1=acc[:, b, :], op0=ALU.mult, op1=ALU.add).then_inc(oms, 1)
                dve.wait_ge(oms, NB * (l + 1))
                v = valid[:, NB - 1:NB]
                dve.tensor_scalar(acc[:, NB - 1, :], acc[:, NB - 1, :], v, None, ALU.mult).then_inc(bns, 1)
                dve.wait_ge(bnp, 2 * l + 1)
                fold = ps[:, 0, 0:7 * F].rearrange("p (b f) -> p f b", f=F)
                link(dve.reduce_sum(mu[:, :], fold, AX))
                link(dve.tensor_scalar(mu[:, :], mu[:, :], 1.0 / N, None, ALU.mult))
                mub = mu[:, :].unsqueeze(1).broadcast_to([P, NB, F])
                link(dve.tensor_tensor(acc[:, :, :], acc[:, :, :], mub, ALU.subtract))
                link(dve.tensor_scalar(acc[:, NB - 1, :], acc[:, NB - 1, :], v, None, ALU.mult))
                dve.tensor_tensor(tmp[:, :, :], acc[:, :, :], acc[:, :, :], ALU.mult).then_inc(bns, 1)
                dve.wait_ge(bnp, 2 * l + 2)
                link(dve.reduce_sum(sd[:, :], fold, AX))
                dve.tensor_scalar(sd[:, :], sd[:, :], 1.0 / N, EPS, ALU.mult, ALU.add).then_inc(rq, 1)
                dve.wait_ge(rs, ORD["bn", l, 0])
                link(dve.reciprocal(sd[:, :], sd[:, :]))
                link(dve.tensor_tensor(sd[:, :], sd[:, :], gam[l][:, :], ALU.mult))
                sdb = sd[:, :].unsqueeze(1).broadcast_to([P, NB, F])
                bb = bet[l][:, :].unsqueeze(1).broadcast_to([P, NB, F])
                link(dve.tensor_tensor(acc[:, :, :], acc[:, :, :], sdb, ALU.mult))
                link(dve.tensor_tensor(acc[:, :, :], acc[:, :, :], bb, ALU.add))
                if l == 0:
                    dve.tensor_scalar(cur[:, :, :], acc[:, :, :], 0.0, None, ALU.max).then_inc(xr, 1)
                else:
                    link(dve.tensor_scalar(acc[:, :, :], acc[:, :, :], 0.0, None, ALU.max))
                    dve.wait_ge(xin, 16)
                    link(dve.tensor_tensor(acc[:, :, :], acc[:, :, :], adst[:, :, :], ALU.add))
                    layer_norm(0, acc, cur)
                    dve.tensor_copy(acc[:, :, :], cur[:, :, :]).then_inc(tbr, 1)
                    dve.wait_ge(tbr, 3)

            dve.wait_ge(ld_w, 16 * len(wl))
            link(dve.memset(scan[:, :, GE - 1:GE], 0.0))
            for l in range(2):
                projection(l)
                segment_scans(l, "pna")
                pna_nodes(l)
            e = ends["lin"][:, :, 0:F]
            nzb = bcast(nz[:, :], F)
            for k in (2, 3, 4):
                segment_scans(k, "lin")
                if k == 2:
                    link(dve.tensor_tensor(st1[:, :], ends["lin"][:, :, F], nz[:, :], ALU.mult))
                    dve.tensor_scalar(st2[:, :], st1[:, :], 1.0, None, ALU.max).then_inc(rq, 1)
                    dve.wait_ge(rs, ORD["norm",])
                    link(dve.reciprocal(norm[:, :], st2[:, :]))
                if k < 4:
                    dve.tensor_tensor(acc[:, :, :], e, nzb, ALU.mult).then_inc(tbr, 1)
                else:
                    link(dve.tensor_tensor(acc[:, :, :], e, nzb, ALU.mult))
                    link(dve.tensor_tensor(acc[:, :, :], acc[:, :, :], cur[:, :, :], ALU.add))
                    layer_norm(1, acc, cur)
            nb = bcast(norm[:, :], F)
            link(dve.tensor_copy(adst[:, :, :], cur[:, :, :]))
            dve.tensor_tensor(acc[:, :, :], cur[:, :, :], nb, ALU.mult).then_inc(tbr, 1)
            for k in (5, 6):
                segment_scans(k, "lin")
                link(dve.tensor_tensor(tmp[:, :, :], e, nzb, ALU.mult))
                link(dve.tensor_tensor(tmp[:, :, :], tmp[:, :, :], nb, ALU.mult))
                link(dve.tensor_tensor(adst[:, :, :], adst[:, :, :], tmp[:, :, :], ALU.add))
                if k == 5:
                    dve.tensor_tensor(acc[:, :, :], tmp[:, :, :], nb, ALU.mult).then_inc(tbr, 1)
            link(dve.tensor_scalar(adst[:, :, :], adst[:, :, :], 1.0 / 3.0, None, ALU.mult))
            link(dve.tensor_tensor(adst[:, :, :], adst[:, :, :], cur[:, :, :], ALU.add))
            layer_norm(2, adst, cur)
            dve.memset(st1[:, 0:1], 0.0).then_inc(xr, 1)
            projection(7)
            segment_scans(7, "mlp")
            em = ends["mlp"]
            link(dve.tensor_tensor(em, em, bcast(nz[:, :], HID), ALU.mult))
            dve.memset(st1[:, 0:1], 0.0).then_inc(agr, 1)
            for j, b, n in chunks(NB, 4):
                dve.wait_ge(m_a, j + 1)
                b2b = b2[:, :].unsqueeze(1).broadcast_to([P, n, F])
                link(dve.tensor_tensor(acc[:, b:b + n, :], b2b, bcast(cnt[:, b:b + n], F), ALU.mult))
                dve.tensor_tensor(acc[:, b:b + n, :], acc[:, b:b + n, :],
                                  ps[:, 1, 0:n * F].rearrange("p (b f) -> p b f", b=n), ALU.add).then_inc(m_as, 1)
                dve.wait_ge(m_o, j + 1)
                u2b = ub2[:, :].unsqueeze(1).broadcast_to([P, n, F])
                link(dve.tensor_tensor(acc[:, b:b + n, :], ps[:, 4, 0:n * F].rearrange("p (b f) -> p b f", b=n), u2b,
                                       ALU.add))
                dve.tensor_tensor(acc[:, b:b + n, :], acc[:, b:b + n, :], cur[:, b:b + n, :], ALU.add).then_inc(m_os, 1)
            dve.wait_ge(m_os, NC4)
            layer_norm(3, acc, acc)
            dve.memset(st1[:, 0:1], 0.0).then_inc(fin, 1)

        @block.scalar
        def _(act):
            def root(name, ap, log=False):
                act.wait_ge(rq, ORD[name])
                act.activation(ap, ap, ACT.Ln if log else ACT.Sqrt).then_inc(rs, 1)

            def turned(k):
                for j, b, n in chunks(NB, 4):
                    act.wait_ge(xtp, XT0[k] + j + 1)
                    act.activation(xt[:, b * P:(b + n) * P], ps[0:F, j % 4, 0:n * P], ACT.Copy).then_inc(xts, 1)

            def evacuate(k, kind, g, s, q):
                w = W_OF[kind]
                n = SUB * g + s
                reach(act, bt, ONE0[k], n + 1)
                if s == 0:
                    reach(act, st[q], ST0[k], 8 * g - 8 * q)
                o = rows_out[kind][:, q, s * ST * w:(s + 1) * ST * w]
                if kind == "pna":
                    src = ps[:, 4 + 2 * (s % 2):6 + 2 * (s % 2), :].rearrange("p a n -> p (a n)")
                elif kind == "lin":
                    src = ps[:, 4 + s, 0:ST * w]
                else:
                    src = ps[:, 4 + s, :]
                act.activation(o, src, ACT.Copy).then_inc(ev, 1)
                if s == SUB - 1:
                    reach(act, ev, ONE0[k], n + 1)
                    act.dma_start(scan_store[kind][g, :, :], rows_out[kind][:, q, 0:TG * w]).then_inc(st[q], 16)

            def rows(k, kind):
                def body(i):
                    for q in range(2):
                        g = 2 * i + q
                        for s in range(SUB):
                            n = SUB * g + s
                            if kind != "lin":
                                if s == 0:
                                    reach(act, ld[q], LD0[k], 16 * LOADS[kind] * (i + 1))
                                reach(act, zt, ONE0[k], n + 1)
                                reach(act, scn, SC0[k], SCANS[kind] * (n - 1))
                            if kind == "pna":
                                r = s % 2
                                act.activation(qm[0:F, r, 0, :], ps[0:F, s, :], ACT.Copy).then_inc(md, 1)
                                act.activation(qm[F:2 * F, r, 0, :], ps[F:2 * F, s, :], ACT.Square).then_inc(md, 1)
                                act.activation(qm[:, r, 1, :], ps[:, s, :], ACT.Copy, scale=sgn[:, 0:1]).then_inc(md, 1)
                                act.activation(lim[:, r, :], keep[:, q, s * SE:(s + 1) * SE], ACT.Copy,
                                               bias=-BIG, scale=2 * BIG).then_inc(md, 1)
                            if kind == "mlp":
                                act.activation(qm[:, s % 2, 0, :], ps[:, s, :], ACT.Relu).then_inc(md, 1)
                            if s > 0:
                                evacuate(k, kind, g, s - 1, q)
                            elif not (isinstance(i, int) and i == 0 and q == 0):
                                evacuate(k, kind, g - 1, SUB - 1, 1 - q)

                turns(act, body)
                evacuate(k, kind, NG - 1, SUB - 1, 1)

            root(("log",), st2[:, :], log=True)
            for l in range(2):
                turned(l)
                rows(l, "pna")
                for c in range(NB // CB):
                    root(("agg", l, c), agg[:, :, 3 * F:4 * F])
                    for b in range(c * CB, (c + 1) * CB):
                        act.wait_ge(atp, NB * l + b + 1)
                        reach(act, omp, NB * l, b - 1)
                        act.activation(aggt[:, b % 2, 0:2, :], ps[:, b % 2, 0:2 * P].rearrange("p (k n) -> p k n", k=2),
                                       ACT.Copy).then_inc(ats, 1)
                        act.activation(aggt[0:F, b % 2, 2, :], ps[0:F, b % 2, 2 * P:3 * P], ACT.Copy).then_inc(ats, 1)
                root(("bn", l, 0), sd[:, :])
            root(("ln", 0), st2[:, :])
            rows(2, "lin")
            root(("norm",), st2[:, :])
            rows(3, "lin")
            rows(4, "lin")
            root(("ln", 1), st2[:, :])
            rows(5, "lin")
            rows(6, "lin")
            root(("ln", 2), st2[:, :])
            turned(7)
            rows(7, "mlp")
            for j, b, n in chunks(NB, 4):
                act.wait_ge(m_e, j + 1)
                act.activation(mid[:, 0:n * P], ps[:, 0, 0:n * P], ACT.Copy).then_inc(m_et, 1)
                act.wait_ge(m_t, j + 1)
                act.activation(mid[0:F, 512:512 + n * P], ps[0:F, 2, 0:n * P], ACT.Copy).then_inc(m_ts, 1)
                act.wait_ge(m_h, j + 1)
                act.activation(mid[:, 1024:1024 + n * P], ps[:, 3, 0:n * P], ACT.Relu, bias=ub1[:, 0:1]).then_inc(m_hs, 1)
            root(("ln", 3), st2[:, :])

        @block.tensor
        def _(pe):
            mm = pe.matmul
            pe.wait_ge(ld_w, 16 * len(wl))
            pe.wait_ge(made, 7)
            pe.wait_ge(ub_ok, 1)
            mm(ps[:, 3, 0:NB], down, ub[:, :], start=True, stop=False)
            mm(ps[:, 3, 1:NB], corner, ub[:, 0:NB - 1], start=False, stop=True).then_inc(ubp_ok, 1)
            for l in range(2):
                if l == 1:
                    pe.wait_ge(wcp, 1)
                mm(ps[0:FE16, 0, 0:F], we[l][:, :], pet[l][:, :], start=True, stop=True)
                mm(ps[0:1, 0, F:2 * F], be[l][:, :], pet[l][:, :], start=True, stop=True)
                mm(ps[0:F, 0, 2 * F:3 * F], wo[l][:, 0:F], wlt[l][:, :], start=True, stop=True)
                mm(ps[0:1, 0, 3 * F:4 * F], bo[l][:, :], wlt[l][:, :], start=True, stop=True)
                for r in range(3):
                    for c in range(3):
                        m = P if c < 2 else F
                        k0 = F + 5 * F * r + P * c
                        o = ps[0:m, 1, (3 * c + r) * F:(3 * c + r + 1) * F] if c < 2 else ps[0:m, 2, r * F:(r + 1) * F]
                        last = mm(o, wo[l][:, k0:k0 + m], wlt[l][:, :], start=True, stop=True)
                last.then_inc(wps, 1)
            pe.wait_ge(wcp, 2)

            def project(k):
                for j, b, n in chunks(NB, 4):
                    if j >= 4:
                        pe.wait_ge(xts, XT0[k] + j - 3)
                    for c in range(n):
                        last = pe.transpose(ps[0:F, j % 4, c * P:(c + 1) * P], cur[:, b + c, :], ident[:, :])
                    last.then_inc(xtp, 1)
                w, bias, m, per = (p3, p3b, 2 * HID, 2) if k == 7 else (proj[k], projb[k], 2 * F, 4)
                for j, b, n in chunks(NB, per):
                    pe.wait_ge(xts, XT0[k] + b * P // 512 + 1)
                    if j >= 4:
                        pe.wait_ge(pjs, PJ0[k] + j - 3)
                    for c in range(n):
                        o = ps[:, 4 + j % 4, c * m:(c + 1) * m]
                        mm(o, xt[:, (b + c) * P:(b + c + 1) * P], w[:, :], start=True, stop=False)
                        last = mm(o, ones[0:1, :], bias[:, :], start=False, stop=True)
                    last.then_inc(pjp, 1)

            def turn_back(k, kind, g, s):
                n = SUB * g + s
                reach(pe, scn, SC0[k], SCANS[kind] * (n + 1))
                reach(pe, ev, ONE0[k], n - (1 if kind == "pna" else 3))
                w = W_OF[kind]
                for t in range(ST):
                    c0 = s * SE + t * P
                    if kind == "pna":
                        o = ps[:, 4 + 2 * (s % 2) + t // 2, (t % 2) * 256:(t % 2) * 256 + 256]
                        pe.transpose(o[:, 0:P], scan[:, 0, c0:c0 + P], ident[:, :])
                        last = pe.transpose(o[:, P:2 * P], scan[:, 1, c0:c0 + P], ident[:, :])
                    else:
                        last = pe.transpose(ps[:, 4 + s, t * w:(t + 1) * w], scan[0:w, 0, c0:c0 + P], ident[0:w, 0:w])
                last.then_inc(bt, 1)

            def edges(k, kind):
                def body(i):
                    for q in range(2):
                        g = 2 * i + q
                        if kind != "lin":
                            pe.wait_ge(gt[k][q], 16 * TG * TABLES[kind] * (i + 1))
                            reach(pe, ld[q], LD0[k], 16 * LOADS[kind] * (i + 1))
                        else:
                            reach(pe, wxd, WX0[k], 2 * (g + 1))
                        for s in range(SUB):
                            n = SUB * g + s
                            if kind == "lin":
                                reach(pe, scn, SC0[k], n - SUB + 1)
                            else:
                                reach(pe, md, MD0[k], MIDS[kind] * (n - SUB + 1))
                            if kind == "pna":
                                mm(ps[:, s, :], gw[k][:, :], attr[0:FE16, q, s * SE:(s + 1) * SE], start=True, stop=False)
                            if kind == "mlp":
                                mm(ps[:, s, :], w1c[:, :], attr[:, q, s * SE:(s + 1) * SE], start=True, stop=False)
                            for t in range(ST):
                                tt = s * ST + t
                                if kind == "lin":
                                    last = pe.transpose(ps[0:WL, s, t * P:(t + 1) * P], wxe[:, q, tt, :], ident[:, :])
                                elif kind == "pna":
                                    for h in range(2):
                                        last = mm(ps[h * F:(h + 1) * F, s, t * P:(t + 1) * P], gat_l[:, q, tt, :],
                                                  ident[:, :], start=False, stop=(t == ST - 1))
                                else:
                                    mm(ps[:, s, t * P:(t + 1) * P], gat_m[:, q, tt, :], ident[:, :],
                                       start=False, stop=False)
                                    last = mm(ps[:, s, t * P:(t + 1) * P], ugat[:, q, tt, :], ident[:, :],
                                              start=False, stop=(t == ST - 1))
                            last.then_inc(zt, 1)
                            if s > 0:
                                turn_back(k, kind, g, s - 1)
                            elif not (isinstance(i, int) and i == 0 and q == 0):
                                turn_back(k, kind, g - 1, SUB - 1)

                turns(pe, body)
                turn_back(k, kind, NG - 1, SUB - 1)

            for l in range(2):
                if l:
                    pe.wait_ge(xr, 1)
                project(l)
                edges(l, "pna")
                for b in range(NB):
                    if b % CB == 0:
                        pe.wait_ge(agr, (NB // CB) * l + b // CB + 1)
                        pe.wait_ge(rs, ORD["agg", l, b // CB])
                    reach(pe, ats, 2 * NB * l, 2 * (b - 1))
                    for c in range(3):
                        m = P if c < 2 else F
                        last = pe.transpose(ps[0:m, b % 2, c * P:(c + 1) * P], agg[:, b % CB, c * P:c * P + m],
                                            ident[:, :])
                    last.then_inc(atp, 1)
                    pe.wait_ge(ats, 2 * NB * l + 2 * (b + 1))
                    reach(pe, oms, NB * l, b - 3)
                    o = ps[:, 4 + b % 4, 0:3 * F]
                    mm(o, xt[:, b * P:(b + 1) * P], wx[l][:, :], start=True, stop=False)
                    mm(o, ones[0:1, :], wxb[l][:, :], start=False, stop=False)
                    for c in range(3):
                        m = P if c < 2 else F
                        last = mm(o, aggt[0:m, b % 2, c, :], wpost[l][0:m, c, :], start=False, stop=(c == 2))
                    last.then_inc(omp, 1)
                for v in range(2):
                    pe.wait_ge(bns, 2 * l + v + 1)
                    src = acc if v == 0 else tmp
                    for j in range(7):
                        last = mm(ps[:, 0, 0:7 * F], ones[:, :],
                                  src[:, 7 * j:7 * j + 7, :].rearrange("p b f -> p (b f)"), start=(j == 0), stop=(j == 6))
                    last.then_inc(bnp, 1)
            for k in range(2, 7):
                edges(k, "lin")
            pe.wait_ge(xr, 2)
            project(7)
            edges(7, "mlp")
            pe.wait_ge(agr, 2 * (NB // CB) + 1)
            for j, b, n in chunks(NB, 4):
                reach(pe, m_et, 0, j)
                for c in range(n):
                    last = pe.transpose(ps[:, 0, c * P:(c + 1) * P], ends["mlp"][:, b + c, :], ident[:, :])
                last.then_inc(m_e, 1)
                pe.wait_ge(m_et, j + 1)
                reach(pe, m_as, 0, j)
                for c in range(n):
                    last = mm(ps[:, 1, c * F:(c + 1) * F], mid[:, c * P:(c + 1) * P], w2[:, :], start=True, stop=True)
                last.then_inc(m_a, 1)
                pe.wait_ge(m_as, j + 1)
                for c in range(n):
                    last = pe.transpose(ps[0:F, 2, c * P:(c + 1) * P], acc[:, b + c, :], ident[:, :])
                last.then_inc(m_t, 1)
                pe.wait_ge(m_ts, j + 1)
                mm(ps[:, 3, 0:n * P], u1b[:, :], mid[0:F, 512:512 + n * P], start=True, stop=False)
                mm(ps[:, 3, 0:n * P], u1a[:, :], xt[:, b * P:(b + n) * P], start=False, stop=True).then_inc(m_h, 1)
                pe.wait_ge(m_hs, j + 1)
                reach(pe, m_os, 0, j)
                for c in range(n):
                    last = mm(ps[:, 4, c * F:(c + 1) * F], mid[:, 1024 + c * P:1024 + (c + 1) * P], u2[:, :],
                              start=True, stop=True)
                last.then_inc(m_o, 1)


def kernel(**inputs):
    import numpy as np
    import concourse.bacc as bacc
    from concourse import mybir
    from concourse.bass_utils import run_bass_kernel_spmd as run

    a = {k: np.asarray(v) for k, v in inputs.items()}
    x = np.zeros((NP, F), a["x"].dtype)
    x[:N] = a["x"]

    def padded(v, fill):
        out = np.full((EP,) + v.shape[1:], fill, v.dtype)
        out[:E] = v
        return out

    src, w = padded(a["src"], 0), padded(a["edge_weight"], 0)
    dst, dst0 = padded(a["dst"], NP), padded(a["dst"], 0)
    before_first = np.full((1,), -1, dst.dtype)

    def by_group(v):
        return np.ascontiguousarray(v.reshape(NG, TG, P).transpose(0, 2, 1))

    def features_first(v):
        return np.ascontiguousarray(v.reshape(NG, GE, v.shape[1]).transpose(0, 2, 1))

    arrays = {
        "x": x, "src_g": by_group(src), "dst_g": by_group(dst0), "w_g": by_group(w),
        "dst_pad": np.concatenate([before_first, dst]), "dst_tiles": dst.reshape(NT, P),
        "dst_last": np.ascontiguousarray(dst.reshape(NT, P)[:, P - 1]),
        "a16_g": features_first(padded(a["edge_attr_16"], 0)), "a32_g": features_first(padded(a["edge_attr_32"], 0)),
        "wpT": np.ascontiguousarray(a["L0_gnn_W_pre"].transpose(0, 2, 1)),
        "wlT": np.ascontiguousarray(a["L0_gnn_W_lin"].transpose(0, 2, 1)),
        "we": a["L0_gnn_W_edge"], "be": a["L0_gnn_b_edge"], "bp": a["L0_gnn_b_pre"], "bo": a["L0_gnn_b_post"],
        "bl": a["L0_gnn_b_lin"], "wo": a["L0_gnn_W_post"], "gam": a["L0_gnn_bn_gamma"], "bet": a["L0_gnn_bn_beta"],
        "mw1": a["L3_gnn_mW1"], "mb1": a["L3_gnn_mb1"], "mw2": a["L3_gnn_mW2"], "mb2": a["L3_gnn_mb2"],
        "uw1": a["L3_gnn_uW1"], "ub1": a["L3_gnn_ub1"], "uw2": a["L3_gnn_uW2"], "ub2": a["L3_gnn_ub2"],
    }
    nc = bacc.Bacc("TRN2", target_bir_lowering=False, num_devices=1)
    inp = {n: nc.dram_tensor(f"in_{n}", v.shape, mybir.dt.from_np(v.dtype), kind="ExternalInput").ap()
           for n, v in arrays.items()}
    out = nc.dram_tensor("out_0", (N, F), mybir.dt.float32, kind="ExternalOutput").ap()
    build(nc, inp, out)
    r = run(nc, [{f"in_{n}": np.ascontiguousarray(v) for n, v in arrays.items()}], core_ids=[0])
    return r.results[0]["out_0"]
```

```python
import numpy as np
import concourse.bass as bass
from concourse import mybir
from contextlib import ExitStack

N, E, F, FE16, FE32, HID = 6250, 200000, 64, 16, 32, 128
P = 128
NB = -(-N // P)
NP = NB * P
TG = 16
GE = TG * P
NI = -(-E // (2 * GE))
NG = 2 * NI
EP = NG * GE
NT = EP // P
SUB = 4
SE = GE // SUB
ST = TG // SUB
D4 = 4
NGR = NP // D4
GB = P // D4
AW = NB * D4
STEPS = 2 * NG * TG
SG = TG
SC = -(-STEPS // P)
SPARE = TG
BLK = GB * AW
BIG = 1.7e38
AVG = float(np.log(17.0))
EPS = 1e-5
CB = 7
NC4 = -(-NB // 4)
KINDS = ["pna", "pna", "mlp"]
NPASS = len(KINDS)
W_OF = {"pna": 4 * F, "mlp": HID}
assert NT + NGR <= STEPS + 1


def before(per_pass):
    out = [0]
    for kind in KINDS:
        out.append(out[-1] + per_pass[kind])
    return out


LOADS = {"pna": 5, "mlp": 2}
LD0 = before({k: 16 * NI * v for k, v in LOADS.items()})
SCANS = {"pna": 2, "mlp": 1}
SC0 = before({k: NG * SUB * v for k, v in SCANS.items()})
MIDS = {"pna": 4, "mlp": 1}
MD0 = before({k: NG * SUB * v for k, v in MIDS.items()})
ONE0 = before({k: NG * SUB for k in SCANS})
PR0 = before({"pna": NG * SG, "mlp": 0})
SG0 = before({"pna": NG, "mlp": 2 * NG})
ST0 = before({k: 16 * NI for k in SCANS})
ER0 = before({k: 16 * NB for k in SCANS})
TABLES = {"pna": 1, "mlp": 2}
XT0 = {0: 0, 1: NC4, 2: 2 * NC4}
PJN = {0: NC4, 1: NC4, 2: -(-NB // 2)}
PJ0 = {0: 0, 1: NC4, 2: 2 * NC4}
SQRTS = [("log",)] + [(n, l, c) for l in (0, 1) for n, m in (("agg", NB // CB), ("bn", 1)) for c in range(m)] \
    + [("ln", 0), ("norm",), ("ln", 1), ("ln", 2), ("ln", 3)]
ORD = {s: n + 1 for n, s in enumerate(SQRTS)}


def build(nc, inp, out):
    f32, bf16, i32 = mybir.dt.float32, mybir.dt.bfloat16, mybir.dt.int32
    ALU, ACT, AX = mybir.AluOpType, mybir.ActivationFunctionType, mybir.AxisListType.X
    ctx = ExitStack()
    with ctx:
        def sb(name, shape, dt=f32):
            return ctx.enter_context(nc.sbuf_tensor(name, shape, dt))

        def sem(name):
            return ctx.enter_context(nc.semaphore(name))

        table = nc.dram_tensor("table", (NP, F), f32).ap()
        vtab = nc.dram_tensor("vtab", (NP, HID), f32).ap()
        utab = nc.dram_tensor("utab", (NP, HID), f32).ap()
        keep_d = nc.dram_tensor("keep_d", (NG, GE), bf16).ap()
        ends_d = nc.dram_tensor("ends_d", (NGR,), i32).ap()
        step_d = nc.dram_tensor("step_d", (P, 3, SC * P), f32).ap()
        same_d = nc.dram_tensor("same_d", (SC * P + 1,), f32).ap()
        dest_d = nc.dram_tensor("dest_d", (SC * P,), i32).ap()
        group_d = nc.dram_tensor("group_d", ((NGR + SPARE) * P, AW), f32).ap()
        scan_d = {k: nc.dram_tensor(f"scan_{k}", (EP, w), f32).ap() for k, w in W_OF.items()}
        scan_store = {k: v.rearrange("(g p t) w -> g p (t w)", p=P, t=TG) for k, v in scan_d.items()}

        arena = sb("arena", [P, NB * 4 * F])
        ident = sb("ident", [P, P])
        lim_buf = sb("lim_buf", [P, 2 * SE])
        ones = sb("ones", [P, P])
        down = lim_buf[:, 0:P]
        corner = lim_buf[:, P:2 * P]
        sgn = sb("sgn", [P, 1])
        nid = sb("nid", [P, NB])
        valid = sb("valid", [P, NB])
        cnt = sb("cnt", [P, NB])
        nz = sb("nz", [P, NB])
        rden = sb("rden", [P, NB])
        amp = sb("amp", [P, NB])
        att = sb("att", [P, NB])
        norm = sb("norm", [P, NB])
        eidx = sb("eidx", [P, NB], i32)
        cur = sb("cur", [P, NB, F])
        acc = sb("acc", [P, NB, F])
        tmp = sb("tmp", [P, NB, F])
        adst = sb("adst", [P, NB, F])
        xt = sb("xt", [F, NP])
        st1 = sb("st1", [P, NB])
        st2 = sb("st2", [P, NB])
        idx = sb("idx", [P, 2, TG], i32)
        idx2 = sb("idx2", [P, 2, TG], i32)
        src_all = sb("src_all", [P, NT], i32)
        keep = sb("keep", [P, 2, GE], bf16)
        step_in = sb("step_in", [P, 2, 3, SG])
        same = sb("same", [P, 2, SG])
        attr = sb("attr", [FE32, 2, GE])
        gat = sb("gat", [P, 2 * GE])
        mid = sb("mid", [P, 4 * SE])
        dest = sb("dest", [1, 2, SG], i32)
        stage = sb("stage", [P, 2, 4, AW])
        iota_c = sb("iota_c", [P, AW])
        b2, ub2 = iota_c[:, 0:F], iota_c[:, F:2 * F]
        mu, sd = mid[:, 0:F], mid[:, F:2 * F]
        dst_all = stage[:, :, :, :].rearrange("p r m n -> p (r m n)").bitcast(i32)
        ints = lim_buf[:, 2 * P:1024].bitcast(i32)
        inid, isid, icol = ints[:, 0:NB], ints[:, NB:NB + SC], ints[:, 80:80 + AW]
        isp = ints[0:SC, 320:320 + P]
        igrp = ints[0:NB, 288:288 + GB]
        lim = lim_buf[:, :].rearrange("p (r n) -> p r n", r=2)
        qm = mid[:, 0:4 * SE].rearrange("p (r k n) -> p r k n", r=2, k=2)
        proj = [sb(f"proj{l}", [F, 2 * F]) for l in range(2)]
        projb = [sb(f"projb{l}", [1, 2 * F]) for l in range(2)]
        gw = [sb(f"gw{l}", [FE16, 2 * F]) for l in range(2)]
        wpost = [sb(f"wpost{l}", [P, 3, 3 * F]) for l in range(2)]
        wx = [sb(f"wx{l}", [F, 3 * F]) for l in range(2)]
        wxb = [sb(f"wxb{l}", [1, 3 * F]) for l in range(2)]
        gam = [sb(f"gam{l}", [P, F]) for l in range(2)]
        bet = [sb(f"bet{l}", [P, F]) for l in range(2)]
        p3 = sb("p3", [F, 2 * HID])
        p3b = sb("p3b", [1, 2 * HID])
        w1c = sb("w1c", [FE32, HID])
        w2 = sb("w2", [HID, F])
        u1a = sb("u1a", [F, HID])
        u1b = sb("u1b", [F, HID])
        ub1 = sb("ub1", [HID, 1])
        u2 = sb("u2", [HID, F])
        ps = ctx.enter_context(nc.psum_tensor("ps", [P, 8, 512], f32))

        rows_out = {k: arena[:, 0:2 * TG * w].rearrange("p (q n) -> p q n", q=2) for k, w in W_OF.items()}
        scan = arena[:, 8192:12288].rearrange("p (k n) -> p k n", k=2)
        ugat = arena[:, 4096:8192].rearrange("p (q t f) -> p q t f", q=2, f=HID)
        gat_l = gat[:, 0:2 * TG * F].rearrange("p (q t f) -> p q t f", q=2, f=F)
        gat_m = gat[:, :].rearrange("p (q t f) -> p q t f", q=2, f=HID)
        hot_l = cur[:, 0:8, :].rearrange("p b f -> p (b f)").rearrange("p (m n) -> p m n", m=4)
        hot_r = cur[:, 8:8 + AW * 4 // F + 1, :].rearrange("p b f -> p (b f)")[:, 0:4 * AW].rearrange(
            "p (m n) -> p m n", m=4)
        ablk = arena[:, :].rearrange("p (r g s d) -> p r g s d", r=2, g=GB, d=D4)
        first_rows = gat[:, 0:NB * (F + 1)].rearrange("p (b f) -> p b f", f=F + 1)
        outt = mid[0:F + 1, 0:2 * P].rearrange("p (r n) -> p r n", r=2)
        ends = {k: arena[:, 0:NB * w].rearrange("p (b w) -> p b w", w=w) for k, w in W_OF.items()}
        agg = gat[:, 0:CB * 5 * F].rearrange("p (b c) -> p b c", c=5 * F)
        aggt = gat[:, CB * 5 * F:CB * 5 * F + 6 * P].rearrange("p (r k n) -> p r k n", r=2, k=3)
        vu = arena[:, 0:NB * 2 * HID].rearrange("p (b w) -> p b w", w=2 * HID)
        used = [0]

        def carve(rows, *free):
            n = int(np.prod(free))
            part = mid[0:rows, used[0]:used[0] + n]
            used[0] += n
            return part.rearrange("p (k n) -> p k n", k=free[0]) if len(free) > 1 else part

        dcur = arena[:, 0:NT].bitcast(i32)
        dprev = arena[:, NT:2 * NT].bitcast(i32)
        keep0 = keep[:, 0, 0:NT]
        lasti = arena[:, 2 * NT:3 * NT].bitcast(i32)
        lastf = arena[:, 3 * NT:4 * NT]
        lcmp = arena[:, 4 * NT:5 * NT]
        drow = arena[:, 0:NP].rearrange("p (b n) -> p b n", n=P).bitcast(i32)
        dcmp = arena[:, NP:2 * NP].rearrange("p (b n) -> p b n", n=P)
        tcount = st1
        tidx = carve(P, NB).bitcast(i32)
        pdst = arena[:, 0:SC * P].rearrange("p (c n) -> p c n", n=P)
        psrc = arena[:, SC * P:2 * SC * P].rearrange("p (c n) -> p c n", n=P)
        pw = arena[:, 2 * SC * P:3 * SC * P].rearrange("p (c n) -> p c n", n=P)
        in_group = tmp[:, 0:NB // 2 * 2, :].rearrange("p (b r) f -> p b (r f)", r=2)
        pblk = gat[:, 0:SC * P].rearrange("p (c n) -> p c n", n=P)
        slotf = arena[:, 0:NGR]
        scmp = arena[:, NGR:2 * NGR]
        slots = arena[:, 2 * NGR:3 * NGR].bitcast(i32)
        sid = carve(P, SC)
        gs = carve(P, SC)
        gs4 = carve(P, SC)
        tsf = carve(P, SC)
        ts = carve(P, SC).bitcast(i32)
        gsm = carve(P, SC)
        endt = carve(NB, GB)
        endi = carve(NB, GB).bitcast(i32)
        endg = carve(NB, GB)
        samet = carve(SC, P)
        samen = carve(SC, P)
        destf = carve(SC, P)
        desti = carve(SC, P).bitcast(i32)
        spare = carve(SC, P)
        turned_in = acc[:, 0:24, :].rearrange("p b f -> p (b f)").rearrange("p (r k n) -> p r k n", r=4, k=3)
        ccount = st2
        ub = carve(P, NB)
        eint = carve(P, NB).bitcast(i32)
        epart = carve(P, 3, NB).bitcast(i32)
        pet = [carve(F, F) for l in range(2)]
        wlt = [carve(F, F) for l in range(2)]
        we = [carve(F, FE16) for l in range(2)]
        be = [carve(F, 1) for l in range(2)]
        bo = [carve(F, 1) for l in range(2)]
        bp = [carve(1, F) for l in range(2)]
        bl = [carve(1, F) for l in range(2)]
        wo = [gat[0:F, 1024 * l:1024 * (l + 1)] for l in range(2)]

        ld_w = sem("weights_loaded")
        ld_d = sem("dst_loaded")
        made = sem("constants_made")
        keep_ok = sem("keep_made")
        keep_st = sem("keep_stored")
        t_ok = sem("tile_index_made")
        drow_ok = sem("dst_rows_gathered")
        ub_ok = sem("upper_bounds_made")
        ubp_ok = sem("bounds_shifted")
        wps = sem("weight_products")
        wcp = sem("weight_products_copied")
        ld = [sem(f"group_loaded{q}") for q in range(2)]
        gt = [[sem(f"gathered{k}_{q}") for q in range(2)] for k in range(NPASS)]
        ends_ok = sem("group_ends_made")
        ends_st = sem("group_ends_stored")
        slot_ld = sem("group_ends_loaded")
        pair_ok = sem("pair_tiles_made")
        pair_ld = sem("pair_edges_gathered")
        pkey_ok = sem("pair_keys_made")
        pair_t = sem("pair_keys_turned")
        pair_s = sem("pair_keys_copied")
        pair_st = [sem(f"pair_keys_stored{r}") for r in range(4)]
        sh_ok = sem("pairs_shifted")
        same_in = sem("same_group_flags")
        same_t = sem("same_group_turned")
        same_ok = sem("same_group_made")
        same_st = sem("same_group_stored")
        hot = sem("one_hots_made")
        bld = sem("pair_products")
        acd = sem("pair_rows_added")
        ast = [sem(f"pair_rows_stored{r}") for r in range(2)]
        samen_ld = sem("next_flags_loaded")
        dest_ok = sem("pair_places_made")
        dst_ld = sem("destinations_loaded")
        b2_ld = sem("late_biases_loaded")
        dest_st = sem("pair_places_stored")
        ablk_ld = [sem(f"block_loaded{r}") for r in range(2)]
        lnp = sem("block_product")
        ltc = sem("block_product_kept")
        lbt = sem("block_product_turned")
        lnc = sem("block_product_copied")
        lxr = sem("propagation_input_ready")
        zt = sem("turned")
        md = sem("mid_ready")
        scn = sem("scanned")
        bt = sem("turned_back")
        ev = sem("evacuated")
        st = [sem(f"rows_stored{q}") for q in range(2)]
        er = sem("ends_gathered")
        xr = sem("x_ready")
        staged = sem("indices_staged")
        go = sem("group_gathers_begun")
        go_sp = sem("group_fetches_begun")
        go_pe = sem("block_turns_begun")
        xin = sem("x_loaded_again")
        xtp = sem("x_turned")
        xts = sem("xt_stored")
        pjp = sem("projected")
        pjs = sem("projection_copied")
        tbr = sem("table_rows_ready")
        tab = sem("table_stored")
        agr = sem("agg_ready")
        atp = sem("agg_turned")
        ats = sem("aggt_copied")
        omp = sem("post_product")
        oms = sem("post_used")
        rq = sem("root_asked")
        rs = sem("root_done")
        bns = sem("bn_rows_ready")
        bnp = sem("bn_summed")
        m_e = sem("mlp_sum_turned")
        m_et = sem("mlp_sum_copied")
        m_a = sem("mlp_message")
        m_as = sem("mlp_message_biased")
        m_t = sem("mlp_message_turned")
        m_ts = sem("mlp_message_copied")
        m_h = sem("mlp_hidden")
        m_hs = sem("mlp_hidden_relu")
        m_o = sem("mlp_out")
        m_os = sem("mlp_out_used")
        dch = sem("vector_chain")
        fin = sem("result_ready")
        outs = sem("result_stored")
        block = ctx.enter_context(nc.Block())

        def reach(eng, s, base, rel):
            if isinstance(rel, int):
                rel = max(rel, 0)
                if base + rel == 0:
                    return
            eng.wait_ge(s, rel + base)

        def turns(eng, body):
            body(0)
            with eng.Fori(1, NI) as i:
                body(i)

        def blocks(eng, body):
            for b in range(3):
                body(b, b // 2, b % 2)
            with eng.Fori(1, (NB - 1) // 2) as i:
                body(2 * i + 1, i, 1)
                body(2 * i + 2, i + 1, 0)

        def bcast(ap, n):
            return ap.unsqueeze(2).broadcast_to([P, ap.shape[1], n])

        def chunks(n, size):
            return [(j, j * size, min(size, n - j * size)) for j in range(-(-n // size))]

        wl = []

        @block.sync
        def _(sp):
            sp.dma_start(dcur, inp["dst_pad"][1:1 + EP].rearrange("(p n) -> p n", p=P)).then_inc(ld_d, 16)
            sp.dma_start(dprev, inp["dst_pad"][0:EP].rearrange("(p n) -> p n", p=P)).then_inc(ld_d, 16)
            sp.dma_start(lasti, inp["dst_last"].partition_broadcast(P)).then_inc(ld_d, 16)

            def w(dst, src):
                wl.append(1)
                sp.dma_start(dst, src).then_inc(ld_w, 16)

            for l in range(2):
                w(proj[l][:, 0:F], inp["wpT"][l, F:2 * F, :])
                w(proj[l][:, F:2 * F], inp["wpT"][l, 0:F, :])
                w(pet[l][:, :], inp["wpT"][l, 2 * F:3 * F, :])
                w(wlt[l][:, :], inp["wlT"][l, :, :])
                w(we[l][:, :], inp["we"][l, :, :])
                w(be[l][:, :], inp["be"][l:l + 1, :].rearrange("a f -> f a"))
                w(bo[l][:, :], inp["bo"][l:l + 1, :].rearrange("a f -> f a"))
                w(bp[l][:, :], inp["bp"][l:l + 1, :])
                w(bl[l][:, :], inp["bl"][l:l + 1, :])
                w(wo[l], inp["wo"][l, :, :])
                w(gam[l][:, :], inp["gam"][l, :].partition_broadcast(P))
                w(bet[l][:, :], inp["bet"][l, :].partition_broadcast(P))
            w(src_all[:, :], inp["src_t"])
            w(cur[:, :, :], inp["x"].rearrange("(b p) f -> p b f", p=P))
            w(p3[:, 0:HID], inp["mw1"][0:F, :])
            w(p3[:, HID:2 * HID], inp["mw1"][F:2 * F, :])
            w(p3b[:, HID:2 * HID], inp["mb1"].rearrange("(a f) -> a f", a=1))
            w(w1c[:, :], inp["mw1"][2 * F:2 * F + FE32, :])
            w(w2[:, :], inp["mw2"])
            w(u1a[:, :], inp["uw1"][0:F, :])
            w(u1b[:, :], inp["uw1"][F:2 * F, :])
            w(ub1[:, :], inp["ub1"].rearrange("(f a) -> f a", a=1))
            w(u2[:, :], inp["uw2"])
            sp.wait_ge(keep_ok, 1)
            sp.dma_start(keep_d.rearrange("g n -> (g n)").rearrange("(p n) -> p n", p=P), keep0).then_inc(keep_st, 16)
            sp.wait_ge(keep_st, 16)
            sp.wait_ge(ends_ok, 1)
            sp.dma_start(ends_d.rearrange("(b g) -> b g", b=NB), endi[:, :]).then_inc(ends_st, 16)
            sp.wait_ge(ends_st, 16)
            sp.dma_start(slots[:, :], ends_d.partition_broadcast(P)).then_inc(slot_ld, 16)
            sp.wait_ge(same_ok, 1)
            sp.dma_start(same_d[0:SC * P].rearrange("(c n) -> c n", c=SC), samet[:, :]).then_inc(same_st, 16)
            sp.dma_start(same_d[SC * P:SC * P + 1].rearrange("(c n) -> c n", c=1), samet[0:1, 0:1]).then_inc(same_st, 16)
            sp.wait_ge(same_st, 32)
            sp.dma_start(samen[:, :], same_d[1:SC * P + 1].rearrange("(c n) -> c n", c=SC)).then_inc(samen_ld, 16)
            sp.wait_ge(dest_ok, 1)
            sp.dma_start(dest_d.rearrange("(c n) -> c n", c=SC), desti[:, :]).then_inc(dest_st, 16)
            for c in range(SC):
                sp.wait_ge(pair_s, c + 1)
                sp.dma_start(step_d[:, :, c * P:(c + 1) * P], turned_in[:, c % 4, :, :]).then_inc(pair_st[c % 4], 16)
            for c in range(4):
                sp.wait_ge(pair_st[c], 16 * len(range(c, SC, 4)))
            sp.wait_ge(dest_st, 16)

            def store_pairs(k, g, s, q):
                n = SUB * g + s
                reach(sp, acd, PR0[k], 4 * (n + 1))
                sp.sem_inc(go_sp, 1)
                for m in range(4):
                    v = sp.value_load(dest[0:1, q, 4 * s + m:4 * s + m + 1], min_val=0, max_val=(NGR + SPARE - 1) * P)
                    sp.dma_start(group_d[bass.ds(v, P), :], stage[:, s % 2, m, :]).then_inc(ast[s % 2], 16)

            for k, kind in enumerate(KINDS):
                if k == 2:
                    sp.wait_ge(er, ER0[2])
                    for q in range(2):
                        sp.wait_ge(ast[q], 256 * NG)
                    sp.dma_start(dst_all, inp["dst_t"]).then_inc(dst_ld, 16)
                    sp.dma_start(b2, inp["mb2"].partition_broadcast(P)).then_inc(b2_ld, 16)
                    sp.dma_start(ub2, inp["ub2"].partition_broadcast(P)).then_inc(b2_ld, 16)
                    for j in range(5):
                        def load_block(b, c, r):
                            reach(sp, lnp, 0, NB * j + b - 1)
                            sp.dma_start(ablk[:, (r + j) % 2, :, :, :].rearrange("p g s d -> p g (s d)"),
                                         group_d[0:NGR * P, :].rearrange("(n g p) w -> n p g w", g=GB, p=P)[
                                             b, :, :, :]).then_inc(ablk_ld[(r + j) % 2], 16)

                        blocks(sp, load_block)
                sp.wait_ge(tbr, k + 1)
                if kind == "mlp":
                    sp.dma_start(vtab.rearrange("(b p) f -> p b f", p=P), vu[:, :, 0:HID]).then_inc(tab, 16)
                    sp.dma_start(utab.rearrange("(b p) f -> p b f", p=P), vu[:, :, HID:2 * HID]).then_inc(tab, 16)
                else:
                    rows = tmp if kind == "pna" else acc
                    sp.dma_start(table.rearrange("(b p) f -> p b f", p=P), rows[:, :, :]).then_inc(tab, 16)

                def body(i):
                    for q in range(2):
                        reach(sp, scn, SC0[k], (2 * i + q - 1) * SUB * SCANS[kind])
                        g = 2 * i + q
                        sp.dma_start(keep[:, q, :], keep_d[g, :].partition_broadcast(P)).then_inc(ld[q], 16)
                        if kind == "pna":
                            sp.dma_start(attr[0:FE16, q, :], inp["a16_g"][g, :, :]).then_inc(ld[q], 16)
                            at = bass.ds(PR0[k] + g * SG, SG)
                            sp.dma_start(step_in[:, q, :, :], step_d[:, :, at]).then_inc(ld[q], 16)
                            sp.dma_start(same[:, q, :], same_d[at].partition_broadcast(P)).then_inc(ld[q], 16)
                            sp.dma_start(dest[:, q, :], dest_d[at].rearrange("(a n) -> a n", a=1)).then_inc(ld[q], 16)
                            if not (isinstance(i, int) and i == 0 and q == 0):
                                for s in range(SUB):
                                    store_pairs(k, g - 1, s, 1 - q)
                        if kind == "mlp":
                            sp.dma_start(attr[:, q, :], inp["a32_g"][g, :, :]).then_inc(ld[q], 16)

                turns(sp, body)
                if kind == "pna":
                    for s in range(SUB):
                        store_pairs(k, NG - 1, s, 1)
                if k == 1:
                    sp.wait_ge(bns, 3)
                    sp.dma_start(adst[:, :, :], inp["x"].rearrange("(b p) f -> p b f", p=P)).then_inc(xin, 16)
            sp.wait_ge(fin, 1)
            full = N // P
            sp.dma_start(out[0:full * P, :].rearrange("(b p) f -> p b f", p=P), acc[:, 0:full, :]).then_inc(outs, 16)
            sp.dma_start(out[full * P:N, :], acc[0:N - full * P, full, :]).then_inc(outs, 16)
            sp.wait_ge(outs, 32)

        @block.gpsimd
        def _(pool):
            pool.memset(ident[:, :], 0.0).then_inc(made, 1)
            pool.memset(ones[:, :], 1.0).then_inc(made, 1)
            pool.memset(lim_buf[:, 0:2 * P], 0.0).then_inc(made, 1)
            pool.iota(inid, pattern=[[P, NB]], base=0, channel_multiplier=1).then_inc(made, 1)
            pool.iota(isid, pattern=[[P, SC]], base=0, channel_multiplier=1).then_inc(made, 1)
            pool.iota(icol, pattern=[[1, AW]], base=0, channel_multiplier=0).then_inc(made, 1)
            pool.iota(isp, pattern=[[0, P // SPARE], [1, SPARE]], base=NGR, channel_multiplier=0).then_inc(made, 1)
            pool.iota(igrp, pattern=[[1, GB]], base=0, channel_multiplier=GB).then_inc(made, 1)
            pool.wait_ge(made, 8)
            pool.affine_select(out=ident[:, :], in_=ident[:, :], compare_op=ALU.not_equal, fill=1.0,
                               base=0, pattern=[[-1, P]], channel_multiplier=1).then_inc(made, 1)
            pool.affine_select(out=down, in_=down, compare_op=ALU.not_equal, fill=1.0,
                               base=1, pattern=[[-1, P]], channel_multiplier=1).then_inc(made, 1)
            pool.affine_select(out=corner, in_=corner, compare_op=ALU.not_equal, fill=1.0,
                               base=1 - P, pattern=[[P, P]], channel_multiplier=1).then_inc(made, 1)
            pool.wait_ge(t_ok, 1)
            for b in range(NB):
                pool.indirect_dma_start(drow[:, b, :], None, inp["dst_tiles"],
                                        bass.IndirectOffsetOnAxis(ap=tidx[:, b:b + 1], axis=0)).then_inc(drow_ok, 16)
            pool.wait_ge(pair_ok, 1)
            for c in range(SC):
                for dst, src in ((pdst.bitcast(i32), "dst_tiles"), (psrc.bitcast(i32), "src_tiles"), (pw, "w_tiles")):
                    pool.indirect_dma_start(dst[:, c, :], None, inp[src], bass.IndirectOffsetOnAxis(
                        ap=ts[:, c:c + 1], axis=0)).then_inc(pair_ld, 16)
            need = 0
            for k, kind in enumerate(KINDS):
                need += 16 * TABLES[kind]
                pool.wait_ge(tab, need)

                if k == 2:
                    pool.wait_ge(dst_ld, 16)

                def body(i):
                    for q in range(2):
                        g = 2 * i + q
                        reach(pool, gt[k][q], 0, 16 * TG * TABLES[kind] * i)
                        reach(pool, zt, ONE0[k], SUB * (g - 1))
                        pool.sem_inc(go, 1)
                        pool.tensor_copy(idx[:, q, :], src_all[:, bass.ds(g * TG, TG)]).then_inc(staged, 1)
                        if kind == "mlp":
                            pool.tensor_copy(idx2[:, q, :], dst_all[:, bass.ds(g * TG, TG)]).then_inc(staged, 1)
                        reach(pool, staged, SG0[k], TABLES[kind] * (g + 1))
                        pool.sem_inc(go, 1)
                        for t in range(TG):
                            if kind == "mlp":
                                pool.indirect_dma_start(gat_m[:, q, t, :], None, vtab, bass.IndirectOffsetOnAxis(
                                    ap=idx[:, q, t:t + 1], axis=0)).then_inc(gt[k][q], 16)
                                pool.indirect_dma_start(ugat[:, q, t, :], None, utab, bass.IndirectOffsetOnAxis(
                                    ap=idx2[:, q, t:t + 1], axis=0)).then_inc(gt[k][q], 16)
                            else:
                                pool.indirect_dma_start(gat_l[:, q, t, :], None, table, bass.IndirectOffsetOnAxis(
                                    ap=idx[:, q, t:t + 1], axis=0)).then_inc(gt[k][q], 16)

                turns(pool, body)
                for q in range(2):
                    pool.wait_ge(st[q], ST0[k + 1])
                for b in range(NB):
                    pool.indirect_dma_start(ends[kind][:, b, :], None, scan_d[kind], bass.IndirectOffsetOnAxis(
                        ap=eidx[:, b:b + 1], axis=0)).then_inc(er, 16)

        @block.vector
        def _(dve):
            chain = [0]

            def link(ins):
                chain[0] += 1
                ins.then_inc(dch, 1)
                dve.wait_ge(dch, chain[0])

            dve.wait_ge(ld_d, 48)
            dve.tensor_tensor(keep0, dcur, dprev, ALU.is_equal).then_inc(keep_ok, 1)
            dve.memset(sgn[0:F, :], 1.0)
            dve.memset(sgn[F:2 * F, :], -1.0)
            for l in range(2):
                dve.memset(wpost[l][:, :, :], 0.0)
                dve.memset(wx[l][:, :], 0.0)
                dve.memset(wxb[l][:, :], 0.0)
                dve.memset(projb[l][:, :], 0.0)
            link(dve.memset(p3b[:, 0:HID], 0.0))
            dve.wait_ge(made, 11)
            link(dve.tensor_copy(nid[:, :], inid))
            dve.tensor_copy(sid[:, :], isid)
            dve.tensor_copy(iota_c[:, :], icol)
            dve.tensor_copy(spare[:, :], isp)
            link(dve.tensor_copy(endg[:, :], igrp))
            link(dve.memset(stage[:, :, :, :], 0.0))
            link(dve.tensor_scalar(valid[:, :], nid[:, :], float(N), None, ALU.is_lt))
            link(dve.tensor_copy(lastf, lasti))
            for b in range(NB):
                link(dve.tensor_scalar(lcmp, lastf, nid[:, b:b + 1], None, ALU.is_le))
                link(dve.reduce_sum(tcount[:, b:b + 1], lcmp, AX))
            link(dve.tensor_copy(tidx[:, :], tcount[:, :]))
            dve.wait_ge(keep_st, 16)
            dve.memset(st2[:, 0:1], 0.0).then_inc(t_ok, 1)
            dve.wait_ge(drow_ok, 16 * NB)
            link(dve.tensor_tensor(dcmp, drow, bcast(nid[:, :], P), ALU.is_le))
            link(dve.reduce_sum(ccount[:, :], dcmp, AX))
            link(dve.scalar_tensor_tensor(out=ub[:, :], in0=tcount[:, :], scalar=float(P), in1=ccount[:, :],
                                          op0=ALU.mult, op1=ALU.add))
            link(dve.tensor_scalar(st1[:, :], ub[:, :], 1.0, -1.0, ALU.max, ALU.add))
            dve.tensor_copy(eint[:, :], st1[:, :]).then_inc(ub_ok, 1)
            dve.wait_ge(ub_ok, 1)
            link(dve.tensor_scalar(epart[:, 0, :], eint[:, :], P - 1, 4, ALU.bitwise_and, ALU.logical_shift_left))
            link(dve.tensor_scalar(epart[:, 1, :], eint[:, :], 7, TG - 1, ALU.logical_shift_right, ALU.bitwise_and))
            link(dve.tensor_scalar(epart[:, 2, :], eint[:, :], 11, 11, ALU.logical_shift_right, ALU.logical_shift_left))
            link(dve.tensor_tensor(epart[:, 0, :], epart[:, 0, :], epart[:, 1, :], ALU.bitwise_or))
            link(dve.tensor_tensor(eidx[:, :], epart[:, 0, :], epart[:, 2, :], ALU.bitwise_or))
            dve.wait_ge(ubp_ok, 1)
            link(dve.tensor_tensor(cnt[:, :], ub[:, :], ps[:, 3, 0:NB], ALU.subtract))
            link(dve.tensor_scalar(nz[:, :], cnt[:, :], 1.0, None, ALU.min))
            link(dve.tensor_scalar(st1[:, :], cnt[:, :], 1.0, None, ALU.max))
            link(dve.reciprocal(rden[:, :], st1[:, :]))
            dve.tensor_scalar(st2[:, :], st1[:, :], 1.0, None, ALU.add).then_inc(rq, 1)
            dve.wait_ge(rs, ORD["log",])
            link(dve.reciprocal(st1[:, :], st2[:, :]))
            link(dve.tensor_scalar(amp[:, :], st2[:, :], 1.0 / AVG, None, ALU.mult))
            link(dve.tensor_scalar(att[:, :], st1[:, :], AVG, None, ALU.mult))
            link(dve.tensor_copy(endi[:, :], ps[0:NB, 4, D4 - 1:P:D4]))
            link(dve.tensor_scalar(endi[:, :], endi[:, :], 7, 0, ALU.logical_shift_right, ALU.logical_shift_left))
            link(dve.tensor_copy(endt[:, :], endi[:, :]))
            link(dve.tensor_tensor(endt[:, :], endt[:, :], endg[:, :], ALU.add))
            dve.tensor_copy(endi[:, :], endt[:, :]).then_inc(ends_ok, 1)
            dve.wait_ge(slot_ld, 16)
            link(dve.tensor_copy(slotf, slots[:, :]))
            for c in range(SC):
                link(dve.tensor_scalar(scmp, slotf, sid[:, c:c + 1], None, ALU.is_lt))
                link(dve.reduce_sum(gs[:, c:c + 1], scmp, AX))
            link(dve.tensor_tensor(tsf[:, :], sid[:, :], gs[:, :], ALU.subtract))
            link(dve.tensor_scalar(tsf[:, :], tsf[:, :], float(NT - 1), None, ALU.min))
            link(dve.tensor_scalar(gs4[:, :], gs[:, :], float(D4), None, ALU.mult))
            dve.tensor_copy(ts[:, :], tsf[:, :]).then_inc(pair_ok, 1)
            dve.wait_ge(sh_ok, 1)
            dve.tensor_tensor(gsm[:, :], gs[:, :], ps[:, 5, 0:SC], ALU.is_equal).then_inc(same_in, 1)
            dve.wait_ge(same_t, 1)
            dve.tensor_copy(samet[:, :], ps[0:SC, 6, 0:P]).then_inc(same_ok, 1)
            link(dve.tensor_copy(destf[:, :], ps[0:SC, 6, P:2 * P]))
            link(dve.tensor_tensor(spare[:, :], spare[:, :], destf[:, :], ALU.subtract))
            dve.wait_ge(samen_ld, 16)
            link(dve.tensor_tensor(spare[:, :], spare[:, :], samen[:, :], ALU.mult))
            link(dve.tensor_tensor(destf[:, :], destf[:, :], spare[:, :], ALU.add))
            dve.tensor_scalar(desti[:, :], destf[:, :], float(P), None, ALU.mult).then_inc(dest_ok, 1)
            for l in range(2):
                dve.wait_ge(wps, l + 1)
                dve.tensor_copy(gw[l][:, 0:F], ps[0:FE16, 0, 0:F])
                dve.tensor_copy(gw[l][:, F:2 * F], ps[0:FE16, 0, 0:F])
                dve.tensor_tensor(projb[l][:, F:2 * F], ps[0:1, 0, F:2 * F], bp[l][:, :], ALU.add)
                dve.tensor_copy(wx[l][:, 0:F], ps[0:F, 0, 2 * F:3 * F])
                dve.tensor_tensor(wxb[l][:, 0:F], ps[0:1, 0, 3 * F:4 * F], bl[l][:, :], ALU.add)
                dve.tensor_copy(wpost[l][:, 0:2, :], ps[:, 1, 0:6 * F].rearrange("p (k n) -> p k n", k=2))
                dve.tensor_copy(wpost[l][0:F, 2, :], ps[0:F, 2, 0:3 * F]).then_inc(wcp, 1)
            dve.wait_ge(pair_ld, 16 * 3 * SC)
            link(dve.tensor_copy(pdst, pdst.bitcast(i32)))
            link(dve.tensor_tensor(pdst, pdst, bcast(gs4[:, :], P), ALU.subtract))
            link(dve.tensor_scalar(pblk.bitcast(i32), psrc.bitcast(i32), 7, 0, ALU.logical_shift_right,
                                   ALU.logical_shift_left))
            link(dve.tensor_copy(pblk, pblk.bitcast(i32)))
            link(dve.scalar_tensor_tensor(out=pblk, in0=pblk, scalar=float(D4), in1=pdst, op0=ALU.mult, op1=ALU.add))
            for c in range(0, SC, NB * F // P):
                cs = slice(c, min(SC, c + NB * F // P))
                inside = in_group[:, 0:cs.stop - cs.start, :]
                link(dve.tensor_scalar(inside, pdst[:, cs, :], 0.0, None, ALU.is_ge))
                link(dve.tensor_scalar(pdst[:, cs, :], pdst[:, cs, :], float(D4 - 1), None, ALU.is_le))
                link(dve.tensor_tensor(pdst[:, cs, :], pdst[:, cs, :], inside, ALU.mult))
            link(dve.tensor_scalar(pblk, pblk, 1.0, None, ALU.add))
            link(dve.tensor_tensor(pdst, pdst, pblk, ALU.mult))
            link(dve.tensor_scalar(pdst, pdst, -1.0, None, ALU.add))
            link(dve.tensor_scalar(psrc.bitcast(i32), psrc.bitcast(i32), P - 1, 0, ALU.bitwise_and, ALU.bitwise_or))
            dve.tensor_copy(psrc, psrc.bitcast(i32)).then_inc(pkey_ok, 1)

            def layer_norm(n, src, res):
                link(dve.reduce_sum(st1[:, :], src[:, :, :], AX))
                link(dve.tensor_scalar(st1[:, :], st1[:, :], 1.0 / F, None, ALU.mult))
                link(dve.tensor_tensor(src[:, :, :], src[:, :, :], bcast(st1[:, :], F), ALU.subtract))
                link(dve.tensor_tensor(tmp[:, :, :], src[:, :, :], src[:, :, :], ALU.mult))
                link(dve.reduce_sum(st2[:, :], tmp[:, :, :], AX))
                dve.tensor_scalar(st2[:, :], st2[:, :], 1.0 / F, EPS, ALU.mult, ALU.add).then_inc(rq, 1)
                dve.wait_ge(rs, ORD["ln", n])
                link(dve.reciprocal(st2[:, :], st2[:, :]))
                link(dve.tensor_tensor(res[:, :, :], src[:, :, :], bcast(st2[:, :], F), ALU.mult))

            def projection(k):
                for j in range(PJN[k]):
                    dve.wait_ge(pjp, PJ0[k] + j + 1)
                    if k == 2:
                        n = min(2, NB - 2 * j)
                        dve.tensor_copy(vu[:, 2 * j:2 * j + n, :], ps[:, 4 + j % 4, 0:n * 2 * HID].rearrange(
                            "p (b w) -> p b w", b=n)).then_inc(pjs, 1)
                    else:
                        n = min(4, NB - 4 * j)
                        v = ps[:, 4 + j % 4, 0:n * 2 * F].rearrange("p (b w) -> p b w", b=n)
                        dve.tensor_copy(tmp[:, 4 * j:4 * j + n, :], v[:, :, 0:F])
                        dve.tensor_copy(adst[:, 4 * j:4 * j + n, :], v[:, :, F:2 * F]).then_inc(pjs, 1)
                dve.wait_ge(pjs, PJ0[k] + PJN[k])
                dve.memset(st2[:, 0:1], 0.0).then_inc(tbr, 1)

            def segment_scans(k, kind):
                def body(i):
                    for q in range(2):
                        g = 2 * i + q
                        reach(dve, ld[q], LD0[k], 16 * LOADS[kind] * (i + 1))
                        for s in range(SUB):
                            n = SUB * g + s
                            if kind == "pna":
                                cols = step_in[:, q, :, 4 * s:4 * s + 4]
                                dve.tensor_tensor(hot_l, iota_c[:, 0:P].unsqueeze(1).broadcast_to([P, 4, P]),
                                                  bcast(cols[:, 1, :], P), ALU.is_equal).then_inc(hot, 1)
                                for m in range(4):
                                    dve.tensor_scalar(hot_r[:, m, :], iota_c[:, :], cols[:, 0, m:m + 1],
                                                      cols[:, 2, m:m + 1], ALU.is_equal, ALU.mult).then_inc(hot, 1)
                            reach(dve, md, MD0[k], MIDS[kind] * (n + 1))
                            data = qm[:, s % 2, 0, :]
                            reach(dve, bt, ONE0[k], n - SUB + 1)
                            reach(dve, scn, SC0[k], SCANS[kind] * n)
                            here = slice(s * SE, (s + 1) * SE)
                            last = (s * SE - 1) % GE
                            dve.tensor_tensor_scan(scan[:, 0, here], keep[:, q, here], data,
                                                   scan[:, 0, last:last + 1], ALU.mult, ALU.add).then_inc(scn, 1)
                            if kind == "pna":
                                dve.tensor_tensor_scan(scan[:, 1, here], lim[:, s % 2, :], qm[:, s % 2, 1, :],
                                                       scan[:, 1, last:last + 1], ALU.min, ALU.max).then_inc(scn, 1)
                                reach(dve, bld, ONE0[k], n + 1)
                                reach(dve, ast[s % 2], 128 * NG * k, 64 * (2 * g + s // 2))
                                for m in range(4):
                                    reach(dve, acd, PR0[k], 4 * n + m)
                                    last_row = stage[:, s % 2, m - 1, :] if m else stage[:, 1 - s % 2, 3, :]
                                    dve.scalar_tensor_tensor(
                                        out=stage[:, s % 2, m, :], in0=last_row,
                                        scalar=same[:, q, 4 * s + m:4 * s + m + 1],
                                        in1=ps[:, 2 + m // 2, (m % 2) * AW:(m % 2 + 1) * AW],
                                        op0=ALU.mult, op1=ALU.add).then_inc(acd, 1)

                turns(dve, body)
                dve.wait_ge(er, ER0[k + 1])

            def pna_nodes(l):
                e = ends["pna"]
                for c in range(NB // CB):
                    bs = slice(c * CB, (c + 1) * CB)
                    reach(dve, atp, NB * l, c * CB)
                    mean, mn, mx, std, ssum = (agg[:, :, f * F:(f + 1) * F] for f in range(5))
                    rd, z = bcast(rden[:, bs], F), bcast(nz[:, bs], F)
                    a = adst[:, bs, :]
                    link(dve.tensor_tensor(mean, e[:, bs, 0:F], rd, ALU.mult))
                    link(dve.tensor_tensor(std, e[:, bs, F:2 * F], rd, ALU.mult))
                    link(dve.tensor_tensor(ssum, mean, mean, ALU.mult))
                    link(dve.tensor_tensor(std, std, ssum, ALU.subtract))
                    link(dve.tensor_tensor(std, std, z, ALU.mult))
                    dve.tensor_scalar(std, std, 0.0, EPS, ALU.max, ALU.add).then_inc(rq, 1)
                    link(dve.tensor_tensor(mean, mean, a, ALU.add))
                    link(dve.tensor_tensor(mean, mean, z, ALU.mult))
                    link(dve.tensor_tensor(mn, a, e[:, bs, 3 * F:4 * F], ALU.subtract))
                    link(dve.tensor_tensor(mn, mn, z, ALU.mult))
                    link(dve.tensor_tensor(mx, a, e[:, bs, 2 * F:3 * F], ALU.add))
                    link(dve.tensor_tensor(mx, mx, z, ALU.mult))
                    dve.tensor_tensor(ssum, mean, bcast(cnt[:, bs], F), ALU.mult).then_inc(agr, 1)
                    for b in range(c * CB, (c + 1) * CB):
                        dve.wait_ge(omp, NB * l + b + 1)
                        o = ps[:, 4 + b % 4, :]
                        link(dve.tensor_copy(acc[:, b, :], o[:, 0:F]))
                        link(dve.scalar_tensor_tensor(out=acc[:, b, :], in0=o[:, F:2 * F], scalar=amp[:, b:b + 1],
                                                      in1=acc[:, b, :], op0=ALU.mult, op1=ALU.add))
                        dve.scalar_tensor_tensor(out=acc[:, b, :], in0=o[:, 2 * F:3 * F], scalar=att[:, b:b + 1],
                                                 in1=acc[:, b, :], op0=ALU.mult, op1=ALU.add).then_inc(oms, 1)
                dve.wait_ge(oms, NB * (l + 1))
                v = valid[:, NB - 1:NB]
                dve.tensor_scalar(acc[:, NB - 1, :], acc[:, NB - 1, :], v, None, ALU.mult).then_inc(bns, 1)
                dve.wait_ge(bnp, 2 * l + 1)
                fold = ps[:, 0, 0:7 * F].rearrange("p (b f) -> p f b", f=F)
                link(dve.reduce_sum(mu[:, :], fold, AX))
                link(dve.tensor_scalar(mu[:, :], mu[:, :], 1.0 / N, None, ALU.mult))
                mub = mu[:, :].unsqueeze(1).broadcast_to([P, NB, F])
                link(dve.tensor_tensor(acc[:, :, :], acc[:, :, :], mub, ALU.subtract))
                link(dve.tensor_scalar(acc[:, NB - 1, :], acc[:, NB - 1, :], v, None, ALU.mult))
                dve.tensor_tensor(tmp[:, :, :], acc[:, :, :], acc[:, :, :], ALU.mult).then_inc(bns, 1)
                dve.wait_ge(bnp, 2 * l + 2)
                link(dve.reduce_sum(sd[:, :], fold, AX))
                dve.tensor_scalar(sd[:, :], sd[:, :], 1.0 / N, EPS, ALU.mult, ALU.add).then_inc(rq, 1)
                dve.wait_ge(rs, ORD["bn", l, 0])
                link(dve.reciprocal(sd[:, :], sd[:, :]))
                link(dve.tensor_tensor(sd[:, :], sd[:, :], gam[l][:, :], ALU.mult))
                sdb = sd[:, :].unsqueeze(1).broadcast_to([P, NB, F])
                bb = bet[l][:, :].unsqueeze(1).broadcast_to([P, NB, F])
                link(dve.tensor_tensor(acc[:, :, :], acc[:, :, :], sdb, ALU.mult))
                link(dve.tensor_tensor(acc[:, :, :], acc[:, :, :], bb, ALU.add))
                if l == 0:
                    dve.tensor_scalar(cur[:, :, :], acc[:, :, :], 0.0, None, ALU.max).then_inc(xr, 1)
                else:
                    link(dve.tensor_scalar(acc[:, :, :], acc[:, :, :], 0.0, None, ALU.max))
                    dve.wait_ge(xin, 16)
                    link(dve.tensor_tensor(acc[:, :, :], acc[:, :, :], adst[:, :, :], ALU.add))
                    layer_norm(0, acc, cur)
                    dve.memset(first_rows[:, :, F], 1.0).then_inc(lxr, 1)
                    dve.tensor_copy(first_rows[:, :, 0:F], cur[:, :, :]).then_inc(lxr, 1)

            dve.wait_ge(ld_w, 16 * len(wl))
            link(dve.memset(scan[:, :, GE - 1:GE], 0.0))
            for l in range(2):
                projection(l)
                segment_scans(l, "pna")
                pna_nodes(l)
            dve.wait_ge(lnc, 3 * NB)
            dve.tensor_scalar(st2[:, :], norm[:, :], 1.0, None, ALU.max).then_inc(rq, 1)
            dve.wait_ge(rs, ORD["norm",])
            link(dve.reciprocal(norm[:, :], st2[:, :]))
            link(dve.tensor_tensor(acc[:, :, :], acc[:, :, :], cur[:, :, :], ALU.add))
            layer_norm(1, acc, cur)
            nb = bcast(norm[:, :], F)
            link(dve.tensor_copy(adst[:, :, :], cur[:, :, :]))
            dve.tensor_tensor(acc[:, :, :], cur[:, :, :], nb, ALU.mult).then_inc(lxr, 1)
            for j in (3, 4):
                dve.wait_ge(lnc, (j + 1) * NB)
                link(dve.tensor_tensor(tmp[:, :, :], tmp[:, :, :], nb, ALU.mult))
                link(dve.tensor_tensor(adst[:, :, :], adst[:, :, :], tmp[:, :, :], ALU.add))
                if j == 3:
                    dve.tensor_tensor(acc[:, :, :], tmp[:, :, :], nb, ALU.mult).then_inc(lxr, 1)
            link(dve.tensor_scalar(adst[:, :, :], adst[:, :, :], 1.0 / 3.0, None, ALU.mult))
            link(dve.tensor_tensor(adst[:, :, :], adst[:, :, :], cur[:, :, :], ALU.add))
            layer_norm(2, adst, cur)
            link(dve.memset(scan[:, :, GE - 1:GE], 0.0))
            dve.memset(st1[:, 0:1], 0.0).then_inc(xr, 1)
            projection(2)
            segment_scans(2, "mlp")
            dve.wait_ge(b2_ld, 32)
            em = ends["mlp"]
            link(dve.tensor_tensor(em, em, bcast(nz[:, :], HID), ALU.mult))
            dve.memset(st1[:, 0:1], 0.0).then_inc(agr, 1)
            for j, b, n in chunks(NB, 4):
                dve.wait_ge(m_a, j + 1)
                b2b = b2[:, :].unsqueeze(1).broadcast_to([P, n, F])
                link(dve.tensor_tensor(acc[:, b:b + n, :], b2b, bcast(cnt[:, b:b + n], F), ALU.mult))
                dve.tensor_tensor(acc[:, b:b + n, :], acc[:, b:b + n, :],
                                  ps[:, 1, 0:n * F].rearrange("p (b f) -> p b f", b=n), ALU.add).then_inc(m_as, 1)
                dve.wait_ge(m_o, j + 1)
                u2b = ub2[:, :].unsqueeze(1).broadcast_to([P, n, F])
                link(dve.tensor_tensor(acc[:, b:b + n, :], ps[:, 4, 0:n * F].rearrange("p (b f) -> p b f", b=n), u2b,
                                       ALU.add))
                dve.tensor_tensor(acc[:, b:b + n, :], acc[:, b:b + n, :], cur[:, b:b + n, :], ALU.add).then_inc(m_os, 1)
            dve.wait_ge(m_os, NC4)
            layer_norm(3, acc, acc)
            dve.memset(st1[:, 0:1], 0.0).then_inc(fin, 1)

        @block.scalar
        def _(act):
            def root(name, ap, log=False):
                act.wait_ge(rq, ORD[name])
                act.activation(ap, ap, ACT.Ln if log else ACT.Sqrt).then_inc(rs, 1)

            def turned(k):
                for j, b, n in chunks(NB, 4):
                    act.wait_ge(xtp, XT0[k] + j + 1)
                    act.activation(xt[:, b * P:(b + n) * P], ps[0:F, j % 4, 0:n * P], ACT.Copy).then_inc(xts, 1)

            def evacuate(k, kind, g, s, q):
                w = W_OF[kind]
                n = SUB * g + s
                reach(act, bt, ONE0[k], n + 1)
                if s == 0:
                    reach(act, st[q], ST0[k], 8 * g - 8 * q)
                o = rows_out[kind][:, q, s * ST * w:(s + 1) * ST * w]
                if kind == "pna":
                    src = ps[:, 4 + 2 * (s % 2):6 + 2 * (s % 2), :].rearrange("p a n -> p (a n)")
                else:
                    src = ps[:, 4 + s, :]
                act.activation(o, src, ACT.Copy).then_inc(ev, 1)
                if s == SUB - 1:
                    reach(act, ev, ONE0[k], n + 1)
                    act.dma_start(scan_store[kind][g, :, :], rows_out[kind][:, q, 0:TG * w]).then_inc(st[q], 16)

            def rows(k, kind):
                def body(i):
                    for q in range(2):
                        g = 2 * i + q
                        for s in range(SUB):
                            n = SUB * g + s
                            if s == 0:
                                reach(act, ld[q], LD0[k], 16 * LOADS[kind] * (i + 1))
                            reach(act, zt, ONE0[k], n + 1)
                            reach(act, scn, SC0[k], SCANS[kind] * (n - 1))
                            if kind == "pna":
                                r = s % 2
                                act.activation(qm[0:F, r, 0, :], ps[0:F, r, :], ACT.Copy).then_inc(md, 1)
                                act.activation(qm[F:2 * F, r, 0, :], ps[F:2 * F, r, :], ACT.Square).then_inc(md, 1)
                                act.activation(qm[:, r, 1, :], ps[:, r, :], ACT.Copy, scale=sgn[:, 0:1]).then_inc(md, 1)
                                act.activation(lim[:, r, :], keep[:, q, s * SE:(s + 1) * SE], ACT.Copy,
                                               bias=-BIG, scale=2 * BIG).then_inc(md, 1)
                            if kind == "mlp":
                                act.activation(qm[:, s % 2, 0, :], ps[:, s % 2, :], ACT.Relu).then_inc(md, 1)
                            if s > 0:
                                evacuate(k, kind, g, s - 1, q)
                            elif not (isinstance(i, int) and i == 0 and q == 0):
                                evacuate(k, kind, g - 1, SUB - 1, 1 - q)

                turns(act, body)
                evacuate(k, kind, NG - 1, SUB - 1, 1)

            root(("log",), st2[:, :], log=True)
            for c in range(SC):
                act.wait_ge(pair_t, c + 1)
                reach(act, pair_st[c % 4], 0, 16 * (c // 4))
                act.activation(turned_in[:, c % 4, :, :], ps[:, c % 4, 0:3 * P].rearrange("p (k n) -> p k n", k=3),
                               ACT.Copy).then_inc(pair_s, 1)
            for l in range(2):
                turned(l)
                rows(l, "pna")
                for c in range(NB // CB):
                    root(("agg", l, c), agg[:, :, 3 * F:4 * F])
                    for b in range(c * CB, (c + 1) * CB):
                        act.wait_ge(atp, NB * l + b + 1)
                        reach(act, omp, NB * l, b - 1)
                        act.activation(aggt[:, b % 2, 0:2, :], ps[:, b % 2, 0:2 * P].rearrange("p (k n) -> p k n", k=2),
                                       ACT.Copy).then_inc(ats, 1)
                        act.activation(aggt[0:F, b % 2, 2, :], ps[0:F, b % 2, 2 * P:3 * P], ACT.Copy).then_inc(ats, 1)
                root(("bn", l, 0), sd[:, :])
            root(("ln", 0), st2[:, :])
            for j in range(5):
                to = acc if j in (0, 2) else tmp

                def block_rows(b, r):
                    reach(act, lbt, NB * j, b + 1)
                    if j == 0:
                        act.activation(norm[:, bass.ds(b, 1)], ps[:, 2 + r, F:F + 1], ACT.Copy)
                    act.activation(to[:, bass.ds(b, 1), :].rearrange("p a f -> p (a f)"), ps[:, 2 + r, 0:F],
                                   ACT.Copy).then_inc(lnc, 1)

                def block_out(b, c, r):
                    m = F + 1 if j == 0 else F
                    reach(act, lnp, NB * j, b + 1)
                    reach(act, lbt, NB * j, b - 1)
                    act.activation(outt[0:m, r, :], ps[0:m, r, 0:P], ACT.Copy).then_inc(ltc, 1)
                    if not (isinstance(b, int) and b == 0):
                        block_rows(b - 1, 1 - r)

                blocks(act, block_out)
                block_rows(NB - 1, (NB - 1) % 2)
                if j == 2:
                    root(("norm",), st2[:, :])
                    root(("ln", 1), st2[:, :])
            root(("ln", 2), st2[:, :])
            turned(2)
            rows(2, "mlp")
            for j, b, n in chunks(NB, 4):
                act.wait_ge(m_e, j + 1)
                act.activation(mid[:, 0:n * P], ps[:, 0, 0:n * P], ACT.Copy).then_inc(m_et, 1)
                act.wait_ge(m_t, j + 1)
                act.activation(mid[0:F, 512:512 + n * P], ps[0:F, 2, 0:n * P], ACT.Copy).then_inc(m_ts, 1)
                act.wait_ge(m_h, j + 1)
                act.activation(mid[:, 1024:1024 + n * P], ps[:, 3, 0:n * P], ACT.Relu, bias=ub1[:, 0:1]).then_inc(m_hs, 1)
            root(("ln", 3), st2[:, :])

        @block.tensor
        def _(pe):
            mm = pe.matmul
            pe.wait_ge(ld_w, 16 * len(wl))
            pe.wait_ge(made, 11)
            pe.wait_ge(ub_ok, 1)
            mm(ps[:, 3, 0:NB], down, ub[:, :], start=True, stop=False)
            mm(ps[:, 3, 1:NB], corner, ub[:, 0:NB - 1], start=False, stop=True)
            pe.transpose(ps[0:NB, 4, 0:P], ub[:, :], ident[:, :]).then_inc(ubp_ok, 1)
            pe.wait_ge(pair_ok, 1)
            mm(ps[:, 5, 0:SC], down, gs[:, :], start=True, stop=False)
            mm(ps[:, 5, 1:SC], corner, gs[:, 0:SC - 1], start=False, stop=True).then_inc(sh_ok, 1)
            pe.wait_ge(same_in, 1)
            pe.transpose(ps[0:SC, 6, P:2 * P], gs[:, :], ident[:, :])
            pe.transpose(ps[0:SC, 6, 0:P], gsm[:, :], ident[:, :]).then_inc(same_t, 1)
            for l in range(2):
                if l == 1:
                    pe.wait_ge(wcp, 1)
                mm(ps[0:FE16, 0, 0:F], we[l][:, :], pet[l][:, :], start=True, stop=True)
                mm(ps[0:1, 0, F:2 * F], be[l][:, :], pet[l][:, :], start=True, stop=True)
                mm(ps[0:F, 0, 2 * F:3 * F], wo[l][:, 0:F], wlt[l][:, :], start=True, stop=True)
                mm(ps[0:1, 0, 3 * F:4 * F], bo[l][:, :], wlt[l][:, :], start=True, stop=True)
                for r in range(3):
                    for c in range(3):
                        m = P if c < 2 else F
                        k0 = F + 5 * F * r + P * c
                        o = ps[0:m, 1, (3 * c + r) * F:(3 * c + r + 1) * F] if c < 2 else ps[0:m, 2, r * F:(r + 1) * F]
                        last = mm(o, wo[l][:, k0:k0 + m], wlt[l][:, :], start=True, stop=True)
                last.then_inc(wps, 1)
            pe.wait_ge(wcp, 2)
            pe.wait_ge(pkey_ok, 1)
            for c in range(SC):
                reach(pe, pair_s, 0, c - 3)
                for n, v in enumerate((pdst, psrc, pw)):
                    last = pe.transpose(ps[:, c % 4, n * P:(n + 1) * P], v[:, c, :], ident[:, :])
                last.then_inc(pair_t, 1)
            pe.wait_ge(pair_s, SC)

            def project(k):
                for j, b, n in chunks(NB, 4):
                    if j >= 4:
                        pe.wait_ge(xts, XT0[k] + j - 3)
                    for c in range(n):
                        last = pe.transpose(ps[0:F, j % 4, c * P:(c + 1) * P], cur[:, b + c, :], ident[:, :])
                    last.then_inc(xtp, 1)
                w, bias, m, per = (p3, p3b, 2 * HID, 2) if k == 2 else (proj[k], projb[k], 2 * F, 4)
                for j, b, n in chunks(NB, per):
                    pe.wait_ge(xts, XT0[k] + b * P // 512 + 1)
                    if j >= 4:
                        pe.wait_ge(pjs, PJ0[k] + j - 3)
                    for c in range(n):
                        o = ps[:, 4 + j % 4, c * m:(c + 1) * m]
                        mm(o, xt[:, (b + c) * P:(b + c + 1) * P], w[:, :], start=True, stop=False)
                        last = mm(o, ones[0:1, :], bias[:, :], start=False, stop=True)
                    last.then_inc(pjp, 1)

            def turn_back(k, kind, g, s):
                n = SUB * g + s
                reach(pe, scn, SC0[k], SCANS[kind] * (n + 1))
                reach(pe, ev, ONE0[k], n - (1 if kind == "pna" else 3))
                w = W_OF[kind]
                for t in range(ST):
                    c0 = s * SE + t * P
                    if kind == "pna":
                        o = ps[:, 4 + 2 * (s % 2) + t // 2, (t % 2) * 256:(t % 2) * 256 + 256]
                        pe.transpose(o[:, 0:P], scan[:, 0, c0:c0 + P], ident[:, :])
                        last = pe.transpose(o[:, P:2 * P], scan[:, 1, c0:c0 + P], ident[:, :])
                    else:
                        last = pe.transpose(ps[:, 4 + s, t * w:(t + 1) * w], scan[0:w, 0, c0:c0 + P], ident[0:w, 0:w])
                last.then_inc(bt, 1)

            def edges(k, kind):
                def body(i):
                    for q in range(2):
                        g = 2 * i + q
                        pe.wait_ge(gt[k][q], 16 * TG * TABLES[kind] * (i + 1))
                        reach(pe, ld[q], LD0[k], 16 * LOADS[kind] * (i + 1))
                        for s in range(SUB):
                            n = SUB * g + s
                            z = ps[:, s % 2, :]
                            reach(pe, md, MD0[k], MIDS[kind] * (n - 1))
                            if kind == "pna":
                                mm(z, gw[k][:, :], attr[0:FE16, q, s * SE:(s + 1) * SE], start=True, stop=False)
                            if kind == "mlp":
                                mm(z, w1c[:, :], attr[:, q, s * SE:(s + 1) * SE], start=True, stop=False)
                            for t in range(ST):
                                tt = s * ST + t
                                if kind == "pna":
                                    for h in range(2):
                                        last = mm(ps[h * F:(h + 1) * F, s % 2, t * P:(t + 1) * P], gat_l[:, q, tt, :],
                                                  ident[:, :], start=False, stop=(t == ST - 1))
                                else:
                                    mm(z[:, t * P:(t + 1) * P], gat_m[:, q, tt, :], ident[:, :],
                                       start=False, stop=False)
                                    last = mm(z[:, t * P:(t + 1) * P], ugat[:, q, tt, :], ident[:, :],
                                              start=False, stop=(t == ST - 1))
                            last.then_inc(zt, 1)
                            if kind == "pna":
                                reach(pe, hot, 5 * ONE0[k], 5 * (n + 1))
                                reach(pe, acd, PR0[k], 4 * n)
                                for m in range(4):
                                    last = mm(ps[:, 2 + m // 2, (m % 2) * AW:(m % 2 + 1) * AW], hot_l[:, m, :],
                                              hot_r[:, m, :], start=True, stop=True)
                                last.then_inc(bld, 1)
                            if s > 0:
                                turn_back(k, kind, g, s - 1)
                            elif not (isinstance(i, int) and i == 0 and q == 0):
                                turn_back(k, kind, g - 1, SUB - 1)

                turns(pe, body)
                turn_back(k, kind, NG - 1, SUB - 1)

            for l in range(2):
                if l:
                    pe.wait_ge(xr, 1)
                project(l)
                edges(l, "pna")
                for b in range(NB):
                    if b % CB == 0:
                        pe.wait_ge(agr, (NB // CB) * l + b // CB + 1)
                        pe.wait_ge(rs, ORD["agg", l, b // CB])
                    reach(pe, ats, 2 * NB * l, 2 * (b - 1))
                    for c in range(3):
                        m = P if c < 2 else F
                        last = pe.transpose(ps[0:m, b % 2, c * P:(c + 1) * P], agg[:, b % CB, c * P:c * P + m],
                                            ident[:, :])
                    last.then_inc(atp, 1)
                    pe.wait_ge(ats, 2 * NB * l + 2 * (b + 1))
                    reach(pe, oms, NB * l, b - 3)
                    o = ps[:, 4 + b % 4, 0:3 * F]
                    mm(o, xt[:, b * P:(b + 1) * P], wx[l][:, :], start=True, stop=False)
                    mm(o, ones[0:1, :], wxb[l][:, :], start=False, stop=False)
                    for c in range(3):
                        m = P if c < 2 else F
                        last = mm(o, aggt[0:m, b % 2, c, :], wpost[l][0:m, c, :], start=False, stop=(c == 2))
                    last.then_inc(omp, 1)
                for v in range(2):
                    pe.wait_ge(bns, 2 * l + v + 1)
                    src = acc if v == 0 else tmp
                    for j in range(7):
                        last = mm(ps[:, 0, 0:7 * F], ones[:, :],
                                  src[:, 7 * j:7 * j + 7, :].rearrange("p b f -> p (b f)"), start=(j == 0), stop=(j == 6))
                    last.then_inc(bnp, 1)
            loaded = [0, 0]
            for j in range(5):
                rows = [first_rows, acc, tmp, acc, acc][j]
                m = F + 1 if j == 0 else F
                if j in (0, 3, 4):
                    pe.wait_ge(lxr, max(2, j))
                else:
                    pe.wait_ge(lnc, NB * j)

                def turn(b, r):
                    reach(pe, ltc, NB * j, b + 1)
                    reach(pe, lnc, NB * j, b - 1)
                    pe.sem_inc(go_pe, 1)
                    pe.transpose(ps[:, 2 + r, 0:m], outt[0:m, r, :], ident[0:m, 0:m]).then_inc(lbt, 1)

                def product(b, c, r):
                    slot = (r + j) % 2
                    reach(pe, ablk_ld[slot], loaded[slot], 16 * (c + 1))
                    reach(pe, ltc, NB * j, b - 1)
                    for sh in range(NB):
                        last = mm(ps[0:m, r, 0:P], rows[:, sh, :], ablk[:, slot, :, sh, :],
                                  start=(sh == 0), stop=(sh == NB - 1))
                    last.then_inc(lnp, 1)
                    if not (isinstance(b, int) and b == 0):
                        turn(b - 1, 1 - r)

                blocks(pe, product)
                turn(NB - 1, (NB - 1) % 2)
                for r in range(2):
                    loaded[(r + j) % 2] += 16 * (NB // 2 + 1 - r)
            pe.wait_ge(xr, 2)
            project(2)
            edges(2, "mlp")
            pe.wait_ge(agr, 2 * (NB // CB) + 1)
            for j, b, n in chunks(NB, 4):
                reach(pe, m_et, 0, j)
                for c in range(n):
                    last = pe.transpose(ps[:, 0, c * P:(c + 1) * P], ends["mlp"][:, b + c, :], ident[:, :])
                last.then_inc(m_e, 1)
                pe.wait_ge(m_et, j + 1)
                reach(pe, m_as, 0, j)
                for c in range(n):
                    last = mm(ps[:, 1, c * F:(c + 1) * F], mid[:, c * P:(c + 1) * P], w2[:, :], start=True, stop=True)
                last.then_inc(m_a, 1)
                pe.wait_ge(m_as, j + 1)
                for c in range(n):
                    last = pe.transpose(ps[0:F, 2, c * P:(c + 1) * P], acc[:, b + c, :], ident[:, :])
                last.then_inc(m_t, 1)
                pe.wait_ge(m_ts, j + 1)
                mm(ps[:, 3, 0:n * P], u1b[:, :], mid[0:F, 512:512 + n * P], start=True, stop=False)
                mm(ps[:, 3, 0:n * P], u1a[:, :], xt[:, b * P:(b + n) * P], start=False, stop=True).then_inc(m_h, 1)
                pe.wait_ge(m_hs, j + 1)
                reach(pe, m_os, 0, j)
                for c in range(n):
                    last = mm(ps[:, 4, c * F:(c + 1) * F], mid[:, 1024 + c * P:1024 + (c + 1) * P], u2[:, :],
                              start=True, stop=True)
                last.then_inc(m_o, 1)


def kernel(**inputs):
    import numpy as np
    import concourse.bacc as bacc
    from concourse import mybir
    from concourse.bass_utils import run_bass_kernel_spmd as run

    a = {k: np.asarray(v) for k, v in inputs.items()}
    x = np.zeros((NP, F), a["x"].dtype)
    x[:N] = a["x"]

    def padded(v, fill):
        out = np.full((EP,) + v.shape[1:], fill, v.dtype)
        out[:E] = v
        return out

    src, w = padded(a["src"], 0), padded(a["edge_weight"], 0)
    dst, dst0 = padded(a["dst"], NP), padded(a["dst"], 0)
    before_first = np.full((1,), -1, dst.dtype)

    def features_first(v):
        return np.ascontiguousarray(v.reshape(NG, GE, v.shape[1]).transpose(0, 2, 1))

    arrays = {
        "x": x, "src_t": np.ascontiguousarray(src.reshape(NT, P).T), "dst_t": np.ascontiguousarray(dst0.reshape(NT, P).T), 
        "dst_pad": np.concatenate([before_first, dst]), "dst_tiles": dst.reshape(NT, P),
        "src_tiles": src.reshape(NT, P), "w_tiles": w.reshape(NT, P),
        "dst_last": np.ascontiguousarray(dst.reshape(NT, P)[:, P - 1]),
        "a16_g": features_first(padded(a["edge_attr_16"], 0)), "a32_g": features_first(padded(a["edge_attr_32"], 0)),
        "wpT": np.ascontiguousarray(a["L0_gnn_W_pre"].transpose(0, 2, 1)),
        "wlT": np.ascontiguousarray(a["L0_gnn_W_lin"].transpose(0, 2, 1)),
        "we": a["L0_gnn_W_edge"], "be": a["L0_gnn_b_edge"], "bp": a["L0_gnn_b_pre"], "bo": a["L0_gnn_b_post"],
        "bl": a["L0_gnn_b_lin"], "wo": a["L0_gnn_W_post"], "gam": a["L0_gnn_bn_gamma"], "bet": a["L0_gnn_bn_beta"],
        "mw1": a["L3_gnn_mW1"], "mb1": a["L3_gnn_mb1"], "mw2": a["L3_gnn_mW2"], "mb2": a["L3_gnn_mb2"],
        "uw1": a["L3_gnn_uW1"], "ub1": a["L3_gnn_ub1"], "uw2": a["L3_gnn_uW2"], "ub2": a["L3_gnn_ub2"],
    }
    nc = bacc.Bacc("TRN2", target_bir_lowering=False, num_devices=1)
    inp = {n: nc.dram_tensor(f"in_{n}", v.shape, mybir.dt.from_np(v.dtype), kind="ExternalInput").ap()
           for n, v in arrays.items()}
    out = nc.dram_tensor("out_0", (N, F), mybir.dt.float32, kind="ExternalOutput").ap()
    build(nc, inp, out)
    r = run(nc, [{f"in_{n}": np.ascontiguousarray(v) for n, v in arrays.items()}], core_ids=[0])
    return r.results[0]["out_0"]
```

```python
import numpy as np
import concourse.bass as bass
from concourse import mybir
from contextlib import ExitStack

N, E, F, FE16, FE32, HID = 6250, 200000, 64, 16, 32, 128
P = 128
NB = -(-N // P)
NP = NB * P
TG = 16
GE = TG * P
NI = -(-E // (2 * GE))
NG = 2 * NI
EP = NG * GE
NT = EP // P
SUB = 4
SE = GE // SUB
ST = TG // SUB
D4 = 4
NGR = NP // D4
GB = P // D4
AW = NB * D4
STEPS = 2 * NG * TG
SG = TG
SC = -(-STEPS // P)
SPARE = TG
BLK = GB * AW
BIG = 1.7e38
AVG = float(np.log(17.0))
EPS = 1e-5
CB = 7
NC4 = -(-NB // 4)
KINDS = ["pna", "pna", "mlp"]
NPASS = len(KINDS)
W_OF = {"pna": 4 * F, "mlp": HID}
assert NT + NGR <= STEPS + 1


def before(per_pass):
    out = [0]
    for kind in KINDS:
        out.append(out[-1] + per_pass[kind])
    return out


LOADS = {"pna": 5, "mlp": 3}
LD0 = before({k: 16 * NI * v for k, v in LOADS.items()})
SCANS = {"pna": 2, "mlp": 1}
SC0 = before({k: NG * SUB * v for k, v in SCANS.items()})
MIDS = {"pna": 4, "mlp": 1}
MD0 = before({k: NG * SUB * v for k, v in MIDS.items()})
ONE0 = before({k: NG * SUB for k in SCANS})
PR0 = before({"pna": NG * SG, "mlp": 0})
SG0 = before({"pna": NG, "mlp": NG})
ST0 = before({k: 16 * NI for k in SCANS})
ER0 = before({k: 16 * NB for k in SCANS})
GT0 = before({k: 16 * NI * ST for k in SCANS})
TC = -(-NT // P)
UR = 2 * NP + P
XT0 = {0: 0, 1: NC4, 2: 2 * NC4}
PJN = {0: NC4, 1: NC4, 2: -(-NB // 2)}
PJ0 = {0: 0, 1: NC4, 2: 2 * NC4}
SQRTS = [("log",)] + [(n, l, c) for l in (0, 1) for n, m in (("agg", NB // CB), ("bn", 1)) for c in range(m)] \
    + [("ln", 0), ("norm",), ("ln", 1), ("ln", 2), ("ln", 3)]
ORD = {s: n + 1 for n, s in enumerate(SQRTS)}


def build(nc, inp, out):
    f32, bf16, i32 = mybir.dt.float32, mybir.dt.bfloat16, mybir.dt.int32
    ALU, ACT, AX = mybir.AluOpType, mybir.ActivationFunctionType, mybir.AxisListType.X
    ctx = ExitStack()
    with ctx:
        def sb(name, shape, dt=f32):
            return ctx.enter_context(nc.sbuf_tensor(name, shape, dt))

        def sem(name):
            return ctx.enter_context(nc.semaphore(name))

        vtab = nc.dram_tensor("vtab", (NP, HID), f32).ap()
        utab = nc.dram_tensor("utab", (UR, HID), f32).ap()
        rank_d = nc.dram_tensor("rank_d", (NG, GE), bf16).ap()
        base_d = nc.dram_tensor("base_d", (TC * P,), i32).ap()
        keep_d = nc.dram_tensor("keep_d", (NG, GE), bf16).ap()
        ends_d = nc.dram_tensor("ends_d", (NGR,), i32).ap()
        step_d = nc.dram_tensor("step_d", (P, SC * P // SG, 3, SG), f32).ap()
        same_d = nc.dram_tensor("same_d", (SC * P + 1,), f32).ap()
        dest_d = nc.dram_tensor("dest_d", (SC * P,), i32).ap()
        group_d = nc.dram_tensor("group_d", ((NGR + SPARE) * P, AW), f32).ap()
        scan_d = {k: nc.dram_tensor(f"scan_{k}", (EP, w), f32).ap() for k, w in W_OF.items()}
        scan_store = {k: v.rearrange("(g p t) w -> g p (t w)", p=P, t=TG) for k, v in scan_d.items()}

        arena = sb("arena", [P, NB * 4 * F])
        ident = sb("ident", [P, P])
        lim_buf = sb("lim_buf", [P, 2 * SE])
        ones = sb("ones", [P, P])
        down = lim_buf[:, 0:P]
        corner = lim_buf[:, P:2 * P]
        sgn = sb("sgn", [P, 1])
        nid = sb("nid", [P, NB])
        valid = sb("valid", [P, NB])
        cnt = sb("cnt", [P, NB])
        nz = sb("nz", [P, NB])
        rden = sb("rden", [P, NB])
        amp = sb("amp", [P, NB])
        att = sb("att", [P, NB])
        norm = sb("norm", [P, NB])
        eidx = sb("eidx", [P, NB], i32)
        cur = sb("cur", [P, NB, F])
        acc = sb("acc", [P, NB, F])
        tmp = sb("tmp", [P, NB, F])
        adst = sb("adst", [P, NB, F])
        xt = sb("xt", [F, NP])
        st1 = sb("st1", [P, NB])
        st2 = sb("st2", [P, NB])
        idx = sb("idx", [P, 2, TG], i32)
        src_all = sb("src_all", [P, NT], i32)
        keep = sb("keep", [P, 2, GE], bf16)
        step_in = sb("step_in", [P, 2, 3, SG])
        same = sb("same", [P, 2, SG])
        attr = sb("attr", [FE32, 2, GE])
        gat = sb("gat", [P, 2 * GE])
        mid = sb("mid", [P, 4 * SE])
        dest = sb("dest", [1, 2, SG], i32)
        stage = sb("stage", [P, 2, 4, AW])
        iota_c = sb("iota_c", [P, AW])
        b2, ub2 = iota_c[:, 0:F], iota_c[:, F:2 * F]
        mu, sd = mid[:, 0:F], mid[:, F:2 * F]
        ints = lim_buf[:, 2 * P:1024].bitcast(i32)
        inid, isid, icol = ints[:, 0:NB], ints[:, NB:NB + SC], ints[:, 80:80 + AW]
        isp = ints[0:SC, 320:320 + P]
        igrp = ints[0:NB, 288:288 + GB]
        lim = lim_buf[:, :].rearrange("p (r n) -> p r n", r=2)
        qm = mid[:, 0:4 * SE].rearrange("p (r k n) -> p r k n", r=2, k=2)
        proj = [sb(f"proj{l}", [F, 2 * F]) for l in range(2)]
        projb = [sb(f"projb{l}", [1, 2 * F]) for l in range(2)]
        gw = [sb(f"gw{l}", [FE16, 2 * F]) for l in range(2)]
        wpost = [sb(f"wpost{l}", [P, 3, 3 * F]) for l in range(2)]
        wx = [sb(f"wx{l}", [F, 3 * F]) for l in range(2)]
        wxb = [sb(f"wxb{l}", [1, 3 * F]) for l in range(2)]
        gam = [sb(f"gam{l}", [P, F]) for l in range(2)]
        bet = [sb(f"bet{l}", [P, F]) for l in range(2)]
        p3 = sb("p3", [F, 2 * HID])
        p3b = sb("p3b", [1, 2 * HID])
        w1c = sb("w1c", [FE32, HID])
        w2 = sb("w2", [HID, F])
        u1a = sb("u1a", [F, HID])
        u1b = sb("u1b", [F, HID])
        ub1 = sb("ub1", [HID, 1])
        u2 = sb("u2", [HID, F])
        ps = ctx.enter_context(nc.psum_tensor("ps", [P, 8, 512], f32))

        rows_out = {k: arena[:, 0:2 * TG * w].rearrange("p (q n) -> p q n", q=2) for k, w in W_OF.items()}
        scan = arena[:, 8192:12288].rearrange("p (k n) -> p k n", k=2)
        ugat = arena[:, 4096:8192].rearrange("p (q t f) -> p q t f", q=2, f=HID)
        gat_m = gat[:, :].rearrange("p (q t f) -> p q t f", q=2, f=HID)
        hots = cur[:, :, :].rearrange("p b f -> p (b f)")[:, 0:8 * (P + AW)].rearrange("p (r n) -> p r n", r=2)
        hot_l = hots[:, :, 0:4 * P].rearrange("p r (m n) -> p r m n", m=4)
        hot_r = hots[:, :, 4 * P:4 * (P + AW)].rearrange("p r (m n) -> p r m n", m=4)
        tile_keep = keep[:, 0, 0:TC * P].rearrange("p (c n) -> p c n", n=P)
        rank = keep[:, 1, 0:TC * P].rearrange("p (c n) -> p c n", n=P)
        begins = mid[:, 256:256 + TC * P // 2].bitcast(bf16).rearrange("p (c n) -> p c n", n=P)
        inner = mid[:, 1088:1088 + TC * P // 2].bitcast(bf16).rearrange("p (c n) -> p c n", n=P)
        tri = lim_buf[:, 0:P]
        begun, begun_sum, begun_run, places = (lim_buf[:, P + 64 * v:P + 64 * v + TC + NB] for v in range(4))
        placei = lim_buf[:, P + 256:P + 256 + TC + NB].bitcast(i32)
        first = lim_buf[:, P + 320:P + 320 + TC]
        empty = lim_buf[:, P + 384:P + 384 + NB]
        zero = lim_buf[:, 2 * SE - 1:2 * SE]
        rank_in = tmp[:, :, :].rearrange("p b f -> p (b f)")[:, 0:GE].bitcast(bf16).rearrange("p (q n) -> p q n", q=2)
        rank_hot = arena[:, 10240:11264].rearrange("p (r n) -> p r n", r=2)
        outt = mid[0:F + 1, 0:2 * P].rearrange("p (r n) -> p r n", r=2)
        ablk = arena[:, :].rearrange("p (r d s) -> p r d s", r=2, s=NB)
        first_rows = gat[:, 0:NB * (F + 1)].rearrange("p (b f) -> p b f", f=F + 1)
        ends = {k: arena[:, 0:NB * w].rearrange("p (b w) -> p b w", w=w) for k, w in W_OF.items()}
        agg = gat[:, 0:CB * 5 * F].rearrange("p (b c) -> p b c", c=5 * F)
        aggt = gat[:, CB * 5 * F:CB * 5 * F + 6 * P].rearrange("p (r k n) -> p r k n", r=2, k=3)
        vu = arena[:, 0:NB * 2 * HID].rearrange("p (b w) -> p b w", w=2 * HID)
        used = [0]

        def carve(rows, *free):
            n = int(np.prod(free))
            part = mid[0:rows, used[0]:used[0] + n]
            used[0] += n
            return part.rearrange("p (k n) -> p k n", k=free[0]) if len(free) > 1 else part

        dcur = arena[:, 0:NT].bitcast(i32)
        dprev = arena[:, NT:2 * NT].bitcast(i32)
        keep0 = keep[:, 0, 0:NT]
        lasti = arena[:, 2 * NT:3 * NT].bitcast(i32)
        lastf = arena[:, 3 * NT:4 * NT]
        lcmp = arena[:, 4 * NT:5 * NT]
        drow = arena[:, 0:NP].rearrange("p (b n) -> p b n", n=P).bitcast(i32)
        dcmp = arena[:, NP:2 * NP].rearrange("p (b n) -> p b n", n=P)
        tcount = st1
        tidx = carve(P, NB).bitcast(i32)
        pdst = arena[:, 0:SC * P].rearrange("p (c n) -> p c n", n=P)
        psrc = arena[:, SC * P:2 * SC * P].rearrange("p (c n) -> p c n", n=P)
        pw = arena[:, 2 * SC * P:3 * SC * P].rearrange("p (c n) -> p c n", n=P)
        in_group = tmp[:, 0:NB // 2 * 2, :].rearrange("p (b r) f -> p b (r f)", r=2)
        pblk = gat[:, 0:SC * P].rearrange("p (c n) -> p c n", n=P)
        slotf = arena[:, 0:NGR]
        scmp = arena[:, NGR:2 * NGR]
        slots = arena[:, 2 * NGR:3 * NGR].bitcast(i32)
        sid = carve(P, SC)
        gs = carve(P, SC)
        gs4 = carve(P, SC)
        tsf = carve(P, SC)
        ts = carve(P, SC).bitcast(i32)
        gsm = carve(P, SC)
        endt = carve(NB, GB)
        endi = carve(NB, GB).bitcast(i32)
        endg = carve(NB, GB)
        samet = carve(SC, P)
        samen = carve(SC, P)
        destf = carve(SC, P)
        desti = carve(SC, P).bitcast(i32)
        spare = carve(SC, P)
        turned_in = acc[:, 0:24, :].rearrange("p b f -> p (b f)").rearrange(
            "p (r g k n) -> p r g k n", r=4, k=3, n=SG)
        ccount = st2
        ub = carve(P, NB)
        eint = carve(P, NB).bitcast(i32)
        epart = carve(P, 3, NB).bitcast(i32)
        pet = [carve(F, F) for l in range(2)]
        wlt = [carve(F, F) for l in range(2)]
        we = [carve(F, FE16) for l in range(2)]
        be = [carve(F, 1) for l in range(2)]
        bo = [carve(F, 1) for l in range(2)]
        bp = [carve(1, F) for l in range(2)]
        bl = [carve(1, F) for l in range(2)]
        wo = [gat[0:F, 1024 * l:1024 * (l + 1)] for l in range(2)]

        ld_w = sem("weights_loaded")
        ld_d = sem("dst_loaded")
        made = sem("constants_made")
        keep_ok = sem("keep_made")
        keep_st = sem("keep_stored")
        t_ok = sem("tile_index_made")
        drow_ok = sem("dst_rows_gathered")
        ub_ok = sem("upper_bounds_made")
        ubp_ok = sem("bounds_shifted")
        wps = sem("weight_products")
        wcp = sem("weight_products_copied")
        ld = [sem(f"group_loaded{q}") for q in range(2)]
        gt = [[sem(f"gathered{q}_{s}") for s in range(SUB)] for q in range(2)]
        ends_ok = sem("group_ends_made")
        ends_st = sem("group_ends_stored")
        slot_ld = sem("group_ends_loaded")
        pair_ok = sem("pair_tiles_made")
        pair_ld = sem("pair_edges_gathered")
        pkey_ok = sem("pair_keys_made")
        pair_t = sem("pair_keys_turned")
        pair_s = sem("pair_keys_copied")
        pair_st = [sem(f"pair_keys_stored{r}") for r in range(4)]
        sh_ok = sem("pairs_shifted")
        same_in = sem("same_group_flags")
        same_t = sem("same_group_turned")
        same_ok = sem("same_group_made")
        same_st = sem("same_group_stored")
        hot = sem("one_hots_made")
        bld = sem("pair_products")
        acd = sem("pair_rows_added")
        ast = [sem(f"pair_rows_stored{r}") for r in range(2)]
        samen_ld = sem("next_flags_loaded")
        dest_ok = sem("pair_places_made")
        rk_go = sem("tile_keep_cleared")
        rk_ld = sem("tile_keep_loaded")
        rk_in = sem("begun_counted")
        rk_sum = sem("begun_summed")
        rk_ok = sem("ranks_made")
        rk_st = sem("ranks_stored")
        spread = sem("rows_put_by_rank")
        bse = [sem(f"bases_loaded{q}") for q in range(2)]
        win = [[sem(f"window_loaded{q}_{s}") for s in range(SUB)] for q in range(2)]
        rh = sem("rank_hots_made")
        b2_ld = sem("late_biases_loaded")
        dest_st = sem("pair_places_stored")
        ablk_ld = [sem(f"block_loaded{r}") for r in range(2)]
        lnp = sem("block_product")
        ltc = sem("block_product_kept")
        lbt = sem("block_product_turned")
        go_pe = sem("block_turns_begun")
        lnc = sem("block_rows_copied")
        lxr = sem("propagation_input_ready")
        zt = sem("turned")
        md = sem("mid_ready")
        scn = sem("scanned")
        bt = sem("turned_back")
        ev = sem("evacuated")
        st = [sem(f"rows_stored{q}") for q in range(2)]
        er = sem("ends_gathered")
        xr = sem("x_ready")
        staged = sem("indices_staged")
        go = sem("group_gathers_begun")
        go_sp = sem("group_fetches_begun")
        xin = sem("x_loaded_again")
        xtp = sem("x_turned")
        xts = sem("xt_stored")
        pjp = sem("projected")
        pjs = sem("projection_copied")
        tbr = sem("table_rows_ready")
        tab = sem("table_stored")
        agr = sem("agg_ready")
        atp = sem("agg_turned")
        ats = sem("aggt_copied")
        omp = sem("post_product")
        oms = sem("post_used")
        rq = sem("root_asked")
        rs = sem("root_done")
        bns = sem("bn_rows_ready")
        bnp = sem("bn_summed")
        m_e = sem("mlp_sum_turned")
        m_et = sem("mlp_sum_copied")
        m_a = sem("mlp_message")
        m_as = sem("mlp_message_biased")
        m_t = sem("mlp_message_turned")
        m_ts = sem("mlp_message_copied")
        m_h = sem("mlp_hidden")
        m_hs = sem("mlp_hidden_relu")
        m_o = sem("mlp_out")
        m_os = sem("mlp_out_used")
        dch = sem("vector_chain")
        fin = sem("result_ready")
        outs = sem("result_stored")
        block = ctx.enter_context(nc.Block())

        def reach(eng, s, base, rel):
            if isinstance(rel, int):
                rel = max(rel, 0)
                if base + rel == 0:
                    return
            eng.wait_ge(s, rel + base)

        def turns(eng, body):
            body(0)
            with eng.Fori(1, NI) as i:
                body(i)

        def behind(i, q, s, parts, step):
            if s >= parts:
                step(2 * i + q, s - parts, q)
            elif not (isinstance(i, int) and i == 0 and q == 0):
                step(2 * i + q - 1, s - parts + SUB, 1 - q)

        def blocks(eng, body):
            for b in range(3):
                body(b, b // 2, b % 2)
            with eng.Fori(1, (NB - 1) // 2) as i:
                body(2 * i + 1, i, 1)
                body(2 * i + 2, i + 1, 0)

        def bcast(ap, n):
            return ap.unsqueeze(2).broadcast_to([P, ap.shape[1], n])

        def chunks(n, size):
            return [(j, j * size, min(size, n - j * size)) for j in range(-(-n // size))]

        wl = []

        @block.sync
        def _(sp):
            sp.dma_start(dcur, inp["dst_pad"][1:1 + EP].rearrange("(p n) -> p n", p=P)).then_inc(ld_d, 16)
            sp.dma_start(dprev, inp["dst_pad"][0:EP].rearrange("(p n) -> p n", p=P)).then_inc(ld_d, 16)
            sp.dma_start(lasti, inp["dst_last"].partition_broadcast(P)).then_inc(ld_d, 16)

            def w(dst, src):
                wl.append(1)
                sp.dma_start(dst, src).then_inc(ld_w, 16)

            for l in range(2):
                w(proj[l][:, 0:F], inp["wpT"][l, F:2 * F, :])
                w(proj[l][:, F:2 * F], inp["wpT"][l, 0:F, :])
                w(pet[l][:, :], inp["wpT"][l, 2 * F:3 * F, :])
                w(wlt[l][:, :], inp["wlT"][l, :, :])
                w(we[l][:, :], inp["we"][l, :, :])
                w(be[l][:, :], inp["be"][l:l + 1, :].rearrange("a f -> f a"))
                w(bo[l][:, :], inp["bo"][l:l + 1, :].rearrange("a f -> f a"))
                w(bp[l][:, :], inp["bp"][l:l + 1, :])
                w(bl[l][:, :], inp["bl"][l:l + 1, :])
                w(wo[l], inp["wo"][l, :, :])
                w(gam[l][:, :], inp["gam"][l, :].partition_broadcast(P))
                w(bet[l][:, :], inp["bet"][l, :].partition_broadcast(P))
            w(src_all[:, :], inp["src_t"])
            w(cur[:, :, :], inp["x"].rearrange("(b p) f -> p b f", p=P))
            w(p3[:, 0:HID], inp["mw1"][0:F, :])
            w(p3[:, HID:2 * HID], inp["mw1"][F:2 * F, :])
            w(p3b[:, HID:2 * HID], inp["mb1"].rearrange("(a f) -> a f", a=1))
            w(w1c[:, :], inp["mw1"][2 * F:2 * F + FE32, :])
            w(w2[:, :], inp["mw2"])
            w(u1a[:, :], inp["uw1"][0:F, :])
            w(u1b[:, :], inp["uw1"][F:2 * F, :])
            w(ub1[:, :], inp["ub1"].rearrange("(f a) -> f a", a=1))
            w(u2[:, :], inp["uw2"])
            sp.wait_ge(keep_ok, 1)
            sp.dma_start(keep_d.rearrange("g n -> (g n)").rearrange("(p n) -> p n", p=P), keep0).then_inc(keep_st, 16)
            sp.wait_ge(keep_st, 16)
            sp.wait_ge(ends_ok, 1)
            sp.dma_start(ends_d.rearrange("(b g) -> b g", b=NB), endi[:, :]).then_inc(ends_st, 16)
            sp.wait_ge(ends_st, 16)
            sp.dma_start(slots[:, :], ends_d.partition_broadcast(P)).then_inc(slot_ld, 16)
            sp.wait_ge(same_ok, 1)
            sp.dma_start(same_d[0:SC * P].rearrange("(c n) -> c n", c=SC), samet[:, :]).then_inc(same_st, 16)
            sp.dma_start(same_d[SC * P:SC * P + 1].rearrange("(c n) -> c n", c=1), samet[0:1, 0:1]).then_inc(same_st, 16)
            sp.wait_ge(same_st, 32)
            sp.dma_start(samen[:, :], same_d[1:SC * P + 1].rearrange("(c n) -> c n", c=SC)).then_inc(samen_ld, 16)
            sp.wait_ge(dest_ok, 1)
            sp.dma_start(dest_d.rearrange("(c n) -> c n", c=SC), desti[:, :]).then_inc(dest_st, 16)
            for c in range(SC):
                sp.wait_ge(pair_s, c + 1)
                sp.dma_start(step_d[:, c * (P // SG):(c + 1) * (P // SG), :, :], turned_in[:, c % 4, :, :, :]).then_inc(pair_st[c % 4], 16)
            for c in range(4):
                sp.wait_ge(pair_st[c], 16 * len(range(c, SC, 4)))
            sp.wait_ge(dest_st, 16)

            def store_pairs(k, g, s, q):
                n = SUB * g + s
                reach(sp, acd, PR0[k], 4 * (n + 1))
                sp.sem_inc(go_sp, 1)
                for m in range(4):
                    v = sp.value_load(dest[0:1, q, 4 * s + m:4 * s + m + 1], min_val=0, max_val=(NGR + SPARE - 1) * P)
                    sp.dma_start(group_d[bass.ds(v, P), :], stage[:, s % 2, m, :]).then_inc(ast[s % 2], 16)

            for k, kind in enumerate(KINDS):
                if k == 2:
                    sp.wait_ge(er, ER0[2])
                    for q in range(2):
                        sp.wait_ge(ast[q], 256 * NG)
                    sp.wait_ge(rk_go, 1)
                    flat = keep_d.rearrange("g n -> (g n)")
                    full = NT // P
                    sp.dma_start(tile_keep[:, 0:full, :], flat[0:full * P * P].rearrange(
                        "(c p n) -> p c n", p=P, n=P)).then_inc(rk_ld, 16)
                    sp.dma_start(tile_keep[0:NT % P, full, :], flat[full * P * P:EP].rearrange(
                        "(p n) -> p n", n=P)).then_inc(rk_ld, 16)
                    for j in range(5):
                        if j == 2:
                            sp.wait_ge(rk_ok, 1)
                            flat = rank_d.rearrange("g n -> (g n)")
                            sp.dma_start(flat[0:full * P * P].rearrange("(c p n) -> p c n", p=P, n=P),
                                         rank[:, 0:full, :]).then_inc(rk_st, 16)
                            sp.dma_start(flat[full * P * P:EP].rearrange("(p n) -> p n", n=P),
                                         rank[0:NT % P, full, :]).then_inc(rk_st, 16)
                            sp.dma_start(base_d.rearrange("(c p) -> p c", p=P), placei[:, 0:TC],
                                         allow_slow_non_contiguous=True).then_inc(rk_st, 16)
                            sp.dma_start(b2, inp["mb2"].partition_broadcast(P)).then_inc(b2_ld, 16)
                            sp.dma_start(ub2, inp["ub2"].partition_broadcast(P)).then_inc(b2_ld, 16)

                        def load_block(b, c, r):
                            reach(sp, lnp, 0, NB * j + b - 1)
                            sp.dma_start(ablk[:, (r + j) % 2, :, :].rearrange("p (g d) s -> p g (d s)", g=GB),
                                         group_d[0:NGR * P, :].rearrange("(n g p) w -> n p g w", g=GB, p=P)[
                                             b, :, :, :]).then_inc(ablk_ld[(r + j) % 2], 16)

                        blocks(sp, load_block)
                sp.wait_ge(tbr, k + 1)
                if kind == "mlp":
                    sp.dma_start(vtab.rearrange("(b p) f -> p b f", p=P), vu[:, :, 0:HID]).then_inc(tab, 16)
                    sp.dma_start(utab[0:NP, :].rearrange("(b p) f -> p b f", p=P),
                                 vu[:, :, HID:2 * HID]).then_inc(tab, 16)
                    sp.dma_start(utab[NP:NP + P, :], vu[:, 0, HID:2 * HID]).then_inc(tab, 16)
                    sp.wait_ge(rk_st, 48)
                    sp.dma_start(dest[:, 0, :], base_d[0:SG].rearrange("(a n) -> a n", a=1)).then_inc(bse[0], 16)
                    sp.wait_ge(spread, 16 * NB)
                else:
                    for h in range(2):
                        sp.dma_start(vtab[:, h * F:(h + 1) * F].rearrange("(b p) f -> p b f", p=P),
                                     tmp[:, :, :]).then_inc(tab, 16)

                def windows(i, q):
                    g = 2 * i + q
                    at = bass.ds((g + 1) * SG, SG)
                    sp.dma_start(dest[:, 1 - q, :], base_d[at].rearrange("(a n) -> a n", a=1)).then_inc(bse[1 - q], 16)
                    sp.wait_ge(bse[q], 16 * (i + 1))
                    sp.sem_inc(go_sp, 1)
                    for s in range(SUB):
                        if s == SUB - 1:
                            reach(sp, scn, SC0[k], (g - 1) * SUB)
                            sp.sem_inc(go_sp, 1)
                            sp.dma_start(keep[:, q, :], keep_d[g, :].partition_broadcast(P)).then_inc(ld[q], 16)
                            sp.dma_start(rank_in[:, q, :], rank_d[g, :].partition_broadcast(P)).then_inc(ld[q], 16)
                            sp.dma_start(attr[:, q, :], inp["a32_g"][g, :, :]).then_inc(ld[q], 16)
                        reach(sp, zt, ONE0[k], SUB * (g - 2) + s + 1)
                        sp.sem_inc(go_sp, 1)
                        for t in range(s * ST, (s + 1) * ST):
                            v = sp.value_load(dest[0:1, q, t:t + 1], min_val=0, max_val=NP)
                            sp.dma_start(ugat[:, q, t, :], utab[bass.ds(v, P), :]).then_inc(win[q][s], 16)

                def body(i):
                    for q in range(2):
                        if kind == "mlp":
                            windows(i, q)
                            continue
                        reach(sp, scn, SC0[k], (2 * i + q - 1) * SUB * SCANS[kind])
                        g = 2 * i + q
                        sp.dma_start(keep[:, q, :], keep_d[g, :].partition_broadcast(P)).then_inc(ld[q], 16)
                        if kind == "pna":
                            sp.dma_start(attr[0:FE16, q, :], inp["a16_g"][g, :, :]).then_inc(ld[q], 16)
                            at = bass.ds(PR0[k] + g * SG, SG)
                            sp.dma_start(step_in[:, q, :, :], step_d[:, bass.ds(PR0[k] // SG + g, 1), :, :].rearrange(
                                "p a k n -> p (a k) n")).then_inc(ld[q], 16)
                            sp.dma_start(same[:, q, :], same_d[at].partition_broadcast(P)).then_inc(ld[q], 16)
                            sp.dma_start(dest[:, q, :], dest_d[at].rearrange("(a n) -> a n", a=1)).then_inc(ld[q], 16)
                            if not (isinstance(i, int) and i == 0 and q == 0):
                                for s in range(SUB):
                                    store_pairs(k, g - 1, s, 1 - q)

                turns(sp, body)
                if kind == "mlp":
                    sp.wait_ge(bse[0], 16 * (NI + 1))
                if kind == "pna":
                    for s in range(SUB):
                        store_pairs(k, NG - 1, s, 1)
                if k == 1:
                    sp.wait_ge(bns, 3)
                    sp.dma_start(adst[:, :, :], inp["x"].rearrange("(b p) f -> p b f", p=P)).then_inc(xin, 16)
            sp.wait_ge(fin, 1)
            full = N // P
            sp.dma_start(out[0:full * P, :].rearrange("(b p) f -> p b f", p=P), acc[:, 0:full, :]).then_inc(outs, 16)
            sp.dma_start(out[full * P:N, :], acc[0:N - full * P, full, :]).then_inc(outs, 16)
            sp.wait_ge(outs, 32)

        @block.gpsimd
        def _(pool):
            pool.memset(ident[:, :], 0.0).then_inc(made, 1)
            pool.memset(ones[:, :], 1.0).then_inc(made, 1)
            pool.memset(lim_buf[:, 0:2 * P], 0.0).then_inc(made, 1)
            pool.iota(inid, pattern=[[P, NB]], base=0, channel_multiplier=1).then_inc(made, 1)
            pool.iota(isid, pattern=[[P, SC]], base=0, channel_multiplier=1).then_inc(made, 1)
            pool.iota(icol, pattern=[[1, AW]], base=0, channel_multiplier=0).then_inc(made, 1)
            pool.iota(isp, pattern=[[0, P // SPARE], [1, SPARE]], base=NGR, channel_multiplier=0).then_inc(made, 1)
            pool.iota(igrp, pattern=[[1, GB]], base=0, channel_multiplier=GB).then_inc(made, 1)
            pool.wait_ge(made, 8)
            pool.affine_select(out=ident[:, :], in_=ident[:, :], compare_op=ALU.not_equal, fill=1.0,
                               base=0, pattern=[[-1, P]], channel_multiplier=1).then_inc(made, 1)
            pool.affine_select(out=down, in_=down, compare_op=ALU.not_equal, fill=1.0,
                               base=1, pattern=[[-1, P]], channel_multiplier=1).then_inc(made, 1)
            pool.affine_select(out=corner, in_=corner, compare_op=ALU.not_equal, fill=1.0,
                               base=1 - P, pattern=[[P, P]], channel_multiplier=1).then_inc(made, 1)
            pool.wait_ge(t_ok, 1)
            for b in range(NB):
                pool.indirect_dma_start(drow[:, b, :], None, inp["dst_tiles"],
                                        bass.IndirectOffsetOnAxis(ap=tidx[:, b:b + 1], axis=0)).then_inc(drow_ok, 16)
            pool.wait_ge(pair_ok, 1)
            for c in range(SC):
                for dst, src in ((pdst.bitcast(i32), "dst_tiles"), (psrc.bitcast(i32), "src_tiles"), (pw, "w_tiles")):
                    pool.indirect_dma_start(dst[:, c, :], None, inp[src], bass.IndirectOffsetOnAxis(
                        ap=ts[:, c:c + 1], axis=0)).then_inc(pair_ld, 16)
            need = 0
            for k, kind in enumerate(KINDS):
                need += 48 if kind == "mlp" else 32
                pool.wait_ge(tab, need)
                if kind == "mlp":
                    for b in range(NB):
                        pool.indirect_dma_start(utab, bass.IndirectOffsetOnAxis(
                            ap=placei[:, TC + b:TC + b + 1], axis=0), vu[:, b, HID:2 * HID], None).then_inc(spread, 16)

                def body(i):
                    for q in range(2):
                        g = 2 * i + q
                        for s in range(SUB):
                            reach(pool, gt[q][s], GT0[k], 16 * ST * i)
                        pool.sem_inc(go, 1)
                        pool.tensor_copy(idx[:, q, :], src_all[:, bass.ds(g * TG, TG)]).then_inc(staged, 1)
                        reach(pool, staged, SG0[k], g + 1)
                        for s in range(SUB):
                            reach(pool, zt, ONE0[k], SUB * (g - 2) + s + 1)
                            pool.sem_inc(go, 1)
                            for t in range(s * ST, (s + 1) * ST):
                                pool.indirect_dma_start(gat_m[:, q, t, :], None, vtab, bass.IndirectOffsetOnAxis(
                                    ap=idx[:, q, t:t + 1], axis=0)).then_inc(gt[q][s], 16)

                turns(pool, body)
                for q in range(2):
                    pool.wait_ge(st[q], ST0[k + 1])
                for b in range(NB):
                    pool.indirect_dma_start(ends[kind][:, b, :], None, scan_d[kind], bass.IndirectOffsetOnAxis(
                        ap=eidx[:, b:b + 1], axis=0)).then_inc(er, 16)

        @block.vector
        def _(dve):
            chain = [0]

            def link(ins):
                chain[0] += 1
                ins.then_inc(dch, 1)
                dve.wait_ge(dch, chain[0])

            dve.wait_ge(ld_d, 48)
            dve.tensor_tensor(keep0, dcur, dprev, ALU.is_equal).then_inc(keep_ok, 1)
            dve.memset(sgn[0:F, :], 1.0)
            dve.memset(sgn[F:2 * F, :], -1.0)
            for l in range(2):
                dve.memset(wpost[l][:, :, :], 0.0)
                dve.memset(wx[l][:, :], 0.0)
                dve.memset(wxb[l][:, :], 0.0)
                dve.memset(projb[l][:, :], 0.0)
            link(dve.memset(p3b[:, 0:HID], 0.0))
            dve.wait_ge(made, 11)
            link(dve.tensor_copy(nid[:, :], inid))
            dve.tensor_copy(sid[:, :], isid)
            dve.tensor_copy(iota_c[:, :], icol)
            dve.tensor_copy(spare[:, :], isp)
            link(dve.tensor_copy(endg[:, :], igrp))
            link(dve.memset(stage[:, :, :, :], 0.0))
            link(dve.tensor_scalar(valid[:, :], nid[:, :], float(N), None, ALU.is_lt))
            link(dve.tensor_copy(lastf, lasti))
            for b in range(NB):
                link(dve.tensor_scalar(lcmp, lastf, nid[:, b:b + 1], None, ALU.is_le))
                link(dve.reduce_sum(tcount[:, b:b + 1], lcmp, AX))
            link(dve.tensor_copy(tidx[:, :], tcount[:, :]))
            dve.wait_ge(keep_st, 16)
            dve.memset(st2[:, 0:1], 0.0).then_inc(t_ok, 1)
            dve.wait_ge(drow_ok, 16 * NB)
            link(dve.tensor_tensor(dcmp, drow, bcast(nid[:, :], P), ALU.is_le))
            link(dve.reduce_sum(ccount[:, :], dcmp, AX))
            link(dve.scalar_tensor_tensor(out=ub[:, :], in0=tcount[:, :], scalar=float(P), in1=ccount[:, :],
                                          op0=ALU.mult, op1=ALU.add))
            link(dve.tensor_scalar(st1[:, :], ub[:, :], 1.0, -1.0, ALU.max, ALU.add))
            dve.tensor_copy(eint[:, :], st1[:, :]).then_inc(ub_ok, 1)
            dve.wait_ge(ub_ok, 1)
            link(dve.tensor_scalar(epart[:, 0, :], eint[:, :], P - 1, 4, ALU.bitwise_and, ALU.logical_shift_left))
            link(dve.tensor_scalar(epart[:, 1, :], eint[:, :], 7, TG - 1, ALU.logical_shift_right, ALU.bitwise_and))
            link(dve.tensor_scalar(epart[:, 2, :], eint[:, :], 11, 11, ALU.logical_shift_right, ALU.logical_shift_left))
            link(dve.tensor_tensor(epart[:, 0, :], epart[:, 0, :], epart[:, 1, :], ALU.bitwise_or))
            link(dve.tensor_tensor(eidx[:, :], epart[:, 0, :], epart[:, 2, :], ALU.bitwise_or))
            dve.wait_ge(ubp_ok, 1)
            link(dve.tensor_tensor(cnt[:, :], ub[:, :], ps[:, 3, 0:NB], ALU.subtract))
            link(dve.tensor_scalar(nz[:, :], cnt[:, :], 1.0, None, ALU.min))
            link(dve.tensor_scalar(st1[:, :], cnt[:, :], 1.0, None, ALU.max))
            link(dve.reciprocal(rden[:, :], st1[:, :]))
            dve.tensor_scalar(st2[:, :], st1[:, :], 1.0, None, ALU.add).then_inc(rq, 1)
            dve.wait_ge(rs, ORD["log",])
            link(dve.reciprocal(st1[:, :], st2[:, :]))
            link(dve.tensor_scalar(amp[:, :], st2[:, :], 1.0 / AVG, None, ALU.mult))
            link(dve.tensor_scalar(att[:, :], st1[:, :], AVG, None, ALU.mult))
            link(dve.tensor_copy(endi[:, :], ps[0:NB, 4, D4 - 1:P:D4]))
            link(dve.tensor_scalar(endi[:, :], endi[:, :], 7, 0, ALU.logical_shift_right, ALU.logical_shift_left))
            link(dve.tensor_copy(endt[:, :], endi[:, :]))
            link(dve.tensor_tensor(endt[:, :], endt[:, :], endg[:, :], ALU.add))
            dve.tensor_copy(endi[:, :], endt[:, :]).then_inc(ends_ok, 1)
            dve.wait_ge(slot_ld, 16)
            link(dve.tensor_copy(slotf, slots[:, :]))
            for c in range(SC):
                link(dve.tensor_scalar(scmp, slotf, sid[:, c:c + 1], None, ALU.is_lt))
                link(dve.reduce_sum(gs[:, c:c + 1], scmp, AX))
            link(dve.tensor_tensor(tsf[:, :], sid[:, :], gs[:, :], ALU.subtract))
            link(dve.tensor_scalar(tsf[:, :], tsf[:, :], float(NT - 1), None, ALU.min))
            link(dve.tensor_scalar(gs4[:, :], gs[:, :], float(D4), None, ALU.mult))
            dve.tensor_copy(ts[:, :], tsf[:, :]).then_inc(pair_ok, 1)
            dve.wait_ge(sh_ok, 1)
            dve.tensor_tensor(gsm[:, :], gs[:, :], ps[:, 5, 0:SC], ALU.is_equal).then_inc(same_in, 1)
            dve.wait_ge(same_t, 1)
            dve.tensor_copy(samet[:, :], ps[0:SC, 6, 0:P]).then_inc(same_ok, 1)
            link(dve.tensor_copy(destf[:, :], ps[0:SC, 6, P:2 * P]))
            link(dve.tensor_tensor(spare[:, :], spare[:, :], destf[:, :], ALU.subtract))
            dve.wait_ge(samen_ld, 16)
            link(dve.tensor_tensor(spare[:, :], spare[:, :], samen[:, :], ALU.mult))
            link(dve.tensor_tensor(destf[:, :], destf[:, :], spare[:, :], ALU.add))
            dve.tensor_scalar(desti[:, :], destf[:, :], float(P), None, ALU.mult).then_inc(dest_ok, 1)
            for l in range(2):
                dve.wait_ge(wps, l + 1)
                dve.tensor_copy(gw[l][:, 0:F], ps[0:FE16, 0, 0:F])
                dve.tensor_copy(gw[l][:, F:2 * F], ps[0:FE16, 0, 0:F])
                dve.tensor_tensor(projb[l][:, F:2 * F], ps[0:1, 0, F:2 * F], bp[l][:, :], ALU.add)
                dve.tensor_copy(wx[l][:, 0:F], ps[0:F, 0, 2 * F:3 * F])
                dve.tensor_tensor(wxb[l][:, 0:F], ps[0:1, 0, 3 * F:4 * F], bl[l][:, :], ALU.add)
                dve.tensor_copy(wpost[l][:, 0:2, :], ps[:, 1, 0:6 * F].rearrange("p (k n) -> p k n", k=2))
                dve.tensor_copy(wpost[l][0:F, 2, :], ps[0:F, 2, 0:3 * F]).then_inc(wcp, 1)
            dve.wait_ge(pair_ld, 16 * 3 * SC)
            link(dve.tensor_copy(pdst, pdst.bitcast(i32)))
            link(dve.tensor_tensor(pdst, pdst, bcast(gs4[:, :], P), ALU.subtract))
            link(dve.tensor_scalar(pblk.bitcast(i32), psrc.bitcast(i32), 7, 0, ALU.logical_shift_right,
                                   ALU.logical_shift_left))
            link(dve.tensor_copy(pblk, pblk.bitcast(i32)))
            link(dve.scalar_tensor_tensor(out=pblk, in0=pdst, scalar=float(NB), in1=pblk, op0=ALU.mult, op1=ALU.add))
            for c in range(0, SC, NB * F // P):
                cs = slice(c, min(SC, c + NB * F // P))
                inside = in_group[:, 0:cs.stop - cs.start, :]
                link(dve.tensor_scalar(inside, pdst[:, cs, :], 0.0, None, ALU.is_ge))
                link(dve.tensor_scalar(pdst[:, cs, :], pdst[:, cs, :], float(D4 - 1), None, ALU.is_le))
                link(dve.tensor_tensor(pdst[:, cs, :], pdst[:, cs, :], inside, ALU.mult))
            link(dve.tensor_scalar(pblk, pblk, 1.0, None, ALU.add))
            link(dve.tensor_tensor(pdst, pdst, pblk, ALU.mult))
            link(dve.tensor_scalar(pdst, pdst, -1.0, None, ALU.add))
            link(dve.tensor_scalar(psrc.bitcast(i32), psrc.bitcast(i32), P - 1, 0, ALU.bitwise_and, ALU.bitwise_or))
            dve.tensor_copy(psrc, psrc.bitcast(i32)).then_inc(pkey_ok, 1)

            def layer_norm(n, src, res):
                link(dve.reduce_sum(st1[:, :], src[:, :, :], AX))
                link(dve.tensor_scalar(st1[:, :], st1[:, :], 1.0 / F, None, ALU.mult))
                link(dve.tensor_tensor(src[:, :, :], src[:, :, :], bcast(st1[:, :], F), ALU.subtract))
                link(dve.tensor_tensor(tmp[:, :, :], src[:, :, :], src[:, :, :], ALU.mult))
                link(dve.reduce_sum(st2[:, :], tmp[:, :, :], AX))
                dve.tensor_scalar(st2[:, :], st2[:, :], 1.0 / F, EPS, ALU.mult, ALU.add).then_inc(rq, 1)
                dve.wait_ge(rs, ORD["ln", n])
                link(dve.reciprocal(st2[:, :], st2[:, :]))
                link(dve.tensor_tensor(res[:, :, :], src[:, :, :], bcast(st2[:, :], F), ALU.mult))

            def projection(k):
                for j in range(PJN[k]):
                    dve.wait_ge(pjp, PJ0[k] + j + 1)
                    if k == 2:
                        n = min(2, NB - 2 * j)
                        dve.tensor_copy(vu[:, 2 * j:2 * j + n, :], ps[:, 4 + j % 4, 0:n * 2 * HID].rearrange(
                            "p (b w) -> p b w", b=n)).then_inc(pjs, 1)
                    else:
                        n = min(4, NB - 4 * j)
                        v = ps[:, 4 + j % 4, 0:n * 2 * F].rearrange("p (b w) -> p b w", b=n)
                        dve.tensor_copy(tmp[:, 4 * j:4 * j + n, :], v[:, :, 0:F])
                        dve.tensor_copy(adst[:, 4 * j:4 * j + n, :], v[:, :, F:2 * F]).then_inc(pjs, 1)
                dve.wait_ge(pjs, PJ0[k] + PJN[k])
                dve.memset(st2[:, 0:1], 0.0).then_inc(tbr, 1)

            def one_hots(q, s):
                cols = step_in[:, q, :, 4 * s:4 * s + 4]
                dve.tensor_tensor(hot_l[:, s % 2, :, :], iota_c[:, 0:P].unsqueeze(1).broadcast_to([P, 4, P]),
                                  bcast(cols[:, 1, :], P), ALU.is_equal).then_inc(hot, 1)
                for m in range(4):
                    dve.tensor_scalar(hot_r[:, s % 2, m, :], iota_c[:, :], cols[:, 0, m:m + 1],
                                      cols[:, 2, m:m + 1], ALU.is_equal, ALU.mult).then_inc(hot, 1)

            def make_ranks():
                dve.wait_ge(rk_ld, 32)
                link(dve.tensor_scalar(begins, tile_keep, -1.0, 1.0, ALU.mult, ALU.add))
                link(dve.tensor_copy(first, begins[:, :, 0]))
                link(dve.reduce_sum(begun[:, 0:TC], begins, AX))
                link(dve.tensor_copy(begun[:, TC:TC + NB], nz[:, :]))
                dve.tensor_scalar(tri, iota_c[:, 0:P], nid[:, 0:1], None, ALU.is_gt).then_inc(rk_in, 1)
                link(dve.memset(begins[:, :, 0], 0.0))
                link(dve.memset(inner, 1.0))
                link(dve.memset(inner[:, :, 0], 0.0))
                link(dve.memset(zero, 0.0))
                link(dve.tensor_tensor_scan(rank.rearrange("p c n -> p (c n)"), inner.rearrange("p c n -> p (c n)"),
                                            begins.rearrange("p c n -> p (c n)"), zero, ALU.mult, ALU.add))
                dve.wait_ge(rk_sum, 1)
                link(dve.tensor_copy(begun_sum, ps[:, 7, 64:64 + TC + NB]))
                for part in (slice(0, TC), slice(TC, TC + NB)):
                    link(dve.tensor_tensor_scan(begun_run[:, part], ones[:, part], begun_sum[:, part], zero,
                                                ALU.mult, ALU.add))
                link(dve.tensor_tensor(places, begun_run, begun_sum, ALU.subtract))
                link(dve.tensor_tensor(places, places, ps[:, 7, 0:TC + NB], ALU.add))
                link(dve.tensor_tensor(places[:, 0:TC], places[:, 0:TC], first, ALU.add))
                link(dve.tensor_scalar(places[:, 0:TC], places[:, 0:TC], -1.0, None, ALU.add))
                link(dve.tensor_scalar(empty, nid[:, :], float(NP + P), None, ALU.add))
                link(dve.tensor_tensor(places[:, TC:], places[:, TC:], empty, ALU.subtract))
                link(dve.tensor_tensor(places[:, TC:], places[:, TC:], nz[:, :], ALU.mult))
                link(dve.tensor_tensor(places[:, TC:], places[:, TC:], empty, ALU.add))
                dve.tensor_copy(placei, places).then_inc(rk_ok, 1)

            def rank_hots(q, s, n):
                reach(dve, zt, ONE0[2], n - 1)
                dve.tensor_scalar(rank_hot[:, s % 2, :], rank_in[:, q, s * SE:(s + 1) * SE], nid[:, 0:1], None,
                                  ALU.is_equal).then_inc(rh, 1)

            def segment_scans(k, kind):
                def body(i):
                    for q in range(2):
                        g = 2 * i + q
                        reach(dve, ld[q], LD0[k], 16 * LOADS[kind] * (i + 1))
                        for s in range(SUB):
                            n = SUB * g + s
                            for ahead in range(0 if s == 0 else s + 1, min(s + 2, SUB)):
                                if kind == "pna":
                                    one_hots(q, ahead)
                                else:
                                    rank_hots(q, ahead, SUB * g + ahead)
                            reach(dve, md, MD0[k], MIDS[kind] * (n + 1))
                            data = qm[:, s % 2, 0, :]
                            reach(dve, bt, ONE0[k], n - SUB + 1)
                            reach(dve, scn, SC0[k], SCANS[kind] * n)
                            here = slice(s * SE, (s + 1) * SE)
                            last = (s * SE - 1) % GE
                            dve.tensor_tensor_scan(scan[:, 0, here], keep[:, q, here], data,
                                                   scan[:, 0, last:last + 1], ALU.mult, ALU.add).then_inc(scn, 1)
                            if kind == "pna":
                                dve.tensor_tensor_scan(scan[:, 1, here], lim[:, s % 2, :], qm[:, s % 2, 1, :],
                                                       scan[:, 1, last:last + 1], ALU.min, ALU.max).then_inc(scn, 1)
                                reach(dve, bld, ONE0[k], n + 1)
                                reach(dve, ast[s % 2], 128 * NG * k, 64 * (2 * g + s // 2))
                                for m in range(4):
                                    reach(dve, acd, PR0[k], 4 * n + m)
                                    last_row = stage[:, s % 2, m - 1, :] if m else stage[:, 1 - s % 2, 3, :]
                                    dve.scalar_tensor_tensor(
                                        out=stage[:, s % 2, m, :], in0=last_row,
                                        scalar=same[:, q, 4 * s + m:4 * s + m + 1],
                                        in1=ps[:, 2 + m // 2, (m % 2) * AW:(m % 2 + 1) * AW],
                                        op0=ALU.mult, op1=ALU.add).then_inc(acd, 1)

                turns(dve, body)
                dve.wait_ge(er, ER0[k + 1])

            def pna_nodes(l):
                e = ends["pna"]
                for c in range(NB // CB):
                    bs = slice(c * CB, (c + 1) * CB)
                    reach(dve, atp, NB * l, c * CB)
                    mean, mn, mx, std, ssum = (agg[:, :, f * F:(f + 1) * F] for f in range(5))
                    rd, z = bcast(rden[:, bs], F), bcast(nz[:, bs], F)
                    a = adst[:, bs, :]
                    link(dve.tensor_tensor(mean, e[:, bs, 0:F], rd, ALU.mult))
                    link(dve.tensor_tensor(std, e[:, bs, F:2 * F], rd, ALU.mult))
                    link(dve.tensor_tensor(ssum, mean, mean, ALU.mult))
                    link(dve.tensor_tensor(std, std, ssum, ALU.subtract))
                    link(dve.tensor_tensor(std, std, z, ALU.mult))
                    dve.tensor_scalar(std, std, 0.0, EPS, ALU.max, ALU.add).then_inc(rq, 1)
                    link(dve.tensor_tensor(mean, mean, a, ALU.add))
                    link(dve.tensor_tensor(mean, mean, z, ALU.mult))
                    link(dve.tensor_tensor(mn, a, e[:, bs, 3 * F:4 * F], ALU.subtract))
                    link(dve.tensor_tensor(mn, mn, z, ALU.mult))
                    link(dve.tensor_tensor(mx, a, e[:, bs, 2 * F:3 * F], ALU.add))
                    link(dve.tensor_tensor(mx, mx, z, ALU.mult))
                    dve.tensor_tensor(ssum, mean, bcast(cnt[:, bs], F), ALU.mult).then_inc(agr, 1)
                    for b in range(c * CB, (c + 1) * CB):
                        dve.wait_ge(omp, NB * l + b + 1)
                        o = ps[:, 4 + b % 4, :]
                        link(dve.tensor_copy(acc[:, b, :], o[:, 0:F]))
                        link(dve.scalar_tensor_tensor(out=acc[:, b, :], in0=o[:, F:2 * F], scalar=amp[:, b:b + 1],
                                                      in1=acc[:, b, :], op0=ALU.mult, op1=ALU.add))
                        dve.scalar_tensor_tensor(out=acc[:, b, :], in0=o[:, 2 * F:3 * F], scalar=att[:, b:b + 1],
                                                 in1=acc[:, b, :], op0=ALU.mult, op1=ALU.add).then_inc(oms, 1)
                dve.wait_ge(oms, NB * (l + 1))
                v = valid[:, NB - 1:NB]
                dve.tensor_scalar(acc[:, NB - 1, :], acc[:, NB - 1, :], v, None, ALU.mult).then_inc(bns, 1)
                dve.wait_ge(bnp, 2 * l + 1)
                fold = ps[:, 0, 0:7 * F].rearrange("p (b f) -> p f b", f=F)
                link(dve.reduce_sum(mu[:, :], fold, AX))
                link(dve.tensor_scalar(mu[:, :], mu[:, :], 1.0 / N, None, ALU.mult))
                mub = mu[:, :].unsqueeze(1).broadcast_to([P, NB, F])
                link(dve.tensor_tensor(acc[:, :, :], acc[:, :, :], mub, ALU.subtract))
                link(dve.tensor_scalar(acc[:, NB - 1, :], acc[:, NB - 1, :], v, None, ALU.mult))
                dve.tensor_tensor(tmp[:, :, :], acc[:, :, :], acc[:, :, :], ALU.mult).then_inc(bns, 1)
                dve.wait_ge(bnp, 2 * l + 2)
                link(dve.reduce_sum(sd[:, :], fold, AX))
                dve.tensor_scalar(sd[:, :], sd[:, :], 1.0 / N, EPS, ALU.mult, ALU.add).then_inc(rq, 1)
                dve.wait_ge(rs, ORD["bn", l, 0])
                link(dve.reciprocal(sd[:, :], sd[:, :]))
                link(dve.tensor_tensor(sd[:, :], sd[:, :], gam[l][:, :], ALU.mult))
                sdb = sd[:, :].unsqueeze(1).broadcast_to([P, NB, F])
                bb = bet[l][:, :].unsqueeze(1).broadcast_to([P, NB, F])
                link(dve.tensor_tensor(acc[:, :, :], acc[:, :, :], sdb, ALU.mult))
                link(dve.tensor_tensor(acc[:, :, :], acc[:, :, :], bb, ALU.add))
                if l == 0:
                    dve.tensor_scalar(cur[:, :, :], acc[:, :, :], 0.0, None, ALU.max).then_inc(xr, 1)
                else:
                    link(dve.tensor_scalar(acc[:, :, :], acc[:, :, :], 0.0, None, ALU.max))
                    dve.wait_ge(xin, 16)
                    link(dve.tensor_tensor(acc[:, :, :], acc[:, :, :], adst[:, :, :], ALU.add))
                    layer_norm(0, acc, cur)
                    dve.memset(first_rows[:, :, F], 1.0).then_inc(lxr, 1)
                    dve.tensor_copy(first_rows[:, :, 0:F], cur[:, :, :]).then_inc(lxr, 1)

            dve.wait_ge(ld_w, 16 * len(wl))
            link(dve.memset(scan[:, :, GE - 1:GE], 0.0))
            for l in range(2):
                projection(l)
                segment_scans(l, "pna")
                if l == 1:
                    dve.memset(keep[:, 0, :], 1.0).then_inc(rk_go, 1)
                pna_nodes(l)
            make_ranks()
            dve.wait_ge(lnc, 3 * NB)
            dve.tensor_scalar(st2[:, :], norm[:, :], 1.0, None, ALU.max).then_inc(rq, 1)
            dve.wait_ge(rs, ORD["norm",])
            link(dve.reciprocal(norm[:, :], st2[:, :]))
            link(dve.tensor_tensor(acc[:, :, :], acc[:, :, :], cur[:, :, :], ALU.add))
            layer_norm(1, acc, cur)
            nb = bcast(norm[:, :], F)
            link(dve.tensor_copy(adst[:, :, :], cur[:, :, :]))
            dve.tensor_tensor(acc[:, :, :], cur[:, :, :], nb, ALU.mult).then_inc(lxr, 1)
            for j in (3, 4):
                dve.wait_ge(lnc, (j + 1) * NB)
                link(dve.tensor_tensor(tmp[:, :, :], tmp[:, :, :], nb, ALU.mult))
                link(dve.tensor_tensor(adst[:, :, :], adst[:, :, :], tmp[:, :, :], ALU.add))
                if j == 3:
                    dve.tensor_tensor(acc[:, :, :], tmp[:, :, :], nb, ALU.mult).then_inc(lxr, 1)
            link(dve.tensor_scalar(adst[:, :, :], adst[:, :, :], 1.0 / 3.0, None, ALU.mult))
            link(dve.tensor_tensor(adst[:, :, :], adst[:, :, :], cur[:, :, :], ALU.add))
            layer_norm(2, adst, cur)
            link(dve.memset(scan[:, :, GE - 1:GE], 0.0))
            dve.memset(st1[:, 0:1], 0.0).then_inc(xr, 1)
            projection(2)
            dve.wait_ge(spread, 16 * NB)
            segment_scans(2, "mlp")
            dve.wait_ge(b2_ld, 32)
            em = ends["mlp"]
            link(dve.tensor_tensor(em, em, bcast(nz[:, :], HID), ALU.mult))
            dve.memset(st1[:, 0:1], 0.0).then_inc(agr, 1)
            for j, b, n in chunks(NB, 4):
                dve.wait_ge(m_a, j + 1)
                b2b = b2[:, :].unsqueeze(1).broadcast_to([P, n, F])
                link(dve.tensor_tensor(acc[:, b:b + n, :], b2b, bcast(cnt[:, b:b + n], F), ALU.mult))
                dve.tensor_tensor(acc[:, b:b + n, :], acc[:, b:b + n, :],
                                  ps[:, 1, 0:n * F].rearrange("p (b f) -> p b f", b=n), ALU.add).then_inc(m_as, 1)
                dve.wait_ge(m_o, j + 1)
                u2b = ub2[:, :].unsqueeze(1).broadcast_to([P, n, F])
                link(dve.tensor_tensor(acc[:, b:b + n, :], ps[:, 4, 0:n * F].rearrange("p (b f) -> p b f", b=n), u2b,
                                       ALU.add))
                dve.tensor_tensor(acc[:, b:b + n, :], acc[:, b:b + n, :], cur[:, b:b + n, :], ALU.add).then_inc(m_os, 1)
            dve.wait_ge(m_os, NC4)
            layer_norm(3, acc, acc)
            dve.memset(st1[:, 0:1], 0.0).then_inc(fin, 1)

        @block.scalar
        def _(act):
            def root(name, ap, log=False):
                act.wait_ge(rq, ORD[name])
                act.activation(ap, ap, ACT.Ln if log else ACT.Sqrt).then_inc(rs, 1)

            def turned(k):
                for j, b, n in chunks(NB, 4):
                    act.wait_ge(xtp, XT0[k] + j + 1)
                    act.activation(xt[:, b * P:(b + n) * P], ps[0:F, j % 4, 0:n * P], ACT.Copy).then_inc(xts, 1)

            def evacuate(k, kind, g, s, q):
                w = W_OF[kind]
                n = SUB * g + s
                reach(act, bt, ONE0[k], n + 1)
                if s == 0:
                    reach(act, st[q], ST0[k], 8 * g - 8 * q)
                o = rows_out[kind][:, q, s * ST * w:(s + 1) * ST * w]
                if kind == "pna":
                    src = ps[:, 4 + 2 * (s % 2):6 + 2 * (s % 2), :].rearrange("p a n -> p (a n)")
                else:
                    src = ps[:, 4 + s, :]
                act.activation(o, src, ACT.Copy).then_inc(ev, 1)
                if s == SUB - 1:
                    reach(act, ev, ONE0[k], n + 1)
                    act.dma_start(scan_store[kind][g, :, :], rows_out[kind][:, q, 0:TG * w]).then_inc(st[q], 16)

            def rows(k, kind):
                def body(i):
                    for q in range(2):
                        g = 2 * i + q
                        for s in range(SUB):
                            n = SUB * g + s
                            if s == 0:
                                reach(act, ld[q], LD0[k], 16 * LOADS[kind] * (i + 1))
                            reach(act, zt, ONE0[k], n + 1)
                            reach(act, scn, SC0[k], SCANS[kind] * (n - 1))
                            if kind == "pna":
                                r = s % 2
                                act.activation(qm[0:F, r, 0, :], ps[0:F, r, :], ACT.Copy).then_inc(md, 1)
                                act.activation(qm[F:2 * F, r, 0, :], ps[F:2 * F, r, :], ACT.Square).then_inc(md, 1)
                                act.activation(qm[:, r, 1, :], ps[:, r, :], ACT.Copy, scale=sgn[:, 0:1]).then_inc(md, 1)
                                act.activation(lim[:, r, :], keep[:, q, s * SE:(s + 1) * SE], ACT.Copy,
                                               bias=-BIG, scale=2 * BIG).then_inc(md, 1)
                            if kind == "mlp":
                                act.activation(qm[:, s % 2, 0, :], ps[:, s % 2, :], ACT.Relu).then_inc(md, 1)
                            behind(i, q, s, 2, lambda *at: evacuate(k, kind, *at))

                turns(act, body)
                for s in (SUB - 2, SUB - 1):
                    evacuate(k, kind, NG - 1, s, 1)

            root(("log",), st2[:, :], log=True)
            for c in range(SC):
                act.wait_ge(pair_t, c + 1)
                reach(act, pair_st[c % 4], 0, 16 * (c // 4))
                act.activation(turned_in[:, c % 4, :, :, :].rearrange("p g k n -> p k g n"), ps[:, c % 4, 0:3 * P].rearrange(
                    "p (k g n) -> p k g n", k=3, n=SG), ACT.Copy).then_inc(pair_s, 1)
            for l in range(2):
                turned(l)
                rows(l, "pna")
                for c in range(NB // CB):
                    root(("agg", l, c), agg[:, :, 3 * F:4 * F])
                    for b in range(c * CB, (c + 1) * CB):
                        act.wait_ge(atp, NB * l + b + 1)
                        reach(act, omp, NB * l, b - 1)
                        act.activation(aggt[:, b % 2, 0:2, :], ps[:, b % 2, 0:2 * P].rearrange("p (k n) -> p k n", k=2),
                                       ACT.Copy).then_inc(ats, 1)
                        act.activation(aggt[0:F, b % 2, 2, :], ps[0:F, b % 2, 2 * P:3 * P], ACT.Copy).then_inc(ats, 1)
                root(("bn", l, 0), sd[:, :])
            root(("ln", 0), st2[:, :])
            for j in range(5):
                to = acc if j in (0, 2) else tmp

                def block_rows(b, r):
                    reach(act, lbt, NB * j, b + 1)
                    if j == 0:
                        act.activation(norm[:, bass.ds(b, 1)], ps[:, 2 + r, F:F + 1], ACT.Copy)
                    act.activation(to[:, bass.ds(b, 1), :].rearrange("p a f -> p (a f)"), ps[:, 2 + r, 0:F],
                                   ACT.Copy).then_inc(lnc, 1)

                def block_out(b, c, r):
                    m = F + 1 if j == 0 else F
                    reach(act, lnp, NB * j, b + 1)
                    reach(act, lbt, NB * j, b - 1)
                    act.activation(outt[0:m, r, :], ps[0:m, r, 0:P], ACT.Copy).then_inc(ltc, 1)
                    if not (isinstance(b, int) and b == 0):
                        block_rows(b - 1, 1 - r)

                blocks(act, block_out)
                block_rows(NB - 1, (NB - 1) % 2)
                if j == 2:
                    root(("norm",), st2[:, :])
                    root(("ln", 1), st2[:, :])
            root(("ln", 2), st2[:, :])
            turned(2)
            rows(2, "mlp")
            for j, b, n in chunks(NB, 4):
                act.wait_ge(m_e, j + 1)
                act.activation(mid[:, 0:n * P], ps[:, 0, 0:n * P], ACT.Copy).then_inc(m_et, 1)
                act.wait_ge(m_t, j + 1)
                act.activation(mid[0:F, 512:512 + n * P], ps[0:F, 2, 0:n * P], ACT.Copy).then_inc(m_ts, 1)
                act.wait_ge(m_h, j + 1)
                act.activation(mid[:, 1024:1024 + n * P], ps[:, 3, 0:n * P], ACT.Relu, bias=ub1[:, 0:1]).then_inc(m_hs, 1)
            root(("ln", 3), st2[:, :])

        @block.tensor
        def _(pe):
            mm = pe.matmul
            pe.wait_ge(ld_w, 16 * len(wl))
            pe.wait_ge(made, 11)
            pe.wait_ge(ub_ok, 1)
            mm(ps[:, 3, 0:NB], down, ub[:, :], start=True, stop=False)
            mm(ps[:, 3, 1:NB], corner, ub[:, 0:NB - 1], start=False, stop=True)
            pe.transpose(ps[0:NB, 4, 0:P], ub[:, :], ident[:, :]).then_inc(ubp_ok, 1)
            pe.wait_ge(pair_ok, 1)
            mm(ps[:, 5, 0:SC], down, gs[:, :], start=True, stop=False)
            mm(ps[:, 5, 1:SC], corner, gs[:, 0:SC - 1], start=False, stop=True).then_inc(sh_ok, 1)
            pe.wait_ge(same_in, 1)
            pe.transpose(ps[0:SC, 6, P:2 * P], gs[:, :], ident[:, :])
            pe.transpose(ps[0:SC, 6, 0:P], gsm[:, :], ident[:, :]).then_inc(same_t, 1)
            for l in range(2):
                if l == 1:
                    pe.wait_ge(wcp, 1)
                mm(ps[0:FE16, 0, 0:F], we[l][:, :], pet[l][:, :], start=True, stop=True)
                mm(ps[0:1, 0, F:2 * F], be[l][:, :], pet[l][:, :], start=True, stop=True)
                mm(ps[0:F, 0, 2 * F:3 * F], wo[l][:, 0:F], wlt[l][:, :], start=True, stop=True)
                mm(ps[0:1, 0, 3 * F:4 * F], bo[l][:, :], wlt[l][:, :], start=True, stop=True)
                for r in range(3):
                    for c in range(3):
                        m = P if c < 2 else F
                        k0 = F + 5 * F * r + P * c
                        o = ps[0:m, 1, (3 * c + r) * F:(3 * c + r + 1) * F] if c < 2 else ps[0:m, 2, r * F:(r + 1) * F]
                        last = mm(o, wo[l][:, k0:k0 + m], wlt[l][:, :], start=True, stop=True)
                last.then_inc(wps, 1)
            pe.wait_ge(wcp, 2)
            pe.wait_ge(pkey_ok, 1)
            for c in range(SC):
                reach(pe, pair_s, 0, c - 3)
                for n, v in enumerate((pdst, psrc, pw)):
                    last = pe.transpose(ps[:, c % 4, n * P:(n + 1) * P], v[:, c, :], ident[:, :])
                last.then_inc(pair_t, 1)
            pe.wait_ge(pair_s, SC)

            def project(k):
                for j, b, n in chunks(NB, 4):
                    if j >= 4:
                        pe.wait_ge(xts, XT0[k] + j - 3)
                    for c in range(n):
                        last = pe.transpose(ps[0:F, j % 4, c * P:(c + 1) * P], cur[:, b + c, :], ident[:, :])
                    last.then_inc(xtp, 1)
                w, bias, m, per = (p3, p3b, 2 * HID, 2) if k == 2 else (proj[k], projb[k], 2 * F, 4)
                for j, b, n in chunks(NB, per):
                    pe.wait_ge(xts, XT0[k] + b * P // 512 + 1)
                    if j >= 4:
                        pe.wait_ge(pjs, PJ0[k] + j - 3)
                    for c in range(n):
                        o = ps[:, 4 + j % 4, c * m:(c + 1) * m]
                        mm(o, xt[:, (b + c) * P:(b + c + 1) * P], w[:, :], start=True, stop=False)
                        last = mm(o, ones[0:1, :], bias[:, :], start=False, stop=True)
                    last.then_inc(pjp, 1)

            def pair_rows(k, g, s, q):
                if KINDS[k] != "pna":
                    return
                n = SUB * g + s
                reach(pe, hot, 5 * ONE0[k], 5 * (n + 1))
                reach(pe, acd, PR0[k], 4 * n)
                for m in range(4):
                    last = mm(ps[:, 2 + m // 2, (m % 2) * AW:(m % 2 + 1) * AW], hot_l[:, s % 2, m, :],
                              hot_r[:, s % 2, m, :], start=True, stop=True)
                last.then_inc(bld, 1)

            def turn_back(k, kind, g, s, q):
                n = SUB * g + s
                reach(pe, scn, SC0[k], SCANS[kind] * (n + 1))
                reach(pe, ev, ONE0[k], n - (1 if kind == "pna" else 3))
                w = W_OF[kind]
                for t in range(ST):
                    c0 = s * SE + t * P
                    if kind == "pna":
                        o = ps[:, 4 + 2 * (s % 2) + t // 2, (t % 2) * 256:(t % 2) * 256 + 256]
                        pe.transpose(o[:, 0:P], scan[:, 0, c0:c0 + P], ident[:, :])
                        last = pe.transpose(o[:, P:2 * P], scan[:, 1, c0:c0 + P], ident[:, :])
                    else:
                        last = pe.transpose(ps[:, 4 + s, t * w:(t + 1) * w], scan[0:w, 0, c0:c0 + P], ident[0:w, 0:w])
                last.then_inc(bt, 1)

            def edges(k, kind):
                def body(i):
                    for q in range(2):
                        g = 2 * i + q
                        for s in range(SUB):
                            reach(pe, gt[q][s], GT0[k], 16 * ST * (i + 1))
                            if kind == "mlp":
                                pe.wait_ge(win[q][s], 16 * ST * (i + 1))
                        reach(pe, ld[q], LD0[k], 16 * LOADS[kind] * (i + 1))
                        for s in range(SUB):
                            n = SUB * g + s
                            z = ps[:, s % 2, :]
                            reach(pe, md, MD0[k], MIDS[kind] * (n - 1))
                            if kind == "pna":
                                mm(z, gw[k][:, :], attr[0:FE16, q, s * SE:(s + 1) * SE], start=True, stop=False)
                            if kind == "mlp":
                                reach(pe, rh, 0, n + 1)
                                mm(z, w1c[:, :], attr[:, q, s * SE:(s + 1) * SE], start=True, stop=False)
                            for t in range(ST):
                                tt = s * ST + t
                                last = mm(z[:, t * P:(t + 1) * P], gat_m[:, q, tt, :], ident[:, :],
                                          start=False, stop=(t == ST - 1 and kind == "pna"))
                                if kind == "mlp":
                                    last = mm(z[:, t * P:(t + 1) * P], ugat[:, q, tt, :],
                                              rank_hot[:, s % 2, t * P:(t + 1) * P],
                                              start=False, stop=(t == ST - 1))
                            last.then_inc(zt, 1)
                            behind(i, q, s, 1, lambda *at: pair_rows(k, *at))
                            behind(i, q, s, 2, lambda *at: turn_back(k, kind, *at))

                turns(pe, body)
                pair_rows(k, NG - 1, SUB - 1, 1)
                for s in (SUB - 2, SUB - 1):
                    turn_back(k, kind, NG - 1, s, 1)

            for l in range(2):
                if l:
                    pe.wait_ge(xr, 1)
                project(l)
                edges(l, "pna")
                for b in range(NB):
                    if b % CB == 0:
                        pe.wait_ge(agr, (NB // CB) * l + b // CB + 1)
                        pe.wait_ge(rs, ORD["agg", l, b // CB])
                    reach(pe, ats, 2 * NB * l, 2 * (b - 1))
                    for c in range(3):
                        m = P if c < 2 else F
                        last = pe.transpose(ps[0:m, b % 2, c * P:(c + 1) * P], agg[:, b % CB, c * P:c * P + m],
                                            ident[:, :])
                    last.then_inc(atp, 1)
                    pe.wait_ge(ats, 2 * NB * l + 2 * (b + 1))
                    reach(pe, oms, NB * l, b - 3)
                    o = ps[:, 4 + b % 4, 0:3 * F]
                    mm(o, xt[:, b * P:(b + 1) * P], wx[l][:, :], start=True, stop=False)
                    mm(o, ones[0:1, :], wxb[l][:, :], start=False, stop=False)
                    for c in range(3):
                        m = P if c < 2 else F
                        last = mm(o, aggt[0:m, b % 2, c, :], wpost[l][0:m, c, :], start=False, stop=(c == 2))
                    last.then_inc(omp, 1)
                for v in range(2):
                    pe.wait_ge(bns, 2 * l + v + 1)
                    src = acc if v == 0 else tmp
                    for j in range(7):
                        last = mm(ps[:, 0, 0:7 * F], ones[:, :],
                                  src[:, 7 * j:7 * j + 7, :].rearrange("p b f -> p (b f)"), start=(j == 0), stop=(j == 6))
                    last.then_inc(bnp, 1)
            loaded = [0, 0]
            for j in range(5):
                if j == 1:
                    pe.wait_ge(rk_in, 1)
                    mm(ps[:, 7, 0:TC + NB], tri, begun, start=True, stop=True)
                    mm(ps[:, 7, 64:64 + TC + NB], ones[:, :], begun, start=True, stop=True).then_inc(rk_sum, 1)
                rows = [first_rows, acc, tmp, acc, acc][j]
                m = F + 1 if j == 0 else F
                if j in (0, 3, 4):
                    pe.wait_ge(lxr, max(2, j))
                else:
                    pe.wait_ge(lnc, NB * j)

                def turn(b, r):
                    reach(pe, ltc, NB * j, b + 1)
                    reach(pe, lnc, NB * j, b - 1)
                    pe.sem_inc(go_pe, 1)
                    pe.transpose(ps[:, 2 + r, 0:m], outt[0:m, r, :], ident[0:m, 0:m]).then_inc(lbt, 1)

                def product(b, c, r):
                    slot = (r + j) % 2
                    reach(pe, ablk_ld[slot], loaded[slot], 16 * (c + 1))
                    reach(pe, ltc, NB * j, b - 1)
                    for sh in range(NB):
                        last = mm(ps[0:m, r, 0:P], rows[:, sh, :], ablk[:, slot, :, sh],
                                  start=(sh == 0), stop=(sh == NB - 1))
                    last.then_inc(lnp, 1)
                    if not (isinstance(b, int) and b == 0):
                        turn(b - 1, 1 - r)

                blocks(pe, product)
                turn(NB - 1, (NB - 1) % 2)
                for r in range(2):
                    loaded[(r + j) % 2] += 16 * (NB // 2 + 1 - r)
            pe.wait_ge(xr, 2)
            project(2)
            edges(2, "mlp")
            pe.wait_ge(agr, 2 * (NB // CB) + 1)
            for j, b, n in chunks(NB, 4):
                reach(pe, m_et, 0, j)
                for c in range(n):
                    last = pe.transpose(ps[:, 0, c * P:(c + 1) * P], ends["mlp"][:, b + c, :], ident[:, :])
                last.then_inc(m_e, 1)
                pe.wait_ge(m_et, j + 1)
                reach(pe, m_as, 0, j)
                for c in range(n):
                    last = mm(ps[:, 1, c * F:(c + 1) * F], mid[:, c * P:(c + 1) * P], w2[:, :], start=True, stop=True)
                last.then_inc(m_a, 1)
                pe.wait_ge(m_as, j + 1)
                for c in range(n):
                    last = pe.transpose(ps[0:F, 2, c * P:(c + 1) * P], acc[:, b + c, :], ident[:, :])
                last.then_inc(m_t, 1)
                pe.wait_ge(m_ts, j + 1)
                mm(ps[:, 3, 0:n * P], u1b[:, :], mid[0:F, 512:512 + n * P], start=True, stop=False)
                mm(ps[:, 3, 0:n * P], u1a[:, :], xt[:, b * P:(b + n) * P], start=False, stop=True).then_inc(m_h, 1)
                pe.wait_ge(m_hs, j + 1)
                reach(pe, m_os, 0, j)
                for c in range(n):
                    last = mm(ps[:, 4, c * F:(c + 1) * F], mid[:, 1024 + c * P:1024 + (c + 1) * P], u2[:, :],
                              start=True, stop=True)
                last.then_inc(m_o, 1)


def kernel(**inputs):
    import numpy as np
    import concourse.bacc as bacc
    from concourse import mybir
    from concourse.bass_utils import run_bass_kernel_spmd as run

    a = {k: np.asarray(v) for k, v in inputs.items()}
    x = np.zeros((NP, F), a["x"].dtype)
    x[:N] = a["x"]

    def padded(v, fill):
        out = np.full((EP,) + v.shape[1:], fill, v.dtype)
        out[:E] = v
        return out

    src, w = padded(a["src"], 0), padded(a["edge_weight"], 0)
    dst = padded(a["dst"], NP)
    before_first = np.full((1,), -1, dst.dtype)

    def features_first(v):
        return np.ascontiguousarray(v.reshape(NG, GE, v.shape[1]).transpose(0, 2, 1))

    arrays = {
        "x": x, "src_t": np.ascontiguousarray(src.reshape(NT, P).T),
        "dst_pad": np.concatenate([before_first, dst]), "dst_tiles": dst.reshape(NT, P),
        "src_tiles": src.reshape(NT, P), "w_tiles": w.reshape(NT, P),
        "dst_last": np.ascontiguousarray(dst.reshape(NT, P)[:, P - 1]),
        "a16_g": features_first(padded(a["edge_attr_16"], 0)), "a32_g": features_first(padded(a["edge_attr_32"], 0)),
        "wpT": np.ascontiguousarray(a["L0_gnn_W_pre"].transpose(0, 2, 1)),
        "wlT": np.ascontiguousarray(a["L0_gnn_W_lin"].transpose(0, 2, 1)),
        "we": a["L0_gnn_W_edge"], "be": a["L0_gnn_b_edge"], "bp": a["L0_gnn_b_pre"], "bo": a["L0_gnn_b_post"],
        "bl": a["L0_gnn_b_lin"], "wo": a["L0_gnn_W_post"], "gam": a["L0_gnn_bn_gamma"], "bet": a["L0_gnn_bn_beta"],
        "mw1": a["L3_gnn_mW1"], "mb1": a["L3_gnn_mb1"], "mw2": a["L3_gnn_mW2"], "mb2": a["L3_gnn_mb2"],
        "uw1": a["L3_gnn_uW1"], "ub1": a["L3_gnn_ub1"], "uw2": a["L3_gnn_uW2"], "ub2": a["L3_gnn_ub2"],
    }
    nc = bacc.Bacc("TRN2", target_bir_lowering=False, num_devices=1)
    inp = {n: nc.dram_tensor(f"in_{n}", v.shape, mybir.dt.from_np(v.dtype), kind="ExternalInput").ap()
           for n, v in arrays.items()}
    out = nc.dram_tensor("out_0", (N, F), mybir.dt.float32, kind="ExternalOutput").ap()
    build(nc, inp, out)
    r = run(nc, [{f"in_{n}": np.ascontiguousarray(v) for n, v in arrays.items()}], core_ids=[0])
    return r.results[0]["out_0"]
```
